# Optimizing a Trainium2 kernel written in Bass

```python
import numpy as np
import jax
import jax.numpy as jnp

def _softmax(x, axis=-1):
    return jax.nn.softmax(x, axis=axis)

def _gelu(x):
    return jax.nn.gelu(x, approximate=True)

def _silu(x):
    return jax.nn.silu(x)

def _sigmoid(x):
    return jax.nn.sigmoid(x)

def _layernorm(x, axis=-1, eps=1e-05):
    m = jnp.mean(x, axis=axis, keepdims=True)
    v = jnp.var(x, axis=axis, keepdims=True)
    return (x - m) / jnp.sqrt(v + eps)

def _scatter_add(tgt, idx, src, axis=0):
    return tgt.at[idx].add(src)

def _segment_sum(src, seg, n):
    return jax.ops.segment_sum(src, seg, n)
kernel_name = 'mk_seq_postln_d2_jaxref_r4_77c8c9'

def setup_inputs(seed: int=0):
    np.random.seed(seed)
    _w = jnp.asarray

    def _L0_attn_setup():
        import jax, jax.numpy as jnp
        import numpy as np
        import math
        B, S, D, H = (4, 512, 256, 16)
        HD = D // H
        key = jax.random.key(seed)
        ks = jax.random.split(key, 9)
        scale = 1.0 / math.sqrt(D)
        inputs = jax.random.normal(ks[0], (B, S, D), dtype=jnp.float32)
        W_q = jax.random.uniform(ks[1], (H, D, HD), minval=-scale, maxval=scale)
        b_q = jax.random.uniform(ks[2], (H, HD), minval=-scale, maxval=scale)
        W_k = jax.random.uniform(ks[3], (H, D, HD), minval=-scale, maxval=scale)
        b_k = jax.random.uniform(ks[4], (H, HD), minval=-scale, maxval=scale)
        W_v = jax.random.uniform(ks[5], (H, D, HD), minval=-scale, maxval=scale)
        b_v = jax.random.uniform(ks[6], (H, HD), minval=-scale, maxval=scale)
        W_o = jax.random.uniform(ks[7], (D, D), minval=-scale, maxval=scale)
        b_o = jax.random.uniform(ks[8], (D,), minval=-scale, maxval=scale)
        return {'inputs': inputs, 'W_q': W_q, 'b_q': b_q, 'W_k': W_k, 'b_k': b_k, 'W_v': W_v, 'b_v': b_v, 'W_o': W_o, 'b_o': b_o}
    _L0_attn_in = _L0_attn_setup()

    def _L0_ffn_setup():
        import jax, jax.numpy as jnp
        import numpy as np
        D_MODEL = 256
        HIDDEN = 1024
        N_ROUTING = 2
        key = jax.random.key(seed)
        ks = jax.random.split(key, 10)
        s = 0.02
        x = jax.random.normal(ks[0], (4, 1024, D_MODEL), dtype=jnp.float32)
        gate_w = jax.random.normal(ks[1], (N_ROUTING, D_MODEL), dtype=jnp.float32) * s
        w1 = jax.random.normal(ks[2], (N_ROUTING, D_MODEL, HIDDEN), dtype=jnp.float32) * s
        b1 = jax.random.normal(ks[3], (N_ROUTING, HIDDEN), dtype=jnp.float32) * s
        w2 = jax.random.normal(ks[4], (N_ROUTING, HIDDEN, D_MODEL), dtype=jnp.float32) * s
        b2 = jax.random.normal(ks[5], (N_ROUTING, D_MODEL), dtype=jnp.float32) * s
        sw1 = jax.random.normal(ks[6], (D_MODEL, HIDDEN), dtype=jnp.float32) * s
        sb1 = jax.random.normal(ks[7], (HIDDEN,), dtype=jnp.float32) * s
        sw2 = jax.random.normal(ks[8], (HIDDEN, D_MODEL), dtype=jnp.float32) * s
        sb2 = jax.random.normal(ks[9], (D_MODEL,), dtype=jnp.float32) * s
        return {'x': x, 'gate_w': gate_w, 'w1': w1, 'b1': b1, 'w2': w2, 'b2': b2, 'sw1': sw1, 'sb1': sb1, 'sw2': sw2, 'sb2': sb2}
    _L0_ffn_in = _L0_ffn_setup()

    def _L1_attn_setup():
        import jax, jax.numpy as jnp
        import numpy as np
        import math
        B, S, D = (2, 512, 256)
        HQ, HKV = (16, 4)
        HD = D // HQ
        N_REP = HQ // HKV
        WINDOW = 64
        ROPE_BASE = 10000.0

        def _rope(x):
            s, hd = (x.shape[1], x.shape[-1])
            inv_freq = 1.0 / ROPE_BASE ** (jnp.arange(0, hd, 2, dtype=jnp.float32) / hd)
            ang = jnp.arange(s, dtype=jnp.float32)[:, None] * inv_freq
            cos = jnp.cos(ang)[None, :, None, :].astype(x.dtype)
            sin = jnp.sin(ang)[None, :, None, :].astype(x.dtype)
            x1, x2 = (x[..., ::2], x[..., 1::2])
            out = jnp.stack([x1 * cos - x2 * sin, x1 * sin + x2 * cos], axis=-1)
            return out.reshape(x.shape)
        key = jax.random.key(seed)
        ks = jax.random.split(key, 5)
        sc = 0.02
        return {'x': jax.random.normal(ks[0], (B, S, D), dtype=jnp.float32), 'Wq': jax.random.normal(ks[1], (D, HQ * HD), dtype=jnp.float32) * sc, 'Wk': jax.random.normal(ks[2], (D, HKV * HD), dtype=jnp.float32) * sc, 'Wv': jax.random.normal(ks[3], (D, HKV * HD), dtype=jnp.float32) * sc, 'Wo': jax.random.normal(ks[4], (HQ * HD, D), dtype=jnp.float32) * sc}
    _L1_attn_in = _L1_attn_setup()

    def _L1_ffn_setup():
        import jax, jax.numpy as jnp
        import numpy as np
        E = 16
        G = 4
        EPG = E // G
        K = 4
        TOPK_GROUP = 2
        PER_GROUP_K = K // TOPK_GROUP

        def _route(xf, router_w, correction_bias):
            S = xf.shape[0]
            logits = xf @ router_w.T
            scores = jax.nn.sigmoid(logits)
            sb = scores + correction_bias
            grp_top = jax.lax.top_k(sb.reshape(S, G, EPG), PER_GROUP_K)[0]
            group_scores = grp_top.sum(axis=-1)
            _, group_idx = jax.lax.top_k(group_scores, TOPK_GROUP)
            group_mask = jnp.zeros((S, G), sb.dtype).at[jnp.arange(S)[:, None], group_idx].set(1.0)
            score_mask = jnp.broadcast_to(group_mask[:, :, None], (S, G, EPG)).reshape(S, E)
            masked = jnp.where(score_mask > 0, sb, -jnp.inf)
            _, topk_idx = jax.lax.top_k(masked, K)
            w = jnp.take_along_axis(scores, topk_idx, axis=1)
            w = w / (w.sum(axis=-1, keepdims=True) + 1e-20)
            return (topk_idx, w, scores)
        key = jax.random.key(seed)
        ks = jax.random.split(key, 9)
        B, T, C, H, HS = (2, 256, 256, 64, 512)
        std = 0.02
        return {'x': jax.random.normal(ks[0], (B, T, C), jnp.float32), 'router_w': jax.random.normal(ks[1], (E, C), jnp.float32) * std, 'correction_bias': jnp.zeros((E,), jnp.float32), 'gate_w': jax.random.normal(ks[2], (E, C, H), jnp.float32) * std, 'up_w': jax.random.normal(ks[3], (E, C, H), jnp.float32) * std, 'down_w': jax.random.normal(ks[4], (E, H, C), jnp.float32) * std, 'shared_gate_w': jax.random.normal(ks[5], (HS, C), jnp.float32) * std, 'shared_up_w': jax.random.normal(ks[6], (HS, C), jnp.float32) * std, 'shared_down_w': jax.random.normal(ks[7], (C, HS), jnp.float32) * std}
    _L1_ffn_in = _L1_ffn_setup()
    _d = {'L0_attn_inputs': _L0_attn_in['inputs'], 'L0_attn_W_q': _L0_attn_in['W_q'], 'L0_attn_b_q': _L0_attn_in['b_q'], 'L0_attn_W_k': _L0_attn_in['W_k'], 'L0_attn_b_k': _L0_attn_in['b_k'], 'L0_attn_W_v': _L0_attn_in['W_v'], 'L0_attn_b_v': _L0_attn_in['b_v'], 'L0_attn_W_o': _L0_attn_in['W_o'], 'L0_attn_b_o': _L0_attn_in['b_o'], 'L0_ffn_gate_w': _L0_ffn_in['gate_w'], 'L0_ffn_w1': _L0_ffn_in['w1'], 'L0_ffn_b1': _L0_ffn_in['b1'], 'L0_ffn_w2': _L0_ffn_in['w2'], 'L0_ffn_b2': _L0_ffn_in['b2'], 'L0_ffn_sw1': _L0_ffn_in['sw1'], 'L0_ffn_sb1': _L0_ffn_in['sb1'], 'L0_ffn_sw2': _L0_ffn_in['sw2'], 'L0_ffn_sb2': _L0_ffn_in['sb2'], 'L1_attn_Wq': _L1_attn_in['Wq'], 'L1_attn_Wk': _L1_attn_in['Wk'], 'L1_attn_Wv': _L1_attn_in['Wv'], 'L1_attn_Wo': _L1_attn_in['Wo'], 'L1_ffn_router_w': _L1_ffn_in['router_w'], 'L1_ffn_correction_bias': _L1_ffn_in['correction_bias'], 'L1_ffn_gate_w': _L1_ffn_in['gate_w'], 'L1_ffn_up_w': _L1_ffn_in['up_w'], 'L1_ffn_down_w': _L1_ffn_in['down_w'], 'L1_ffn_shared_gate_w': _L1_ffn_in['shared_gate_w'], 'L1_ffn_shared_up_w': _L1_ffn_in['shared_up_w'], 'L1_ffn_shared_down_w': _L1_ffn_in['shared_down_w']}
    _x0 = _d['L0_attn_inputs']
    _d['L0_attn_inputs'] = jax.random.normal(jax.random.fold_in(jax.random.key(seed), 1), (8, 512, 256), dtype=_x0.dtype)
    del _x0
    return _d

def reference(L0_attn_inputs, L0_attn_W_q, L0_attn_b_q, L0_attn_W_k, L0_attn_b_k, L0_attn_W_v, L0_attn_b_v, L0_attn_W_o, L0_attn_b_o, L0_ffn_gate_w, L0_ffn_w1, L0_ffn_b1, L0_ffn_w2, L0_ffn_b2, L0_ffn_sw1, L0_ffn_sb1, L0_ffn_sw2, L0_ffn_sb2, L1_attn_Wq, L1_attn_Wk, L1_attn_Wv, L1_attn_Wo, L1_ffn_router_w, L1_ffn_correction_bias, L1_ffn_gate_w, L1_ffn_up_w, L1_ffn_down_w, L1_ffn_shared_gate_w, L1_ffn_shared_up_w, L1_ffn_shared_down_w):

    def _L0_attn_ref(inputs, W_q, b_q, W_k, b_k, W_v, b_v, W_o, b_o):
        import jax, jax.numpy as jnp
        import numpy as np
        import math
        B, S, D, H = (4, 512, 256, 16)
        HD = D // H
        seq_len = inputs.shape[1]
        head_dim = W_q.shape[-1]
        q = jnp.einsum('bsd,hde->bhse', inputs, W_q) + b_q[None, :, None, :]
        k = jnp.einsum('bsd,hde->bhse', inputs, W_k) + b_k[None, :, None, :]
        v = jnp.einsum('bsd,hde->bhse', inputs, W_v) + b_v[None, :, None, :]
        scores = jnp.einsum('bhse,bhte->bhst', q, k) / math.sqrt(head_dim)
        causal = jnp.tril(jnp.ones((seq_len, seq_len), dtype=bool))
        scores = jnp.where(causal[None, None], scores, -jnp.inf)
        attn = jax.nn.softmax(scores, axis=-1)
        wv = jnp.einsum('bhst,bhte->bshe', attn, v).reshape(inputs.shape[0], seq_len, -1)
        return wv @ W_o.T + b_o

    def _L0_ffn_ref(x, gate_w, w1, b1, w2, b2, sw1, sb1, sw2, sb2):
        import jax, jax.numpy as jnp
        import numpy as np
        D_MODEL = 256
        HIDDEN = 1024
        N_ROUTING = 2
        B, S, D = x.shape
        xf = x.reshape(-1, D)
        gate_scores = xf @ gate_w.T
        gate_probs = jax.nn.softmax(gate_scores, axis=-1)
        top1 = jnp.argmax(gate_probs, axis=-1)
        one_hot = jax.nn.one_hot(top1, N_ROUTING, dtype=xf.dtype)
        masked = xf[None, :, :] * one_hot.T[:, :, None]
        h = jax.nn.relu(jnp.einsum('end,edh->enh', masked, w1) + b1[:, None, :])
        expert_out = jnp.einsum('enh,ehd->end', h, w2) + b2[:, None, :]
        routing_output = expert_out.sum(axis=0)
        shared = jax.nn.relu(xf @ sw1 + sb1) @ sw2 + sb2
        return (routing_output + shared).reshape(B, S, D)

    def _L1_attn_ref(x, Wq, Wk, Wv, Wo):
        import jax, jax.numpy as jnp
        import numpy as np
        import math
        B, S, D = (2, 512, 256)
        HQ, HKV = (16, 4)
        HD = D // HQ
        N_REP = HQ // HKV
        WINDOW = 64
        ROPE_BASE = 10000.0

        def _rope(x):
            s, hd = (x.shape[1], x.shape[-1])
            inv_freq = 1.0 / ROPE_BASE ** (jnp.arange(0, hd, 2, dtype=jnp.float32) / hd)
            ang = jnp.arange(s, dtype=jnp.float32)[:, None] * inv_freq
            cos = jnp.cos(ang)[None, :, None, :].astype(x.dtype)
            sin = jnp.sin(ang)[None, :, None, :].astype(x.dtype)
            x1, x2 = (x[..., ::2], x[..., 1::2])
            out = jnp.stack([x1 * cos - x2 * sin, x1 * sin + x2 * cos], axis=-1)
            return out.reshape(x.shape)
        b, s, _ = x.shape
        xq = (x @ Wq).reshape(b, s, HQ, HD)
        xk = (x @ Wk).reshape(b, s, HKV, HD)
        xv = (x @ Wv).reshape(b, s, HKV, HD)
        xq = _rope(xq)
        xk = _rope(xk)
        keys = jnp.repeat(xk, N_REP, axis=2)
        values = jnp.repeat(xv, N_REP, axis=2)
        scores = jnp.einsum('bqhd,bkhd->bhqk', xq, keys) / math.sqrt(HD)
        idx = jnp.arange(s)
        mask = jnp.abs(idx[:, None] - idx[None, :]) <= WINDOW // 2
        scores = jnp.where(mask[None, None], scores, -jnp.inf)
        attn = jax.nn.softmax(scores.astype(jnp.float32), axis=-1).astype(xq.dtype)
        ctx = jnp.einsum('bhqk,bkhd->bqhd', attn, values).reshape(b, s, HQ * HD)
        return ctx @ Wo

    def _L1_ffn_ref(x, router_w, correction_bias, gate_w, up_w, down_w, shared_gate_w, shared_up_w, shared_down_w):
        import jax, jax.numpy as jnp
        import numpy as np
        E = 16
        G = 4
        EPG = E // G
        K = 4
        TOPK_GROUP = 2
        PER_GROUP_K = K // TOPK_GROUP

        def _route(xf, router_w, correction_bias):
            S = xf.shape[0]
            logits = xf @ router_w.T
            scores = jax.nn.sigmoid(logits)
            sb = scores + correction_bias
            grp_top = jax.lax.top_k(sb.reshape(S, G, EPG), PER_GROUP_K)[0]
            group_scores = grp_top.sum(axis=-1)
            _, group_idx = jax.lax.top_k(group_scores, TOPK_GROUP)
            group_mask = jnp.zeros((S, G), sb.dtype).at[jnp.arange(S)[:, None], group_idx].set(1.0)
            score_mask = jnp.broadcast_to(group_mask[:, :, None], (S, G, EPG)).reshape(S, E)
            masked = jnp.where(score_mask > 0, sb, -jnp.inf)
            _, topk_idx = jax.lax.top_k(masked, K)
            w = jnp.take_along_axis(scores, topk_idx, axis=1)
            w = w / (w.sum(axis=-1, keepdims=True) + 1e-20)
            return (topk_idx, w, scores)
        B, T, C = x.shape
        S = B * T
        xf = x.reshape(S, C)
        sg = xf @ shared_gate_w.T
        su = xf @ shared_up_w.T
        shared_out = jax.nn.silu(sg) * su @ shared_down_w.T
        topk_idx, w, _scores = _route(xf, router_w, correction_bias)
        combine = jnp.zeros((S, E), xf.dtype).at[jnp.arange(S)[:, None], topk_idx].add(w)
        g = jnp.einsum('sc,ech->esh', xf, gate_w)
        u = jnp.einsum('sc,ech->esh', xf, up_w)
        h = jax.nn.silu(g) * u
        hw = h * combine.T[:, :, None]
        routed = jnp.einsum('esh,ehc->sc', hw, down_w)
        return (shared_out + routed).reshape(B, T, C)
    x = L0_attn_inputs
    x = _layernorm(x + _L0_attn_ref(x, L0_attn_W_q, L0_attn_b_q, L0_attn_W_k, L0_attn_b_k, L0_attn_W_v, L0_attn_b_v, L0_attn_W_o, L0_attn_b_o), axis=-1)
    x = _layernorm(x + _L0_ffn_ref(x, L0_ffn_gate_w, L0_ffn_w1, L0_ffn_b1, L0_ffn_w2, L0_ffn_b2, L0_ffn_sw1, L0_ffn_sb1, L0_ffn_sw2, L0_ffn_sb2), axis=-1)
    x = _layernorm(x + _L1_attn_ref(x, L1_attn_Wq, L1_attn_Wk, L1_attn_Wv, L1_attn_Wo), axis=-1)
    x = _layernorm(x + _L1_ffn_ref(x, L1_ffn_router_w, L1_ffn_correction_bias, L1_ffn_gate_w, L1_ffn_up_w, L1_ffn_down_w, L1_ffn_shared_gate_w, L1_ffn_shared_up_w, L1_ffn_shared_down_w), axis=-1)
    return x

_drawn_inputs = setup_inputs


def setup_inputs(seed=0):
    import zlib

    import numpy as np

    out = dict(_drawn_inputs(seed))
    spreads = {'L1_ffn_correction_bias': (0.0, 0.8)}
    factors = {'L0_attn_W_q': 3.436,
     'L0_attn_b_q': 8.0,
     'L0_attn_W_k': 3.395,
     'L0_attn_b_k': 64.0,
     'L0_ffn_b1': 5.099,
     'L0_ffn_sb1': 6.717,
     'L0_ffn_sb2': 2.795,
     'L1_attn_Wq': 8.0,
     'L1_attn_Wk': 8.0,
     'L1_attn_Wv': 3.37,
     'L1_attn_Wo': 3.365,
     'L1_ffn_router_w': 8.0,
     'L1_ffn_gate_w': 8.0,
     'L1_ffn_up_w': 8.0,
     'L1_ffn_down_w': 8.0,
     'L1_ffn_shared_gate_w': 7.323,
     'L1_ffn_shared_up_w': 7.196,
     'L1_ffn_shared_down_w': 7.235}
    for name, (base, spread) in spreads.items():
        noise = np.random.default_rng([zlib.crc32(name.encode()), seed]).standard_normal(out[name].shape)
        drawn = base * np.exp(spread * noise) if base else spread * noise
        out[name] = jnp.asarray(drawn.astype(out[name].dtype))
    for name, factor in factors.items():
        out[name] = (out[name] * factor).astype(out[name].dtype)
    return out
```

```python
from contextlib import ExitStack

import concourse.bass as bass
from concourse import mybir

F32 = mybir.dt.float32
F32R = mybir.dt.float32r
BF16 = mybir.dt.bfloat16
ALU = mybir.AluOpType
ACT = mybir.ActivationFunctionType
AX = mybir.AxisListType

P = 128
B = 8
S = 512
D = 256
KD = D // P
NT = S // P
H = 16
HD = D // H
LN_EPS = 1e-5
MASKED = -1.0e37
TERMS = ((0, 0), (0, 1), (1, 0))


class Phase:

    def __init__(self, nc, ctx, name):
        self.nc, self.ctx, self.name = nc, ctx, name

    def sb(self, name, shape, dt=F32):
        return self.ctx.enter_context(self.nc.sbuf_tensor(f"{self.name}_{name}", shape, dt))

    def psum(self, name, shape, dt=F32):
        return self.ctx.enter_context(self.nc.psum_tensor(f"{self.name}_{name}", shape, dt))

    def sem(self, name):
        return self.ctx.enter_context(self.nc.semaphore(f"{self.name}_{name}"))


def raw(ap):
    return ap.bitcast(F32)


def matmul3(pe, out, w, x, wcols, xcols, blocks, last=True):
    n = 0
    for i, j in TERMS:
        for k in range(blocks):
            ins = pe.matmul(out, w[:, i, k, wcols], x[:, j, k, xcols],
                            start=(n == 0), stop=(n == 3 * blocks - 1))
            n += 1
    return ins


def settle(eng, sem, value, passed):
    eng.wait_ge(sem, value)
    eng.sem_inc(passed, 1)


class LayerNorm:

    def __init__(self, ph):
        self.z = ph.sb("ln_z", [P, NT, D])
        self.stats = ph.sb("ln_stats", [P, NT, 6])
        self.mv = ph.sb("ln_mv", [P, NT, 2])
        self.rstd = ph.sb("ln_rstd", [P, NT])
        self.var = ph.sb("ln_var", [P, NT])
        self.power = ph.sb("ln_power", [P, NT])
        self.out = ph.sb("ln_out", [P, NT, D])
        self.stat = ph.sem("ln_stat")
        self.vared = ph.sem("ln_vared")
        self.rooted = ph.sem("ln_rooted")
        self.passed = ph.sem("ln_passed")
        self.applied = ph.sem("ln_applied")

    def constants(self, pool, done):
        pool.memset(self.power[:], -0.5).then_inc(done, 1)

    def transposes(self, pe, take, uses, y, ident, full):
        for pair in range(NT // 2):
            bank = take(uses[pair])
            for t in range(2):
                for k in range(KD):
                    at = t * D + k * P
                    ins = pe.transpose(bank[:, at:at + P], y[:, k, (2 * pair + t) * P:(2 * pair + t + 1) * P], ident[:])
            ins.then_inc(full[uses[pair][0]], 1)

    def root(self, pool, n):
        pool.wait_ge(self.rooted, n + 1)
        settle(pool, self.stat, n * (2 * NT) + (2 * NT + 1), self.passed)
        pool.tensor_scalar(self.var[:], self.mv[:, :, 1], LN_EPS, None, ALU.add).then_inc(self.vared, 1)
        pool.wait_ge(self.vared, n + 1)
        pool.tensor_tensor(self.rstd[:], self.var[:], self.power[:], ALU.pow).then_inc(self.rooted, 1)

    def run(self, dve, n, uses, wait_full, w_free, ps, bank0, x_res, xres_in, stored):
        dve.wait_ge(xres_in, n * 16 + 16)
        dve.wait_ge(self.applied, n * NT + 1)
        for pair, use in enumerate(uses):
            slot = use[0]
            wait_full(use)
            dve.tensor_tensor(self.z[:, 2 * pair:2 * pair + 2],
                              ps[:, bank0 + slot].rearrange("p (t d) -> p t d", t=2),
                              x_res[:, 2 * pair:2 * pair + 2], ALU.add).then_inc(w_free[slot], 1)
        for pair, use in enumerate(uses):
            dve.wait_ge(w_free[use[0]], use[1] + 2)
            for t in range(2 * pair, 2 * pair + 2):
                dve.bn_stats(self.stats[:, t], self.z[:, t]).then_inc(self.stat, 1)
        for t in range(NT):
            settle(dve, self.stat, n * (2 * NT) + (t + 2), self.passed)
            dve.bn_aggr(self.mv[:, t], self.stats[:, t]).then_inc(self.stat, 1)
        dve.wait_ge(self.rooted, n + 2)
        dve.wait_ge(stored, n * 16 + 1)
        for t in range(NT):
            dve.tensor_scalar(self.out[:, t], self.z[:, t], self.mv[:, t, 0:1], self.rstd[:, t:t + 1],
                              ALU.subtract, ALU.mult).then_inc(self.applied, 1)


HALF = 8
PAIRS = HALF // 2
ROWS = 64
TILES = HALF * NT
STEPS = TILES // 4
W_PRE = 9
W_LOOP = 20
M_LAG = 8


def attention0(nc, x_in, wqkv, bqk, bv_row, bo, ident_in, causal_in, qk_scratch, x_out):
    x_view = x_in.rearrange("(n t p) d -> n p t d", t=NT, p=P)
    out_view = x_out.rearrange("(n t p) d -> n p t d", t=NT, p=P)
    qk_write = qk_scratch.rearrange("o h i e s -> o i h e s")
    ctx = ExitStack()
    with ctx:
        ph = Phase(nc, ctx, "a0")
        sb, sem = ph.sb, ph.sem
        w_raw = sb("w_raw", [P, KD, 4 * D])
        w_hl = sb("w_hl", [P, 2, KD, 4 * D], F32R)
        bqk_sb = sb("bqk", [P, 2, 2])
        bo_sb = sb("bo", [P, KD])
        bv_sb = sb("bv", [P, D])
        ident = sb("ident", [P, P])
        ident_b = sb("ident_b", [P, P], BF16)
        causal = sb("causal", [P, 2, P])
        causal_b = sb("causal_b", [P, 2, P], BF16)
        zeros = sb("zeros", [32, P])
        ones = sb("ones", [2, S])
        x_sb = sb("x", [P, NT, D])
        x_res = sb("x_res", [P, NT, D])
        xt = sb("xt", [P, 2, KD, S], F32R)
        qk = sb("qk", [P, 2, 2, S], F32R)
        q_st = [sb(f"q_st{i}", [P, PAIRS, S], F32R) for i in range(2)]
        k_st = [sb(f"k_st{i}", [P, HALF, S], F32R) for i in range(2)]
        v_aug = [sb(f"v_aug{i}", [P, NT, HALF, 32]) for i in range(2)]
        nmax = sb("nmax", [P, 32])
        nmax2 = sb("nmax2", [P, 2, 2, 16], F32R)
        mrow = sb("mrow", [64, P], F32R)
        probs = sb("probs", [P, 8, S])
        pv_sb = [sb(f"pv_sb{i}", [P, S]) for i in range(2)]
        rden = sb("rden", [P, 2, NT, 4])
        o_tok = sb("o_tok", [P, NT, D])
        o_hl = sb("o_hl", [P, 2, KD, S], F32R)
        y_sb = sb("y", [P, KD, S])
        ln = LayerNorm(ph)

        ps = ph.psum("ps", [P, 8, S])

        loaded = sem("loaded")
        set_up = sem("set_up")
        w_split = sem("w_split")
        x_in_sem = sem("x_in")
        xres_in = sem("xres_in")
        w_full = sem("w_full")
        w_free = [sem("w_free0"), sem("w_free1")]
        hi_done = sem("hi_done")
        qk_out = sem("qk_out")
        stack_in = [sem("stack_in0"), sem("stack_in1")]
        s_full = sem("s_full")
        s_free = sem("s_free")
        t_full = sem("t_full")
        t_free = sem("t_free")
        pv_step = sem("pv_step")
        pv_free = sem("pv_free")
        nm_hi = sem("nm_hi")
        nm_ready = sem("nm_ready")
        mrow_in = [sem("mrow_in0"), sem("mrow_in1")]
        rden_ok = sem("rden_ok")
        o_split = sem("o_split")
        oproj_done = sem("oproj_done")
        y_out = sem("y_out")
        ones_in = sem("ones_in")

        def work(c, n):
            return c % 2, c // 2 + n * (W_LOOP // 2), c + n * W_LOOP

        def width(block):
            return S - block * P

        def slot_order(e, m):
            order = []
            for k in range(TILES + (M_LAG if e and m else 0)):
                if e and k < TILES:
                    order.append(("t", k))
                    if k % 4 == 3 and k > 4:
                        order.append(("pv", k // 4 - 1))
                    if k == 22:
                        order.append(("ut", 0))
                j = k - (M_LAG if e and m else 0)
                if m and 0 <= j < TILES:
                    order.append(("s", j))
            if e:
                order.insert(order.index(("t", TILES - 1)) + 4, ("pv", STEPS - 1))
            return order

        LAST = B - 1
        PRE = {"xt": 0, "p": 2, "t": 5, "p2": 6}
        LOOP = {k: W_PRE + v for k, v in dict(a_ut0=0, a_t=1, a_ut1=2, xt=3, p=5, b_ut0=8, b_t=9, b_ut1=10,
                                              p2=11, ot=14, o=16, yt=18).items()}
        TAIL = {k: W_PRE + v for k, v in dict(a_ut0=0, a_t=1, a_ut1=2, b_ut0=3, b_ut1=4, ot=5, o=7, yt=9).items()}

        def program(eng, st):
            st.load_x(0)
            st.transpose_x(0, work(PRE["xt"], 0))
            st.project((0, 0), work(PRE["p"], 0))
            st.slot(None, (0, 0), None)
            st.maxima((0, 0), work(PRE["t"], 0))
            st.project((0, 1), work(PRE["p2"], 0))
            with eng.Fori(0, LAST) as n:
                st.load_res(n)
                st.slot((n, 0), (n, 1), work(LOOP["a_ut0"], n))
                st.maxima((n, 1), work(LOOP["a_t"], n))
                st.normalise((n, 0), 1, work(LOOP["a_ut1"], n))
                st.load_x(n + 1)
                st.transpose_x(n + 1, work(LOOP["xt"], n))
                st.project((n + 1, 0), work(LOOP["p"], n))
                st.slot((n, 1), (n + 1, 0), work(LOOP["b_ut0"], n))
                st.maxima((n + 1, 0), work(LOOP["b_t"], n))
                st.normalise((n, 1), 1, work(LOOP["b_ut1"], n))
                st.project((n + 1, 1), work(LOOP["p2"], n))
                st.output(n, work(LOOP["ot"], n), work(LOOP["o"], n), work(LOOP["yt"], n))
            n = LAST
            st.load_res(n)
            st.slot((n, 0), (n, 1), work(TAIL["a_ut0"], n))
            st.maxima((n, 1), work(TAIL["a_t"], n))
            st.normalise((n, 0), 1, work(TAIL["a_ut1"], n))
            st.slot((n, 1), None, work(TAIL["b_ut0"], n))
            st.normalise((n, 1), 1, work(TAIL["b_ut1"], n))
            st.output(n, work(TAIL["ot"], n), work(TAIL["o"], n), work(TAIL["yt"], n))

        def later(w, k):
            slot, before, count = w
            return (slot + k) % 2, before + (slot + k) // 2, count + k

        def unit(u, per, k):
            return u[0] * (2 * per) + (u[1] * per + k)

        class Stages:
            def load_x(self, n): pass
            def load_res(self, n): pass
            def transpose_x(self, n, w): pass
            def project(self, u, w): pass
            def slot(self, e, m, w): pass
            def maxima(self, u, w): pass
            def normalise(self, u, g, w): pass
            def output(self, n, wot, wo_, wyt): pass

        SETS = 11
        block = ctx.enter_context(nc.Block())

        @block.sync
        def _(sp):
            for dst, src in ((w_raw[:], wqkv.rearrange("(k p) n -> p k n", p=P)),
                             (bqk_sb[:], bqk), (bo_sb[:], bo), (bv_sb[:], bv_row),
                             (ident[:], ident_in), (causal[:], causal_in)):
                sp.dma_start(dst, src).then_inc(loaded, 16)
            sp.sem_inc(w_free[0], 1)
            sp.sem_inc(w_free[1], 1)
            sp.sem_inc(s_free, 2)
            sp.sem_inc(t_free, 2)
            sp.sem_inc(pv_step, 2)
            sp.sem_inc(pv_free, 2)

            class Sync(Stages):
                def load_x(self, n):
                    sp.dma_start(x_sb[:], x_view[n]).then_inc(x_in_sem, 16)

                def load_res(self, n):
                    sp.wait_ge(ln.stat, n * 8 + 1)
                    sp.dma_start(x_res[:], x_view[n]).then_inc(xres_in, 16)

                def project(self, u, w):
                    n, q = u
                    if q == 1:
                        settle(sp, stack_in[0], n * 160 + 160, ln.passed)
                    elif not isinstance(n, int):
                        settle(sp, stack_in[1], n * 160, ln.passed)
                    for o in range(2):
                        slot, before, _ = later(w, o)
                        sp.wait_ge(w_free[slot], before + 2)
                        for i in range(2):
                            sp.dma_start(qk_write[o, i], raw(qk[:, o, i])).then_inc(qk_out, 16)
                    if not (isinstance(n, int) and n == 0):
                        settle(sp, pv_step, unit(u, STEPS, 2 - STEPS), ln.passed)
                    sp.wait_ge(qk_out, unit(u, 64, 64))
                    for p in range(2):
                        r = ROWS * p
                        q_heads = qk_scratch[0].rearrange("(j p) i e s -> p (i e) j s", p=2)[p]
                        k_heads = qk_scratch[1].rearrange("(j p) i e s -> p (i e) j s", p=2)[p]
                        k_dst = raw(k_st[q][:]).rearrange("r (j p) s -> r p j s", p=2)[:, p]
                        q_dst = raw(q_st[q][:])
                        sp.dma_start(q_dst[r:r + 32], q_heads).then_inc(stack_in[q], 16)
                        sp.dma_start(q_dst[r + 32:r + 48], q_heads[0:16]).then_inc(stack_in[q], 16)
                        sp.dma_start(k_dst[r:r + 16], k_heads[0:16]).then_inc(stack_in[q], 16)
                        sp.dma_start(k_dst[r + 16:r + 48], k_heads).then_inc(stack_in[q], 16)
                        sp.dma_start(q_dst[r + 48:r + 50].rearrange("r j (i s) -> r (j i) s", s=P), zeros[:, :])\
                          .then_inc(stack_in[q], 16)

                def maxima(self, u, w):
                    slot, before, _ = w
                    sp.wait_ge(w_free[slot], before + 2)
                    for p in range(2):
                        r = ROWS * p
                        sp.dma_start(raw(q_st[u[1]][r + 48:r + 50]).rearrange("r j (i s) -> r (j i) s", s=P),
                                     raw(mrow[32 * p:32 * p + 32, :])).then_inc(mrow_in[u[1]], 16)

                def output(self, n, wot, wo_, wyt):
                    sp.wait_ge(ln.applied, n * NT + (NT + 1))
                    sp.dma_start(out_view[n], ln.out[:]).then_inc(y_out, 16)

            sp.sem_inc(ln.stat, 1)
            sp.sem_inc(ln.applied, 1)
            sp.sem_inc(ln.rooted, 1)
            sp.sem_inc(y_out, 1)
            sp.wait_ge(set_up, SETS)
            for q in range(2):
                for h in range(HALF):
                    r = ROWS * (h % 2) + 48
                    sp.dma_start(raw(k_st[q][r:r + 2, h]), ones[:, :]).then_inc(ones_in, 16)
            sp.wait_ge(ones_in, 2 * HALF * 16)
            program(sp, Sync())
            sp.wait_ge(y_out, 16 * B + 1)

        @block.gpsimd
        def _(pool):
            pool.memset(zeros[:], 0.0).then_inc(set_up, 1)
            pool.memset(ones[:], 1.0).then_inc(set_up, 1)
            for i in range(2):
                pool.memset(raw(q_st[i][:]), 0.0).then_inc(set_up, 1)
                pool.memset(raw(k_st[i][:]), 0.0).then_inc(set_up, 1)
                pool.memset(v_aug[i][:], 1.0).then_inc(set_up, 1)
            ln.constants(pool, set_up)
            pool.wait_ge(set_up, SETS)
            pool.wait_ge(loaded, 16 * 6)

            class Pool(Stages):
                def output(self, n, wot, wo_, wyt):
                    ln.root(pool, n)

            program(pool, Pool())

        @block.vector
        def _(dve):
            dve.wait_ge(loaded, 16 * 6)
            dve.tensor_copy(ident_b[:], ident[:]).then_inc(set_up, 1)
            dve.tensor_copy(causal_b[:], causal[:]).then_inc(set_up, 1)
            dve.wait_ge(w_split, 1)
            dve.tensor_tensor(w_hl[:, 1], w_raw[:], raw(w_hl[:, 0]), ALU.subtract).then_inc(w_split, 1)
            dve.wait_ge(set_up, SETS)

            class Vector(Stages):

                def lo(self, out, psum, hi, bias, count, w):
                    slot, before, _ = w
                    dve.wait_ge(hi_done, count)
                    if bias is None:
                        ins = dve.tensor_tensor(out, psum, raw(hi), ALU.subtract)
                    else:
                        ins = dve.scalar_tensor_tensor(out, psum, bias, raw(hi), ALU.add, ALU.subtract)
                    ins.then_inc(w_free[slot], 1)

                def transpose_x(self, n, w):
                    for k in range(KD):
                        slot, before, _ = later(w, k)
                        self.lo(xt[:, 1, k], ps[:, 6 + slot], xt[:, 0, k], None, n * 6 + (k + 1), later(w, k))

                def project(self, u, w):
                    n, q = u
                    for o in range(2):
                        slot, _, _ = later(w, o)
                        self.lo(qk[:, o, 1], ps[:, 6 + slot], qk[:, o, 0], bqk_sb[:, o, q:q + 1],
                                n * 6 + (2 + 2 * q + o + 1), later(w, o))
                    slot, _, count = later(w, 2)
                    dve.wait_ge(w_full, count + 1)
                    if not (isinstance(n, int) and n == 0):
                        dve.wait_ge(pv_step, unit(u, STEPS, 2 - STEPS))
                    bias = bv_sb[:, q * P:(q + 1) * P].rearrange("p (h e) -> p h e", e=HD)
                    dve.tensor_tensor(v_aug[q][:, :, :, 0:HD],
                                      ps[:, 6 + slot].rearrange("p (t h e) -> p t h e", t=NT, e=HD),
                                      bias.unsqueeze(1).broadcast_to([P, NT, HALF, HD]),
                                      ALU.add).then_inc(w_free[slot], 1)

                def slot(self, e, m, w):
                    for kind, k in slot_order(e, m):
                        if kind == "s":
                            h, i = k // NT, k % NT
                            dve.wait_ge(s_full, unit(m, TILES, k + 1))
                            at = 16 * (h % 2) + 4 * (h // 2) + i
                            dve.tensor_reduce(nmax[:, at:at + 1], ps[:, k % 2, 0:(i + 1) * P], AX.X, ALU.max,
                                              negate=True).then_inc(s_free, 1)
                        elif kind == "ut":
                            self.normalise(e, 0, w)

                def maxima(self, u, w):
                    dve.wait_ge(s_free, unit(u, TILES, TILES + 2))
                    src = nmax[:].rearrange("p (a r) -> p a r", a=2)
                    dve.tensor_copy(nmax2[:, :, 0], src).then_inc(nm_hi, 1)
                    dve.wait_ge(nm_hi, unit(u, 1, 1))
                    dve.tensor_tensor(nmax2[:, :, 1], src, raw(nmax2[:, :, 0]), ALU.subtract).then_inc(nm_ready, 1)

                def normalise(self, u, g, w):
                    slot, before, count = w
                    dve.wait_ge(w_full, count + 1)
                    tile = ps[:, 6 + slot].rearrange("p (t r c) -> p t r c", t=NT, r=4)
                    dve.reciprocal(rden[:, g], tile[:, :, :, HD]).then_inc(rden_ok, 1)
                    dve.wait_ge(rden_ok, unit(u, 2, g + 1))
                    at = (u[1] * 2 + g) * 4 * HD
                    dve.tensor_tensor(o_tok[:, :, at:at + 4 * HD].rearrange("p t (r e) -> p t r e", e=HD),
                                      tile[:, :, :, 0:HD],
                                      rden[:, g].unsqueeze(3).broadcast_to([P, NT, 4, HD]),
                                      ALU.mult).then_inc(w_free[slot], 1)

                def output(self, n, wot, wo_, wyt):
                    for k in range(KD):
                        slot, _, _ = later(wot, k)
                        dve.wait_ge(o_split, n * KD + (k + 1))
                        dve.tensor_tensor(o_hl[:, 1, k], ps[:, 6 + slot], raw(o_hl[:, 0, k]), ALU.subtract)\
                           .then_inc(w_free[slot], 1)
                    ln.run(dve, n, [later(wyt, k) for k in range(2)], lambda w: dve.wait_ge(w_full, w[2] + 1), w_free, ps, 6,
                           x_res, xres_in, y_out)

            program(dve, Vector())

        @block.scalar
        def _(act):
            act.wait_ge(loaded, 16 * 6)
            act.activation(w_hl[:, 0], w_raw[:], ACT.Copy).then_inc(w_split, 1)
            act.wait_ge(set_up, SETS)

            class Scalar(Stages):
                def transpose_x(self, n, w):
                    for k in range(KD):
                        slot, _, count = later(w, k)
                        act.wait_ge(w_full, count + 1)
                        act.activation(xt[:, 0, k], ps[:, 6 + slot], ACT.Copy).then_inc(hi_done, 1)

                def project(self, u, w):
                    n, q = u
                    for o in range(2):
                        slot, _, count = later(w, o)
                        act.wait_ge(w_full, count + 1)
                        if o == 0 and not (isinstance(n, int) and n == 0 and q == 0):
                            act.wait_ge(qk_out, unit(u, 64, 0))
                        act.activation(qk[:, o, 0], ps[:, 6 + slot], ACT.Identity, bias=bqk_sb[:, o, q:q + 1])\
                           .then_inc(hi_done, 1)

                def slot(self, e, m, w):
                    for kind, k in slot_order(e, m):
                        if kind != "t":
                            continue
                        step, r = k // 4, k % 4
                        wd = width(step % NT)
                        act.wait_ge(t_full, unit(e, TILES, k + 1))
                        if r == 0:
                            act.wait_ge(pv_step, unit(e, STEPS, step + 1))
                        act.activation(probs[:, (step % 2) * 4 + r, 0:wd], ps[:, 2 + k % 2, 0:wd], ACT.Exp,
                                       scale=HD ** -0.5).then_inc(t_free, 1)
                        if k == 20:
                            self.copy_out(e, 0)
                    if e:
                        self.copy_out(e, 1)

                def copy_out(self, u, g):
                    act.wait_ge(pv_step, unit(u, STEPS, 4 * g + 4 + 2))
                    act.activation(pv_sb[g][:], ps[:, 4 + g], ACT.Copy).then_inc(pv_free, 1)

                def maxima(self, u, w):
                    slot, _, count = w
                    act.wait_ge(w_full, count + 1)
                    n, q = u
                    if not (isinstance(n, int) and n == 0 and q == 0):
                        act.wait_ge(mrow_in[1 - q], n * 32 + (32 if q else 0))
                    act.activation(mrow[:, :], ps[0:64, 6 + slot, 0:P], ACT.Copy).then_inc(w_free[slot], 1)

                def output(self, n, wot, wo_, wyt):
                    for k in range(KD):
                        slot, _, count = later(wot, k)
                        act.wait_ge(w_full, count + 1)
                        act.activation(o_hl[:, 0, k], ps[:, 6 + slot], ACT.Copy).then_inc(o_split, 1)
                    for k in range(KD):
                        slot, _, count = later(wo_, k)
                        act.wait_ge(w_full, count + 1)
                        act.activation(y_sb[:, k], ps[:, 6 + slot], ACT.Identity, bias=bo_sb[:, k:k + 1])\
                           .then_inc(w_free[slot], 1)

            program(act, Scalar())

        @block.tensor
        def _(pe):
            pe.wait_ge(set_up, SETS)
            pe.wait_ge(w_split, 2)

            def take(w):
                slot, before, _ = w
                pe.wait_ge(w_free[slot], before + 1)
                return ps[:, 6 + slot]

            def emptied(w):
                slot, before, _ = w
                pe.wait_ge(w_free[slot], before + 2)

            class Tensor(Stages):
                def transpose_x(self, n, w):
                    pe.wait_ge(x_in_sem, n * 16 + 16)
                    for k in range(KD):
                        bank = take(later(w, k))
                        for t in range(NT):
                            ins = pe.transpose(bank[:, t * P:(t + 1) * P], x_sb[:, t, k * P:(k + 1) * P], ident[:])
                        ins.then_inc(w_full, 1)
                    self.w_x = w

                def project(self, u, w):
                    n, q = u
                    if q == 0:
                        for k in range(KD):
                            emptied(later(self.w_x, k))
                    for o in range(2):
                        bank = take(later(w, o))
                        matmul3(pe, bank, w_hl, xt, slice(o * D + q * P, o * D + (q + 1) * P), slice(0, S), KD)\
                            .then_inc(w_full, 1)
                    bank = take(later(w, 2))
                    for t in range(NT):
                        ins = matmul3(pe, bank[:, t * P:(t + 1) * P], xt, w_hl, slice(t * P, (t + 1) * P),
                                      slice(2 * D + q * P, 2 * D + (q + 1) * P), KD)
                    ins.then_inc(w_full, 1)

                def slot(self, e, m, w):
                    for kind, k in slot_order(e, m):
                        if kind == "t":
                            if k == 0:
                                pe.wait_ge(mrow_in[e[1]], e[0] * 32 + 32)
                            g, tb, r = k // 16, k // 4 % NT, k % 4
                            h, wd = 4 * g + r, width(tb)
                            pe.wait_ge(t_free, unit(e, TILES, k + 1))
                            tile = ps[:, 2 + k % 2, 0:wd]
                            pe.matmul(tile, k_st[e[1]][:, h, tb * P:(tb + 1) * P], q_st[e[1]][:, h // 2, tb * P:S],
                                      start=True, stop=False)
                            pe.matmul(tile[:, 0:P], ident_b[:], causal_b[:, 1], start=False, stop=True)\
                              .then_inc(t_full, 1)
                        elif kind == "s":
                            if k == 0:
                                pe.wait_ge(stack_in[m[1]], m[0] * 160 + 160)
                            h, i = k // NT, k % NT
                            pe.wait_ge(s_free, unit(m, TILES, k + 1))
                            tile = ps[:, k % 2, 0:(i + 1) * P]
                            pe.matmul(tile, q_st[m[1]][:, h // 2, i * P:(i + 1) * P], k_st[m[1]][:, h, 0:(i + 1) * P],
                                      start=True, stop=False)
                            pe.matmul(tile[:, i * P:], ident_b[:], causal_b[:, 0], start=False, stop=True)\
                              .then_inc(s_full, 1)
                        elif kind == "pv":
                            g, tb = k // NT, k % NT
                            if tb == 0:
                                pe.wait_ge(pv_free, unit(e, 2, g + 1))
                            pe.wait_ge(t_free, unit(e, TILES, 4 * k + 4 + 2))
                            for r in range(4):
                                ins = pe.matmul(ps[32 * r:32 * r + 32, 4 + g, tb * P:S],
                                                v_aug[e[1]][:, tb, 4 * g + r, :],
                                                probs[:, (k % 2) * 4 + r, 0:width(tb)],
                                                start=(tb == 0), stop=(tb == NT - 1), skip_group_check=True)
                            ins.then_inc(pv_step, 1)
                        else:
                            self.normalise(e, 0, w)

                def maxima(self, u, w):
                    bank = take(w)
                    settle(pe, nm_ready, unit(u, 1, 1), ln.passed)
                    pe.transpose(bank[0:64, 0:P], raw(nmax2[:]).rearrange("p a i r -> p (a i r)"), ident[:])\
                      .then_inc(w_full, 1)

                def normalise(self, u, g, w):
                    bank = take(w)
                    pe.wait_ge(pv_free, unit(u, 2, g + 1 + 2))
                    for t in range(NT):
                        ins = pe.transpose(bank[:, t * P:(t + 1) * P], pv_sb[g][:, t * P:(t + 1) * P], ident[:])
                    ins.then_inc(w_full, 1)
                    self.w_n = w

                def output(self, n, wot, wo_, wyt):
                    emptied(self.w_n)
                    for k in range(KD):
                        bank = take(later(wot, k))
                        for t in range(NT):
                            ins = pe.transpose(bank[:, t * P:(t + 1) * P], o_tok[:, t, k * P:(k + 1) * P], ident[:])
                        ins.then_inc(w_full, 1)
                    for k in range(KD):
                        emptied(later(wot, k))
                    for k in range(KD):
                        bank = take(later(wo_, k))
                        matmul3(pe, bank, w_hl, o_hl, slice(3 * D + k * P, 3 * D + (k + 1) * P), slice(0, S), KD)\
                            .then_inc(w_full, 1)
                    for k in range(KD):
                        emptied(later(wo_, k))
                    ln.transposes(pe, take, [later(wyt, k) for k in range(2)], y_sb, ident, [w_full, w_full])

            program(pe, Tensor())


HID0 = 3 * 1024
TILES0 = HID0 // P
THIRD = TILES0 // 3
RING_H = 3


def feed_forward0(nc, x_in, w1, w2, b1, b2, gate, ident_in, x_out):
    x_view = x_in.rearrange("(n t p) d -> n p t d", t=NT, p=P)
    out_view = x_out.rearrange("(n t p) d -> n p t d", t=NT, p=P)
    w1_view = w1.rearrange("(k p) (c n) -> c p k n", p=P, c=3)
    w2_view = w2.rearrange("(c j p) n -> c p j n", p=P, c=3)
    ctx = ExitStack()
    with ctx:
        ph = Phase(nc, ctx, "f0")
        sb, sem = ph.sb, ph.sem
        stage = [sb(f"stage{i}", [P, 2 * 1024]) for i in range(2)]
        w1_hl = sb("w1", [P, 2, KD, HID0], F32R)
        w2_hl = sb("w2", [P, 2, TILES0, D], F32R)
        b1_sb = sb("b1", [P, TILES0])
        b2_sb = sb("b2", [P, 3, KD])
        b2_sum = sb("b2_sum", [P, 2, KD])
        gate_sb = sb("gate", [P, KD, 2])
        gate_d = sb("gate_d", [P, KD])
        gate_hl = sb("gate_hl", [P, 2, KD, P], F32R)
        ident = sb("ident", [P, P])
        x_sb = sb("x", [P, NT, D])
        x_res = sb("x_res", [P, NT, D])
        xt = sb("xt", [P, 2, KD, S], F32R)
        xm = [sb(f"xm{e}", [P, 2, KD, S], F32R) for e in range(2)]
        chosen0 = sb("chosen0", [P, S])
        h_f = sb("h_f", [P, RING_H, S])
        h_hl = sb("h_hl", [P, RING_H, 2, 1, S], F32R)
        y_sb = sb("y", [P, KD, S])
        ln = LayerNorm(ph)
        ps = ph.psum("ps", [P, 8, S])

        loaded = sem("loaded")
        set_up = sem("set_up")
        staged = [sem("staged0"), sem("staged1")]
        w_hi = sem("w_hi")
        w_lo = sem("w_lo")
        x_in_sem = sem("x_in")
        xres_in = sem("xres_in")
        full = [sem("full0"), sem("full1")]
        free = [sem("free0"), sem("free1")]
        xt_hi = sem("xt_hi")
        h_full = sem("h_full")
        h_free = sem("h_free")
        h_hi = sem("h_hi")
        h_lo = sem("h_lo")
        down_done = sem("down_done")
        y_free = sem("y_free")
        masked = sem("masked")
        y_out = sem("y_out")

        def use_x(k, n, pre=False):
            return (0, 0 if pre else n * 3 + 2) if k == 0 else (1, 0 if pre else n * 2 + 1)

        def use_gate(n, pre=False):
            return (0, 1 if pre else n * 3 + 3)

        def use_y(n, tail=False):
            return [(0, n * 3 + 2) if tail else (0, n * 3 + 4), (1, n * 2 + 1) if tail else (1, n * 2 + 2)]

        LAST = B - 1
        SETS = 4

        def program(eng, st):
            st.load_x(0)
            st.transpose_x(0, True)
            st.gate(0, True)
            st.mask(0, 0)
            st.mask(0, 1)
            st.tile(0, 0)
            st.tile(0, 1)
            with eng.Fori(0, LAST) as n:
                st.load_res(n)
                for j in range(2, TILES0):
                    st.tile(n, j)
                    st.down(n, j - 2)
                    if j == 3:
                        st.load_x(n + 1)
                    if j == 12:
                        st.transpose_x(n + 1, False)
                    if j == 14:
                        st.gate(n + 1, False)
                    if j == 18:
                        st.mask(n + 1, 0)
                st.down(n, TILES0 - 2)
                st.down(n, TILES0 - 1)
                st.output(n)
                st.mask(n + 1, 1)
                st.tile(n + 1, 0)
                st.tile(n + 1, 1)
                st.norm(n, False)
            n = LAST
            st.load_res(n)
            for j in range(2, TILES0):
                st.tile(n, j)
                st.down(n, j - 2)
            st.down(n, TILES0 - 2)
            st.down(n, TILES0 - 1)
            st.output(n)
            st.norm(n, True)

        class Stages:
            def load_x(self, n): pass
            def load_res(self, n): pass
            def transpose_x(self, n, pre): pass
            def gate(self, n, pre): pass
            def mask(self, n, e): pass
            def tile(self, n, j): pass
            def down(self, n, j): pass
            def output(self, n): pass
            def norm(self, n, tail): pass

        block = ctx.enter_context(nc.Block())

        @block.sync
        def _(sp):
            for dst, src in ((ident[:], ident_in), (b1_sb[:], b1), (b2_sb[:], b2), (gate_sb[:], gate)):
                sp.dma_start(dst, src).then_inc(loaded, 16)
            for s, v in ((free[0], 1), (free[1], 1), (h_free, 4), (down_done, 3), (y_free, 2),
                         (ln.stat, 1), (ln.applied, 1), (ln.rooted, 1), (y_out, 1)):
                sp.sem_inc(s, v)
            for c in range(6):
                if c >= 2:
                    sp.wait_ge(w_lo, 2 + c - 1)
                    sp.wait_ge(staged[c % 2], 16 * (c // 2))
                src = w1_view[c // 2] if c % 2 == 0 else w2_view[c // 2]
                dst = stage[c % 2][:].rearrange("p (k n) -> p k n", k=KD if c % 2 == 0 else THIRD)
                sp.dma_start(dst, src).then_inc(staged[c % 2], 16)

            class Sync(Stages):
                def load_x(self, n):
                    if not isinstance(n, int):
                        sp.wait_ge(h_free, n * TILES0 - TILES0 + 6)
                    sp.dma_start(x_sb[:], x_view[n]).then_inc(x_in_sem, 16)

                def load_res(self, n):
                    sp.wait_ge(ln.stat, n * 8 + 1)
                    sp.dma_start(x_res[:], x_view[n]).then_inc(xres_in, 16)

                def norm(self, n, tail):
                    sp.wait_ge(ln.applied, n * NT + (NT + 1))
                    sp.dma_start(out_view[n], ln.out[:]).then_inc(y_out, 16)

            program(sp, Sync())
            sp.wait_ge(y_out, 16 * B + 1)

        @block.gpsimd
        def _(pool):
            ln.constants(pool, set_up)

            class Pool(Stages):
                def norm(self, n, tail):
                    ln.root(pool, n)

            pool.wait_ge(set_up, SETS)
            program(pool, Pool())

        @block.vector
        def _(dve):
            dve.wait_ge(loaded, 64)
            dve.tensor_tensor(gate_d[:], gate_sb[:, :, 0], gate_sb[:, :, 1], ALU.subtract).then_inc(set_up, 1)
            dve.tensor_tensor(b2_sum[:, 0], b2_sb[:, 0], b2_sb[:, 1], ALU.add).then_inc(set_up, 1)
            dve.wait_ge(set_up, 3)
            dve.tensor_tensor(b2_sum[:, 1], b2_sum[:, 0], b2_sb[:, 2], ALU.add).then_inc(set_up, 1)
            spread = gate_d[:].unsqueeze(2).broadcast_to([P, KD, P])
            dve.tensor_copy(gate_hl[:, 0], spread).then_inc(w_lo, 1)
            dve.wait_ge(w_lo, 1)
            dve.tensor_tensor(gate_hl[:, 1], spread, raw(gate_hl[:, 0]), ALU.subtract).then_inc(w_lo, 1)
            for c in range(6):
                dve.wait_ge(w_hi, c + 1)
                third = c // 2
                if c % 2 == 0:
                    at, view = slice(third * 1024, third * 1024 + 1024), stage[0][:].rearrange("p (k n) -> p k n", k=KD)
                    dve.tensor_tensor(w1_hl[:, 1, :, at], view, raw(w1_hl[:, 0, :, at]), ALU.subtract).then_inc(w_lo, 1)
                else:
                    at, view = slice(third * THIRD, third * THIRD + THIRD), stage[1][:].rearrange("p (j n) -> p j n", j=THIRD)
                    dve.tensor_tensor(w2_hl[:, 1, at], view, raw(w2_hl[:, 0, at]), ALU.subtract).then_inc(w_lo, 1)

            class Vector(Stages):
                def transpose_x(self, n, pre):
                    for k in range(KD):
                        bank, before = use_x(k, n - 1 if not pre else 0, pre)
                        dve.wait_ge(xt_hi, n * KD + (k + 1))
                        dve.tensor_tensor(xt[:, 1, k], ps[:, 6 + bank], raw(xt[:, 0, k]), ALU.subtract)\
                           .then_inc(free[bank], 1)

                def gate(self, n, pre):
                    bank, before = use_gate(n - 1 if not pre else 0, pre)
                    dve.wait_ge(full[bank], before + 1)
                    dve.tensor_scalar(chosen0[:], ps[:, 6 + bank], 0.0, None, ALU.is_ge).then_inc(free[bank], 1)

                def mask(self, n, e):
                    if e == 0:
                        bank, before = use_gate(n - 1 if not isinstance(n, int) else 0, isinstance(n, int))
                        dve.wait_ge(free[bank], before + 2)
                        if not isinstance(n, int):
                            dve.wait_ge(h_full, n * TILES0 - THIRD)
                        dve.tensor_tensor(xm[0][:].rearrange("p i k s -> p (i k) s"),
                                          raw(xt[:]).rearrange("p i k s -> p (i k) s"),
                                          chosen0[:].unsqueeze(1).broadcast_to([P, 2 * KD, S]), ALU.mult)\
                           .then_inc(masked, 1)
                    else:
                        dve.wait_ge(masked, n * 2 + 1)
                        if not isinstance(n, int):
                            dve.wait_ge(h_full, n * TILES0)
                        dve.tensor_tensor(xm[1][:].rearrange("p i k s -> p (i k s)"),
                                          raw(xt[:]).rearrange("p i k s -> p (i k s)"),
                                          raw(xm[0][:]).rearrange("p i k s -> p (i k s)"), ALU.subtract)\
                           .then_inc(masked, 1)

                def tile(self, n, j):
                    dve.wait_ge(h_hi, n * TILES0 + (j + 1))
                    r = j % RING_H
                    dve.tensor_tensor(h_hl[:, r, 1, 0], h_f[:, r], raw(h_hl[:, r, 0, 0]), ALU.subtract)\
                       .then_inc(h_lo, 1)

                def norm(self, n, tail):
                    ln.run(dve, n, use_y(n, tail), lambda w: dve.wait_ge(full[w[0]], w[1] + 1), free, ps, 6,
                           x_res, xres_in, y_out)

            dve.wait_ge(set_up, SETS)
            program(dve, Vector())

        @block.scalar
        def _(act):
            act.wait_ge(loaded, 64)
            for c in range(6):
                act.wait_ge(staged[c % 2], 16 * (c // 2 + 1))
                third = c // 2
                if c % 2 == 0:
                    at = slice(third * 1024, third * 1024 + 1024)
                    act.activation(w1_hl[:, 0, :, at], stage[0][:].rearrange("p (k n) -> p k n", k=KD), ACT.Copy)\
                       .then_inc(w_hi, 1)
                else:
                    at = slice(third * THIRD, third * THIRD + THIRD)
                    act.activation(w2_hl[:, 0, at], stage[1][:].rearrange("p (j n) -> p j n", j=THIRD), ACT.Copy)\
                       .then_inc(w_hi, 1)

            class Scalar(Stages):
                def transpose_x(self, n, pre):
                    for k in range(KD):
                        bank, before = use_x(k, n - 1 if not pre else 0, pre)
                        act.wait_ge(full[bank], before + 1)
                        act.activation(xt[:, 0, k], ps[:, 6 + bank], ACT.Copy).then_inc(xt_hi, 1)

                def tile(self, n, j):
                    r = j % RING_H
                    act.wait_ge(h_full, n * TILES0 + (j + 1))
                    act.wait_ge(down_done, n * TILES0 + (j + 1))
                    act.activation(h_f[:, r], ps[:, j % 4], ACT.Relu, bias=b1_sb[:, j:j + 1]).then_inc(h_free, 1)
                    act.wait_ge(h_free, n * TILES0 + (j + 5))
                    act.activation(h_hl[:, r, 0, 0], h_f[:, r], ACT.Copy).then_inc(h_hi, 1)

                def output(self, n):
                    act.wait_ge(down_done, n * TILES0 + (TILES0 + 3))
                    for k in range(KD):
                        act.activation(y_sb[:, k], ps[:, 4 + k], ACT.Identity, bias=b2_sum[:, 1, k:k + 1])\
                           .then_inc(y_free, 1)

            act.wait_ge(set_up, SETS)
            program(act, Scalar())

        @block.tensor
        def _(pe):
            pe.wait_ge(set_up, SETS)
            pe.wait_ge(w_lo, 8)

            def take(use):
                pe.wait_ge(free[use[0]], use[1] + 1)
                return ps[:, 6 + use[0]]

            class Tensor(Stages):
                def transpose_x(self, n, pre):
                    pe.wait_ge(x_in_sem, n * 16 + 16)
                    for k in range(KD):
                        use = use_x(k, n - 1 if not pre else 0, pre)
                        bank = take(use)
                        for t in range(NT):
                            ins = pe.transpose(bank[:, t * P:(t + 1) * P], x_sb[:, t, k * P:(k + 1) * P], ident[:])
                        ins.then_inc(full[use[0]], 1)

                def gate(self, n, pre):
                    m = n - 1 if not pre else 0
                    for k in range(KD):
                        bank, before = use_x(k, m, pre)
                        pe.wait_ge(free[bank], before + 2)
                    use = use_gate(m, pre)
                    matmul3(pe, take(use), gate_hl, xt, slice(0, P), slice(0, S), KD).then_inc(full[use[0]], 1)

                def tile(self, n, j):
                    third = j // THIRD
                    pe.wait_ge(h_free, n * TILES0 + (j + 1))
                    if j == THIRD:
                        pe.wait_ge(masked, n * 2 + 1)
                    if j == 2 * THIRD:
                        pe.wait_ge(masked, n * 2 + 2)
                    x = xt if third == 0 else xm[third - 1]
                    matmul3(pe, ps[:, j % 4], w1_hl, x, slice(j * P, (j + 1) * P), slice(0, S), KD).then_inc(h_full, 1)

                def down(self, n, j):
                    r = j % RING_H
                    pe.wait_ge(h_lo, n * TILES0 + (j + 1))
                    if j == 0:
                        pe.wait_ge(y_free, n * 2 + 2)
                    for k in range(KD):
                        for i, (a, b) in enumerate(TERMS):
                            ins = pe.matmul(ps[:, 4 + k], w2_hl[:, a, j, k * P:(k + 1) * P], h_hl[:, r, b, 0],
                                            start=(j == 0 and i == 0), stop=(j == TILES0 - 1 and i == 2))
                    ins.then_inc(down_done, 1)

                def norm(self, n, tail):
                    pe.wait_ge(y_free, n * 2 + 4)
                    ln.transposes(pe, take, use_y(n, tail), y_sb, ident, full)

            program(pe, Tensor())


KV = 4
REACH = 32
WINDOW = P + 2 * REACH
G_HEADS = 8
G_TILES = 2 * NT * 2
G_STEPS = 2 * NT
C_Q, C_QS, C_K, C_KS, C_V, C_O = 0, D, 2 * D, 2 * D + P, 2 * D + 2 * P, 2 * D + 2 * P + KV * HD
W1_COLS = C_O + D
A1_PRE = 23
A1_LOOP = 34
S_LAG = 2


def attention1(nc, x_in, weights, tables, select, ident_in, band_in, x_out):
    x_view = x_in.rearrange("(n t p) d -> n p t d", t=NT, p=P)
    out_view = x_out.rearrange("(n t p) d -> n p t d", t=NT, p=P)
    ctx = ExitStack()
    with ctx:
        ph = Phase(nc, ctx, "a1")
        sb, sem = ph.sb, ph.sem
        w_raw = sb("w_raw", [P, KD, W1_COLS])
        w_hl = sb("w_hl", [P, 2, KD, W1_COLS], F32R)
        sel_raw = sb("sel_raw", [P, 24, P])
        sel = sb("sel", [P, 24, P], F32R)
        rope = sb("rope", [P, 2, S])
        ident = sb("ident", [P, P])
        ident_b = sb("ident_b", [P, P], BF16)
        band = sb("band", [P, 2, WINDOW])
        band_b = sb("band_b", [P, 2, WINDOW], BF16)
        x_sb = sb("x", [P, NT, D])
        x_res = sb("x_res", [P, NT, D])
        xt = sb("xt", [P, 2, KD, S], F32R)
        rot = [[sb(f"rot{o}{i}", [P, S]) for i in range(2)] for o in range(2)]
        qk = [sb(f"qk{o}", [P, S]) for o in range(2)]
        qk_hl = [sb(f"qk_hl{o}", [P, 2, S], F32R) for o in range(2)]
        q_st = [sb(f"q_st{i}", [P, 4, S], F32R) for i in range(2)]
        k_st = [sb(f"k_st{i}", [P, 2, S], F32R) for i in range(2)]
        v_aug = [sb(f"v_aug{i}", [P, NT, 2, 32]) for i in range(2)]
        nmax = sb("nmax", [P, NT, G_HEADS])
        nmax2 = sb("nmax2", [P, NT, P], F32R)
        m_t = sb("m_t", [P, S], F32R)
        probs = sb("probs", [P, 4, 2 * WINDOW])
        pv_sb = [sb(f"pv_sb{i}", [P, S]) for i in range(2)]
        rden = sb("rden", [P, 2, NT, 4])
        o_tok = sb("o_tok", [P, NT, D])
        o_hl = sb("o_hl", [P, 2, KD, S], F32R)
        y_sb = sb("y", [P, KD, S])
        ln = LayerNorm(ph)

        ps = ph.psum("ps", [P, 8, S])

        loaded = sem("loaded")
        set_up = sem("set_up")
        w_split = sem("w_split")
        x_in_sem = sem("x_in")
        xres_in = sem("xres_in")
        w_full = sem("w_full")
        w_free = [sem("w_free0"), sem("w_free1")]
        xt_hi = sem("xt_hi")
        rotated = sem("rotated")
        qk_hi = sem("qk_hi")
        qk_lo = sem("qk_lo")
        s_full = sem("s_full")
        s_free = sem("s_free")
        t_full = sem("t_full")
        t_free = sem("t_free")
        pv_step = sem("pv_step")
        pv_free = sem("pv_free")
        nm_hi = sem("nm_hi")
        nm_ready = sem("nm_ready")
        rden_ok = sem("rden_ok")
        o_hi = sem("o_hi")
        y_out = sem("y_out")

        def work(c, n):
            return c % 2, c // 2 + n * (A1_LOOP // 2), c + n * A1_LOOP

        def later(w, k):
            slot, before, count = w
            return (slot + k) % 2, before + (slot + k) // 2, count + k

        def unit(u, per, k):
            return u[0] * (2 * per) + (u[1] * per + k)

        def window(block):
            lo, hi = max(0, block * P - REACH), min(S, (block + 1) * P + REACH)
            return lo, hi, lo - (block * P - REACH)

        def tile_at(k):
            return k // (2 * NT), k // 2 % NT, 2 * (k % 2)

        def slot_order(e, m):
            order = []
            lag = S_LAG if e and m else 0
            for k in range(G_TILES + lag):
                if e and k < G_TILES:
                    order.append(("t", k))
                    if k == 10:
                        order.append(("copy", 0))
                    if k % 2 and k >= 3:
                        order.append(("pv", k // 2 - 1))
                    if k == 14:
                        order.append(("norm", 0))
                if m and k >= lag:
                    order.append(("s", k - lag))
            if e:
                order.append(("pv", G_STEPS - 1))
                order.append(("copy", 1))
            return order

        LAST = B - 1
        PRE = {"xt": 0, "p": 2, "t": 13, "p2": 14}
        LOOP = {k: A1_PRE + v for k, v in dict(a_n0=0, a_t=1, a_n1=2, xt=3, p=5, b_n0=16, b_t=17, b_n1=18,
                                               p2=19, ot=28, o=30, yt=32).items()}
        TAIL = {k: A1_PRE + v for k, v in dict(a_n0=0, a_t=1, a_n1=2, b_n0=3, b_n1=4, ot=5, o=7, yt=9).items()}

        def program(eng, st):
            st.load_x(0)
            st.transpose_x(0, work(PRE["xt"], 0))
            st.project((0, 0), work(PRE["p"], 0))
            st.slot(None, (0, 0), None)
            st.maxima((0, 0), work(PRE["t"], 0))
            st.project((0, 1), work(PRE["p2"], 0))
            with eng.Fori(0, LAST) as n:
                st.load_res(n)
                st.slot((n, 0), (n, 1), work(LOOP["a_n0"], n))
                st.maxima((n, 1), work(LOOP["a_t"], n))
                st.normalise((n, 0), 1, work(LOOP["a_n1"], n))
                st.load_x(n + 1)
                st.transpose_x(n + 1, work(LOOP["xt"], n))
                st.project((n + 1, 0), work(LOOP["p"], n))
                st.slot((n, 1), (n + 1, 0), work(LOOP["b_n0"], n))
                st.maxima((n + 1, 0), work(LOOP["b_t"], n))
                st.normalise((n, 1), 1, work(LOOP["b_n1"], n))
                st.project((n + 1, 1), work(LOOP["p2"], n))
                st.output(n, work(LOOP["ot"], n), work(LOOP["o"], n), work(LOOP["yt"], n))
            n = LAST
            st.load_res(n)
            st.slot((n, 0), (n, 1), work(TAIL["a_n0"], n))
            st.maxima((n, 1), work(TAIL["a_t"], n))
            st.normalise((n, 0), 1, work(TAIL["a_n1"], n))
            st.slot((n, 1), None, work(TAIL["b_n0"], n))
            st.normalise((n, 1), 1, work(TAIL["b_n1"], n))
            st.output(n, work(TAIL["ot"], n), work(TAIL["o"], n), work(TAIL["yt"], n))

        def project_uses(u, w):
            ops = (0, 1) if u[1] == 0 else (0,)
            at = 2 * len(ops)
            return (ops, {o: later(w, 2 * o) for o in ops}, later(w, at),
                    [later(w, at + 1 + r) for r in range(4)], [later(w, at + 5 + c) for c in range(2)])

        def operand(u, o):
            return u[0] * 3 + (2 if u[1] else o)

        class Stages:
            def load_x(self, n): pass
            def load_res(self, n): pass
            def transpose_x(self, n, w): pass
            def project(self, u, w): pass
            def slot(self, e, m, w): pass
            def maxima(self, u, w): pass
            def normalise(self, u, g, w): pass
            def output(self, n, wot, wo_, wyt): pass

        SETS = 6
        block = ctx.enter_context(nc.Block())

        @block.sync
        def _(sp):
            for dst, src in ((w_raw[:], weights.rearrange("(k p) n -> p k n", p=P)), (sel_raw[:], select),
                             (rope[:], tables), (ident[:], ident_in), (band[:], band_in)):
                sp.dma_start(dst, src).then_inc(loaded, 16)
            for s, v in ((w_free[0], 1), (w_free[1], 1), (s_free, 2), (t_free, 2), (pv_step, 2), (pv_free, 2),
                         (ln.stat, 1), (ln.applied, 1), (ln.rooted, 1), (y_out, 1)):
                sp.sem_inc(s, v)

            class Sync(Stages):
                def load_x(self, n):
                    if not isinstance(n, int):
                        sp.wait_ge(rotated, n * 3)
                    sp.dma_start(x_sb[:], x_view[n]).then_inc(x_in_sem, 16)

                def load_res(self, n):
                    sp.wait_ge(ln.stat, n * 8 + 1)
                    sp.dma_start(x_res[:], x_view[n]).then_inc(xres_in, 16)

                def output(self, n, wot, wo_, wyt):
                    sp.wait_ge(ln.applied, n * NT + (NT + 1))
                    sp.dma_start(out_view[n], ln.out[:]).then_inc(y_out, 16)

            program(sp, Sync())
            sp.wait_ge(y_out, 16 * B + 1)

        @block.gpsimd
        def _(pool):
            pool.memset(raw(nmax2[:]), 0.0).then_inc(set_up, 1)
            for i in range(2):
                pool.memset(v_aug[i][:], 1.0).then_inc(set_up, 1)
            ln.constants(pool, set_up)
            pool.wait_ge(set_up, SETS)

            class Pool(Stages):
                def project(self, u, w):
                    ops, pair, _, _, _ = project_uses(u, w)
                    for o in ops:
                        for i in range(2):
                            slot, before, _ = later(pair[o], i)
                            pool.wait_ge(w_free[slot], before + 2)
                        pool.tensor_tensor(qk[o][:], rot[o][0][:], rot[o][1][:], ALU.add).then_inc(rotated, 1)
                    for o in ops:
                        pool.wait_ge(qk_hi, operand(u, o) + 1)
                        pool.tensor_tensor(qk_hl[o][:, 1], qk[o][:], raw(qk_hl[o][:, 0]), ALU.subtract)\
                            .then_inc(qk_lo, 1)

                def output(self, n, wot, wo_, wyt):
                    ln.root(pool, n)

            program(pool, Pool())

        @block.vector
        def _(dve):
            dve.wait_ge(loaded, 16 * 5)
            dve.tensor_copy(ident_b[:], ident[:]).then_inc(set_up, 1)
            dve.tensor_copy(band_b[:], band[:]).then_inc(set_up, 1)
            dve.wait_ge(w_split, 2)
            dve.tensor_tensor(w_hl[:, 1], w_raw[:], raw(w_hl[:, 0]), ALU.subtract).then_inc(w_split, 1)
            dve.wait_ge(set_up, SETS)

            class Vector(Stages):
                def transpose_x(self, n, w):
                    for k in range(KD):
                        slot, _, _ = later(w, k)
                        dve.wait_ge(xt_hi, n * KD + (k + 1))
                        dve.tensor_tensor(xt[:, 1, k], ps[:, 6 + slot], raw(xt[:, 0, k]), ALU.subtract)\
                           .then_inc(w_free[slot], 1)

                def project(self, u, w):
                    q = u[1]
                    ops, pair, v_use, q_uses, k_uses = project_uses(u, w)
                    for o in ops:
                        for i in range(2):
                            slot, _, count = later(pair[o], i)
                            dve.wait_ge(w_full, count + 1)
                            dve.tensor_tensor(rot[o][i][:], ps[:, 6 + slot], rope[:, i], ALU.mult)\
                               .then_inc(w_free[slot], 1)
                    slot, _, count = v_use
                    dve.wait_ge(w_full, count + 1)
                    dve.tensor_copy(v_aug[q][:, :, :, 0:HD],
                                    ps[:, 6 + slot, 0:NT * 2 * HD].rearrange("p (t c e) -> p t c e", t=NT, e=HD))\
                       .then_inc(w_free[slot], 1)
                    for dst, (slot, _, count) in ((q_st[q][:, 1], q_uses[1]), (q_st[q][:, 3], q_uses[3]),
                                                  (k_st[q][:, 1], k_uses[1])):
                        dve.wait_ge(w_full, count + 1)
                        dve.tensor_copy(dst, ps[:, 6 + slot]).then_inc(w_free[slot], 1)

                def slot(self, e, m, w):
                    for kind, k in slot_order(e, m):
                        if kind == "s":
                            c, i, r = tile_at(k)
                            lo, hi, _ = window(i)
                            dve.wait_ge(s_full, unit(m, G_TILES, k + 1))
                            dve.tensor_reduce(nmax[:, i, 4 * c + r:4 * c + r + 2],
                                              ps[:, k % 2, 0:2 * (hi - lo)].rearrange("p (h s) -> p h s", h=2),
                                              AX.X, ALU.max, negate=True).then_inc(s_free, 1)
                        elif kind == "norm":
                            self.normalise(e, 0, w)

                def maxima(self, u, w):
                    dve.wait_ge(s_free, unit(u, G_TILES, G_TILES + 2))
                    dve.tensor_copy(nmax2[:, :, 0:G_HEADS], nmax[:]).then_inc(nm_hi, 1)
                    dve.wait_ge(nm_hi, unit(u, 1, 1))
                    dve.tensor_tensor(nmax2[:, :, G_HEADS:2 * G_HEADS], nmax[:], raw(nmax2[:, :, 0:G_HEADS]),
                                      ALU.subtract).then_inc(nm_ready, 1)

                def normalise(self, u, g, w):
                    slot, _, count = w
                    dve.wait_ge(w_full, count + 1)
                    tile = ps[:, 6 + slot].rearrange("p (t r c) -> p t r c", t=NT, r=4)
                    dve.reciprocal(rden[:, g], tile[:, :, :, HD]).then_inc(rden_ok, 1)
                    dve.wait_ge(rden_ok, unit(u, 2, g + 1))
                    at = (u[1] * 2 + g) * 4 * HD
                    dve.tensor_tensor(o_tok[:, :, at:at + 4 * HD].rearrange("p t (r e) -> p t r e", e=HD),
                                      tile[:, :, :, 0:HD],
                                      rden[:, g].unsqueeze(3).broadcast_to([P, NT, 4, HD]),
                                      ALU.mult).then_inc(w_free[slot], 1)

                def output(self, n, wot, wo_, wyt):
                    for k in range(KD):
                        slot, _, _ = later(wot, k)
                        dve.wait_ge(o_hi, n * KD + (k + 1))
                        dve.tensor_tensor(o_hl[:, 1, k], ps[:, 6 + slot], raw(o_hl[:, 0, k]), ALU.subtract)\
                           .then_inc(w_free[slot], 1)
                    ln.run(dve, n, [later(wyt, k) for k in range(2)], lambda w: dve.wait_ge(w_full, w[2] + 1),
                           w_free, ps, 6, x_res, xres_in, y_out)

            program(dve, Vector())

        @block.scalar
        def _(act):
            act.wait_ge(loaded, 16 * 5)
            act.activation(sel[:], sel_raw[:], ACT.Copy).then_inc(w_split, 1)
            act.activation(w_hl[:, 0], w_raw[:], ACT.Copy).then_inc(w_split, 1)
            act.wait_ge(set_up, SETS)

            class Scalar(Stages):
                def transpose_x(self, n, w):
                    for k in range(KD):
                        slot, _, count = later(w, k)
                        act.wait_ge(w_full, count + 1)
                        act.activation(xt[:, 0, k], ps[:, 6 + slot], ACT.Copy).then_inc(xt_hi, 1)

                def project(self, u, w):
                    q = u[1]
                    ops, _, _, q_uses, k_uses = project_uses(u, w)
                    for o in ops:
                        act.wait_ge(rotated, operand(u, o) + 1)
                        act.activation(qk_hl[o][:, 0], qk[o][:], ACT.Copy).then_inc(qk_hi, 1)
                    for dst, (slot, _, count) in ((q_st[q][:, 0], q_uses[0]), (q_st[q][:, 2], q_uses[2]),
                                                  (k_st[q][:, 0], k_uses[0])):
                        act.wait_ge(w_full, count + 1)
                        act.activation(dst, ps[:, 6 + slot], ACT.Copy).then_inc(w_free[slot], 1)

                def slot(self, e, m, w):
                    for kind, k in slot_order(e, m):
                        if kind == "t":
                            lo, hi, _ = window(tile_at(k)[1])
                            act.wait_ge(t_full, unit(e, G_TILES, k + 1))
                            if k % 2 == 0:
                                act.wait_ge(pv_step, unit(e, G_STEPS, k // 2 + 1))
                            act.activation(probs[:, k % 4, 0:2 * (hi - lo)], ps[:, 2 + k % 2, 0:2 * (hi - lo)],
                                           ACT.Exp, scale=HD ** -0.5).then_inc(t_free, 1)
                        elif kind == "copy":
                            act.wait_ge(pv_step, unit(e, G_STEPS, NT * (k + 1) + 2))
                            act.activation(pv_sb[k][:], ps[:, 4 + k], ACT.Copy).then_inc(pv_free, 1)

                def maxima(self, u, w):
                    slot, _, count = w
                    act.wait_ge(w_full, count + 1)
                    act.activation(m_t[:], ps[:, 6 + slot], ACT.Copy).then_inc(w_free[slot], 1)

                def output(self, n, wot, wo_, wyt):
                    for k in range(KD):
                        slot, _, count = later(wot, k)
                        act.wait_ge(w_full, count + 1)
                        act.activation(o_hl[:, 0, k], ps[:, 6 + slot], ACT.Copy).then_inc(o_hi, 1)
                    for k in range(KD):
                        slot, _, count = later(wo_, k)
                        act.wait_ge(w_full, count + 1)
                        act.activation(y_sb[:, k], ps[:, 6 + slot], ACT.Copy).then_inc(w_free[slot], 1)

            program(act, Scalar())

        @block.tensor
        def _(pe):
            pe.wait_ge(set_up, SETS)
            pe.wait_ge(w_split, 3)

            def take(w):
                slot, before, _ = w
                pe.wait_ge(w_free[slot], before + 1)
                return ps[:, 6 + slot]

            def emptied(w):
                slot, before, _ = w
                pe.wait_ge(w_free[slot], before + 2)

            class Tensor(Stages):
                def transpose_x(self, n, w):
                    pe.wait_ge(x_in_sem, n * 16 + 16)
                    for k in range(KD):
                        bank = take(later(w, k))
                        for t in range(NT):
                            ins = pe.transpose(bank[:, t * P:(t + 1) * P], x_sb[:, t, k * P:(k + 1) * P], ident[:])
                        ins.then_inc(w_full, 1)
                    self.w_x = w

                def project(self, u, w):
                    q = u[1]
                    ops, pair, v_use, q_uses, k_uses = project_uses(u, w)
                    if q == 0:
                        for k in range(KD):
                            emptied(later(self.w_x, k))
                    for o in ops:
                        for i in range(2):
                            at = (C_Q, C_QS)[i] + q * P if o == 0 else (C_K, C_KS)[i]
                            matmul3(pe, take(later(pair[o], i)), w_hl, xt, slice(at, at + P), slice(0, S), KD)\
                                .then_inc(w_full, 1)
                    bank = take(v_use)
                    wide = 2 * HD
                    for t in range(NT):
                        ins = matmul3(pe, bank[:, t * wide:(t + 1) * wide], xt, w_hl, slice(t * P, (t + 1) * P),
                                      slice(C_V + q * wide, C_V + (q + 1) * wide), KD)
                    ins.then_inc(w_full, 1)
                    pe.wait_ge(qk_lo, operand(u, ops[-1]) + 1)
                    for o, first, use in ([(0, 2 * r, q_uses[r]) for r in range(4)]
                                          + [(1, 8 + 2 * (2 * q + c), k_uses[c]) for c in range(2)]):
                        bank = take(use)
                        for i in range(2):
                            ins = pe.matmul(bank, sel[:, first + i], qk_hl[o][:, i], start=(i == 0), stop=(i == 1))
                        ins.then_inc(w_full, 1)
                    for c in range(2):
                        emptied(k_uses[c])

                def slot(self, e, m, w):
                    for kind, k in slot_order(e, m):
                        if kind == "t":
                            q = e[1]
                            c, tb, r = tile_at(k)
                            lo, hi, off = window(tb)
                            wd = hi - lo
                            pe.wait_ge(t_free, unit(e, G_TILES, k + 1))
                            tile = ps[:, 2 + k % 2, 0:2 * wd]
                            pe.matmul(tile, ident_b[:], band_b[:, :, off:off + wd], start=True, stop=False)
                            pe.matmul(tile, k_st[q][:, c, tb * P:(tb + 1) * P], q_st[q][:, r:r + 2, lo:hi],
                                      start=False, stop=False)
                            for j in range(2):
                                ins = pe.matmul(tile[:, j * wd:(j + 1) * wd], sel[:, 16 + 4 * c + r + j], m_t[:, lo:hi],
                                                start=False, stop=(j == 1))
                            ins.then_inc(t_full, 1)
                        elif kind == "s":
                            q = m[1]
                            c, i, r = tile_at(k)
                            lo, hi, off = window(i)
                            wd = hi - lo
                            pe.wait_ge(s_free, unit(m, G_TILES, k + 1))
                            tile = ps[:, k % 2, 0:2 * wd]
                            pe.matmul(tile, ident_b[:], band_b[:, :, off:off + wd], start=True, stop=False)
                            for j in range(2):
                                ins = pe.matmul(tile[:, j * wd:(j + 1) * wd], q_st[q][:, r + j, i * P:(i + 1) * P],
                                                k_st[q][:, c, lo:hi], start=False, stop=(j == 1))
                            ins.then_inc(s_full, 1)
                        elif kind == "pv":
                            c, tb = k // NT, k % NT
                            lo, hi, _ = window(tb)
                            wd = hi - lo
                            if tb == 0:
                                pe.wait_ge(pv_free, unit(e, 2, c + 1))
                            pe.wait_ge(t_free, unit(e, G_TILES, 2 * k + 2 + 2))
                            for r in range(4):
                                at = (r % 2) * wd
                                ins = pe.matmul(ps[32 * r:32 * r + 32, 4 + c, lo:hi], v_aug[e[1]][:, tb, c, :],
                                                probs[:, (2 * k + r // 2) % 4, at:at + wd],
                                                start=(tb == 0), stop=(tb == NT - 1), skip_group_check=True)
                            ins.then_inc(pv_step, 1)
                        elif kind == "norm":
                            self.normalise(e, 0, w)

                def maxima(self, u, w):
                    bank = take(w)
                    pe.wait_ge(nm_ready, unit(u, 1, 1))
                    for t in range(NT):
                        ins = pe.transpose(bank[:, t * P:(t + 1) * P], raw(nmax2[:, t]), ident[:])
                    ins.then_inc(w_full, 1)
                    emptied(w)

                def normalise(self, u, g, w):
                    bank = take(w)
                    pe.wait_ge(pv_free, unit(u, 2, g + 1 + 2))
                    for t in range(NT):
                        ins = pe.transpose(bank[:, t * P:(t + 1) * P], pv_sb[g][:, t * P:(t + 1) * P], ident[:])
                    ins.then_inc(w_full, 1)
                    self.w_n = w

                def output(self, n, wot, wo_, wyt):
                    if isinstance(n, int):
                        emptied(self.w_n)
                    for k in range(KD):
                        bank = take(later(wot, k))
                        for t in range(NT):
                            ins = pe.transpose(bank[:, t * P:(t + 1) * P], o_tok[:, t, k * P:(k + 1) * P], ident[:])
                        ins.then_inc(w_full, 1)
                    for k in range(KD):
                        emptied(later(wot, k))
                    for k in range(KD):
                        matmul3(pe, take(later(wo_, k)), w_hl, o_hl, slice(C_O + k * P, C_O + (k + 1) * P),
                                slice(0, S), KD).then_inc(w_full, 1)
                    for k in range(KD):
                        emptied(later(wo_, k))
                    ln.transposes(pe, take, [later(wyt, k) for k in range(2)], y_sb, ident, [w_full, w_full])

            program(pe, Tensor())


E = 16
GROUPS = 4
EPG = E // GROUPS
TOP_GROUPS = 2
TOP_K = 4
HID_SHARED = 512
HID_EXPERT = 64
HID1 = HID_SHARED + E * HID_EXPERT
T_SHARED = HID_SHARED // P
TILES1 = HID1 // P
RING1 = 3
BIG = 1.0e30
ROUTE = 27
F1_PRE = 3
F1_LOOP = 14


def feed_forward1(nc, x_in, w_gu, w_down, w_router, bias, lower, spread, ident_in, x_out):
    x_view = x_in.rearrange("(n t p) d -> n p t d", t=NT, p=P)
    out_view = x_out.rearrange("(n t p) d -> n p t d", t=NT, p=P)
    gu_view = w_gu.rearrange("(k p) (c n) -> c p k n", p=P, c=3)
    down_view = w_down.rearrange("(c j p) n -> c p j n", p=P, c=2)
    ctx = ExitStack()
    with ctx:
        ph = Phase(nc, ctx, "f1")
        sb, sem = ph.sb, ph.sem
        stage = [sb(f"stage{i}", [P, 2 * 1024]) for i in range(2)]
        gu_hl = sb("gu", [P, 2, KD, 2 * HID1], F32R)
        down_hl = sb("down", [P, 2, TILES1, D], F32R)
        router_sb = sb("router", [P, KD, E])
        router_hl = sb("router_hl", [P, 2, KD, E], F32R)
        bias_sb = sb("bias", [P, E])
        lower_sb = sb("lower", [P, E, E])
        spread_sb = sb("spread", [P, E // 2, P])
        spread_r = sb("spread_r", [P, E // 2, P], F32R)
        ident = sb("ident", [P, P])
        x_sb = sb("x", [P, NT, D])
        x_res = sb("x_res", [P, NT, D])
        xt = sb("xt", [P, 2, KD, S], F32R)
        e_neg = sb("e_neg", [P, NT, E])
        denom = sb("denom", [P, NT, E])
        score = sb("score", [P, NT, E])
        biased = sb("biased", [P, NT, E])
        pair_max = sb("pair_max", [P, NT, GROUPS, 2])
        pair_min = sb("pair_min", [P, NT, GROUPS, 2])
        top = sb("top", [P, 4, NT, GROUPS])
        group = sb("group", [P, NT, GROUPS])
        beats_g = sb("beats_g", [P, 2, NT, GROUPS, GROUPS])
        rank_g = sb("rank_g", [P, NT, GROUPS])
        keep_g = sb("keep_g", [P, 2, NT, GROUPS])
        masked = sb("masked", [P, 2, NT, E])
        beats = sb("beats", [P, 2, NT, E, E])
        rank = sb("rank", [P, NT, E])
        chosen = sb("chosen", [P, NT, E])
        total = sb("total", [P, 2, NT])
        inverse = sb("inverse", [P, NT])
        combine = sb("combine", [P, NT, E])
        combine2 = sb("combine2", [P, NT, P], F32R)
        combine_t = sb("combine_t", [P, S], F32R)
        tanh = sb("tanh", [P, 2, S])
        gated = sb("gated", [P, 2, S])
        scaled = sb("scaled", [P, 2, S])
        h_f = sb("h_f", [P, RING1, S])
        h_hl = sb("h_hl", [P, RING1, 2, S], F32R)
        y_sb = sb("y", [P, KD, S])
        ln = LayerNorm(ph)
        ps = ph.psum("ps", [P, 8, S])

        loaded = sem("loaded")
        set_up = sem("set_up")
        staged = [sem("staged0"), sem("staged1")]
        w_hi = sem("w_hi")
        w_lo = sem("w_lo")
        x_in_sem = sem("x_in")
        xres_in = sem("xres_in")
        w_full = sem("w_full")
        w_free = [sem("w_free0"), sem("w_free1")]
        xt_hi = sem("xt_hi")
        g_full = sem("g_full")
        u_full = sem("u_full")
        tanh_done = sem("tanh_done")
        gated_done = sem("gated_done")
        h_made = sem("h_made")
        h_hi = sem("h_hi")
        h_lo = sem("h_lo")
        y_full = sem("y_full")
        y_free = sem("y_free")
        routed = sem("routed")
        combined = sem("combined")
        y_out = sem("y_out")

        def work(c, n):
            return c % 2, c // 2 + n * (F1_LOOP // 2), c + n * F1_LOOP

        def later(w, k):
            slot, before, count = w
            return (slot + k) % 2, before + (slot + k) // 2, count + k

        LAST = B - 1
        LOOP = {k: F1_PRE + v for k, v in dict(comb=0, c=1, xt=9, logits=11, yt=12).items()}
        TAIL = {k: F1_PRE + v for k, v in dict(comb=0, c=1, yt=9).items()}

        def program(eng, st):
            st.load_x(0)
            st.transpose_x(0, work(0, 0))
            st.logits(0, work(2, 0))
            st.tile(0, 0, None)
            st.tile(0, 1, None)
            st.route(0, 0, work(2, 0))
            with eng.Fori(0, LAST) as n:
                turn(st, n, LOOP)
                st.load_x(n + 1)
                st.transpose_x(n + 1, work(LOOP["xt"], n))
                st.down(n, TILES1 - 2)
                st.down(n, TILES1 - 1)
                st.output(n)
                st.logits(n + 1, work(LOOP["logits"], n))
                st.tile(n + 1, 0, None)
                st.tile(n + 1, 1, None)
                st.norm(n, work(LOOP["yt"], n))
                st.route(n + 1, 0, work(LOOP["logits"], n))
            turn(st, LAST, TAIL)
            st.down(LAST, TILES1 - 2)
            st.down(LAST, TILES1 - 1)
            st.output(LAST)
            st.norm(LAST, work(TAIL["yt"], LAST))

        def turn(st, n, uses):
            st.load_res(n)
            for j in range(2, TILES1):
                c_use = work(uses["c"] + j - T_SHARED, n) if j >= T_SHARED else None
                if j == T_SHARED:
                    st.combine(n, work(uses["comb"], n))
                st.tile(n, j, c_use)
                if j < T_SHARED:
                    st.route(n, j - 1, None)
                st.down(n, j - 2)

        class Stages:
            def load_x(self, n): pass
            def load_res(self, n): pass
            def transpose_x(self, n, w): pass
            def logits(self, n, w): pass
            def route(self, n, part, w): pass
            def combine(self, n, w): pass
            def tile(self, n, j, w): pass
            def down(self, n, j): pass
            def output(self, n): pass
            def norm(self, n, w): pass

        SETS = 5
        PIECES = 5
        block = ctx.enter_context(nc.Block())

        def piece(c):
            if c < 3:
                at = slice(c * 1024, (c + 1) * 1024)
                return (stage[c % 2][:].rearrange("p (k n) -> p k n", k=KD), gu_view[c],
                        gu_hl[:, 0, :, at], gu_hl[:, 1, :, at])
            at = slice((c - 3) * 6, (c - 3) * 6 + 6)
            return (stage[c % 2][:, 0:6 * D].rearrange("p (j n) -> p j n", j=6), down_view[c - 3],
                    down_hl[:, 0, at], down_hl[:, 1, at])

        @block.sync
        def _(sp):
            for dst, src in ((ident[:], ident_in), (router_sb[:], w_router), (bias_sb[:], bias),
                             (lower_sb[:], lower), (spread_sb[:], spread)):
                sp.dma_start(dst, src).then_inc(loaded, 16)
            for s, v in ((w_free[0], 1), (w_free[1], 1), (h_made, 2), (y_free, 2), (routed, 1),
                         (ln.stat, 1), (ln.applied, 1), (ln.rooted, 1), (y_out, 1)):
                sp.sem_inc(s, v)
            for c in range(PIECES):
                if c >= 2:
                    sp.wait_ge(w_lo, c - 1)
                    sp.wait_ge(staged[c % 2], 16 * (c // 2))
                sp.dma_start(piece(c)[0], piece(c)[1]).then_inc(staged[c % 2], 16)

            class Sync(Stages):
                def load_x(self, n):
                    if not isinstance(n, int):
                        sp.wait_ge(h_made, n * TILES1 - TILES1 + 3)
                    sp.dma_start(x_sb[:], x_view[n]).then_inc(x_in_sem, 16)

                def load_res(self, n):
                    sp.wait_ge(ln.stat, n * 8 + 1)
                    sp.dma_start(x_res[:], x_view[n]).then_inc(xres_in, 16)

                def norm(self, n, w):
                    sp.wait_ge(ln.applied, n * NT + (NT + 1))
                    sp.dma_start(out_view[n], ln.out[:]).then_inc(y_out, 16)

            program(sp, Sync())
            sp.wait_ge(y_out, 16 * B + 1)

        @block.gpsimd
        def _(pool):
            pool.memset(raw(combine2[:]), 0.0).then_inc(set_up, 1)
            ln.constants(pool, set_up)

            class Pool(Stages):
                def tile(self, n, j, w):
                    r = j % RING1
                    pool.wait_ge(h_hi, n * TILES1 + (j + 1))
                    pool.tensor_tensor(h_hl[:, r, 1], h_f[:, r], raw(h_hl[:, r, 0]), ALU.subtract).then_inc(h_lo, 1)

                def norm(self, n, w):
                    ln.root(pool, n)

            pool.wait_ge(set_up, SETS)
            program(pool, Pool())

        @block.vector
        def _(dve):
            dve.wait_ge(set_up, 4)
            dve.tensor_tensor(router_hl[:, 1], router_sb[:], raw(router_hl[:, 0]), ALU.subtract).then_inc(set_up, 1)
            for c in range(PIECES):
                dve.wait_ge(w_hi, c + 1)
                src, _, hi, lo = piece(c)
                if c < 3:
                    dve.tensor_tensor(lo, src, raw(hi), ALU.subtract).then_inc(w_lo, 1)
                else:
                    dve.scalar_tensor_tensor(lo, src, 0.5, raw(hi), ALU.mult, ALU.subtract).then_inc(w_lo, 1)

            class Vector(Stages):
                def transpose_x(self, n, w):
                    for k in range(KD):
                        slot, _, _ = later(w, k)
                        dve.wait_ge(xt_hi, n * KD + (k + 1))
                        dve.tensor_tensor(xt[:, 1, k], ps[:, 6 + slot], raw(xt[:, 0, k]), ALU.subtract)\
                           .then_inc(w_free[slot], 1)

                def route(self, n, part, w):
                    k = (0, 8, 17)[part]

                    def step():
                        nonlocal k
                        k += 1
                        return n * ROUTE + k

                    def ranks(out2, values, size, result):
                        shape = [P, NT, size, size]
                        own = values.unsqueeze(3).broadcast_to(shape)
                        other = values.unsqueeze(2).broadcast_to(shape)
                        tri = lower_sb[:, 0:size, 0:size].unsqueeze(1).broadcast_to(shape)
                        dve.wait_ge(routed, step())
                        dve.tensor_tensor(out2[:, 0], other, own, ALU.is_equal).then_inc(routed, 1)
                        dve.wait_ge(routed, step())
                        dve.tensor_tensor(out2[:, 0], out2[:, 0], tri, ALU.mult).then_inc(routed, 1)
                        dve.wait_ge(routed, step())
                        dve.tensor_tensor(out2[:, 1], other, own, ALU.is_gt).then_inc(routed, 1)
                        dve.wait_ge(routed, step())
                        dve.tensor_tensor(out2[:, 1], out2[:, 1], out2[:, 0], ALU.add).then_inc(routed, 1)
                        dve.wait_ge(routed, step())
                        dve.tensor_reduce(result, out2[:, 1], AX.X, ALU.add).then_inc(routed, 1)

                    by_group = "p t (g e) -> p t g e"
                    if part == 0:
                        slot, before, _ = w
                        dve.wait_ge(w_free[slot], before + 2)
                        dve.wait_ge(routed, step())
                        dve.tensor_scalar(denom[:], e_neg[:], 1.0, None, ALU.add).then_inc(routed, 1)
                        dve.wait_ge(routed, step())
                        dve.reciprocal(score[:], denom[:]).then_inc(routed, 1)
                        dve.wait_ge(routed, step())
                        dve.tensor_tensor(biased[:], score[:], bias_sb[:].unsqueeze(1).broadcast_to([P, NT, E]),
                                          ALU.add).then_inc(routed, 1)
                        pairs = biased[:].rearrange("p t (g a b) -> p t g a b", g=GROUPS, a=2)
                        dve.wait_ge(routed, step())
                        dve.tensor_tensor(pair_max[:], pairs[:, :, :, :, 0], pairs[:, :, :, :, 1], ALU.max).then_inc(routed, 1)
                        dve.wait_ge(routed, step())
                        dve.tensor_tensor(pair_min[:], pairs[:, :, :, :, 0], pairs[:, :, :, :, 1], ALU.min).then_inc(routed, 1)
                        dve.wait_ge(routed, step())
                        dve.tensor_tensor(top[:, 0], pair_max[:, :, :, 0], pair_max[:, :, :, 1], ALU.max).then_inc(routed, 1)
                        dve.wait_ge(routed, step())
                        dve.tensor_tensor(top[:, 1], pair_max[:, :, :, 0], pair_max[:, :, :, 1], ALU.min).then_inc(routed, 1)
                        dve.wait_ge(routed, step())
                        dve.tensor_tensor(top[:, 2], pair_min[:, :, :, 0], pair_min[:, :, :, 1], ALU.max).then_inc(routed, 1)
                    elif part == 1:
                        dve.wait_ge(routed, step())
                        dve.tensor_tensor(top[:, 3], top[:, 1], top[:, 2], ALU.max).then_inc(routed, 1)
                        dve.wait_ge(routed, step())
                        dve.tensor_tensor(group[:], top[:, 0], top[:, 3], ALU.add).then_inc(routed, 1)
                        ranks(beats_g, group[:], GROUPS, rank_g[:])
                        dve.wait_ge(routed, step())
                        dve.tensor_scalar(keep_g[:, 0], rank_g[:], TOP_GROUPS - 0.5, None, ALU.is_lt).then_inc(routed, 1)
                        dve.wait_ge(routed, step())
                        dve.tensor_scalar(keep_g[:, 1], keep_g[:, 0], 1.0, BIG, ALU.subtract, ALU.mult).then_inc(routed, 1)
                    else:
                        def wide(i):
                            return keep_g[:, i].unsqueeze(3).broadcast_to([P, NT, GROUPS, EPG])
                        dve.wait_ge(routed, step())
                        dve.tensor_tensor(masked[:, 0].rearrange(by_group, g=GROUPS),
                                          biased[:].rearrange(by_group, g=GROUPS), wide(0), ALU.mult).then_inc(routed, 1)
                        dve.wait_ge(routed, step())
                        dve.tensor_tensor(masked[:, 1].rearrange(by_group, g=GROUPS),
                                          masked[:, 0].rearrange(by_group, g=GROUPS), wide(1), ALU.add).then_inc(routed, 1)
                        ranks(beats, masked[:, 1], E, rank[:])
                        dve.wait_ge(routed, step())
                        dve.scalar_tensor_tensor(chosen[:], rank[:], TOP_K - 0.5, score[:], ALU.is_lt, ALU.mult)\
                           .then_inc(routed, 1)
                        dve.wait_ge(routed, step())
                        dve.tensor_reduce(total[:, 0], chosen[:], AX.X, ALU.add).then_inc(routed, 1)
                        dve.wait_ge(routed, step())
                        dve.tensor_scalar(total[:, 1], total[:, 0], 1e-20, None, ALU.add).then_inc(routed, 1)

                def combine(self, n, w):
                    dve.wait_ge(routed, n * ROUTE + (ROUTE + 1))
                    dve.reciprocal(inverse[:], total[:, 1]).then_inc(gated_done, 1)
                    dve.wait_ge(gated_done, n * (TILES1 + 3) + (T_SHARED + 1))
                    dve.tensor_tensor(combine[:], chosen[:], inverse[:].unsqueeze(2).broadcast_to([P, NT, E]),
                                      ALU.mult).then_inc(gated_done, 1)
                    dve.wait_ge(gated_done, n * (TILES1 + 3) + (T_SHARED + 2))
                    dve.tensor_copy(combine2[:, :, 0:E], combine[:]).then_inc(gated_done, 1)
                    dve.wait_ge(gated_done, n * (TILES1 + 3) + (T_SHARED + 3))
                    dve.tensor_tensor(combine2[:, :, E:2 * E], combine[:], raw(combine2[:, :, 0:E]), ALU.subtract)\
                       .then_inc(combined, 1)

                def tile(self, n, j, w):
                    b, r = j % 2, j % RING1
                    steps = n * (TILES1 + 3) + (j + (3 if w else 0))
                    dve.wait_ge(tanh_done, n * TILES1 + (j + 1))
                    dve.scalar_tensor_tensor(gated[:, b], tanh[:, b], 1.0, ps[:, b], ALU.add, ALU.mult)\
                       .then_inc(gated_done, 1)
                    dve.wait_ge(gated_done, steps + 1)
                    src = gated
                    if w:
                        slot, before, count = w
                        dve.wait_ge(w_full, count + 1)
                        dve.tensor_tensor(scaled[:, b], gated[:, b], ps[:, 6 + slot], ALU.mult).then_inc(w_free[slot], 1)
                        dve.wait_ge(w_free[slot], before + 2)
                        src = scaled
                    dve.wait_ge(u_full, n * TILES1 + (j + 1))
                    dve.tensor_tensor(h_f[:, r], src[:, b], ps[:, 2 + b], ALU.mult).then_inc(h_made, 1)

                def norm(self, n, w):
                    ln.run(dve, n, [later(w, k) for k in range(2)], lambda w: dve.wait_ge(w_full, w[2] + 1),
                           w_free, ps, 6, x_res, xres_in, y_out)

            dve.wait_ge(set_up, SETS)
            program(dve, Vector())

        @block.scalar
        def _(act):
            act.wait_ge(loaded, 16 * 5)
            act.activation(spread_r[:], spread_sb[:], ACT.Copy).then_inc(set_up, 1)
            act.activation(router_hl[:, 0], router_sb[:], ACT.Copy).then_inc(set_up, 1)
            for c in range(PIECES):
                act.wait_ge(staged[c % 2], 16 * (c // 2 + 1))
                src, _, hi, _ = piece(c)
                act.activation(hi, src, ACT.Copy, scale=1.0 if c < 3 else 0.5).then_inc(w_hi, 1)

            class Scalar(Stages):
                def transpose_x(self, n, w):
                    for k in range(KD):
                        slot, _, count = later(w, k)
                        act.wait_ge(w_full, count + 1)
                        act.activation(xt[:, 0, k], ps[:, 6 + slot], ACT.Copy).then_inc(xt_hi, 1)

                def logits(self, n, w):
                    slot, _, count = w
                    act.wait_ge(w_full, count + 1)
                    act.activation(e_neg[:], ps[:, 6 + slot, 0:NT * E].rearrange("p (t e) -> p t e", e=E),
                                   ACT.Exp, scale=-1.0).then_inc(w_free[slot], 1)

                def combine(self, n, w):
                    slot, _, count = w
                    act.wait_ge(w_full, count + 1)
                    act.activation(combine_t[:], ps[:, 6 + slot], ACT.Copy).then_inc(w_free[slot], 1)

                def tile(self, n, j, w):
                    b, r = j % 2, j % RING1
                    act.wait_ge(g_full, n * TILES1 + (j + 1))
                    act.activation(tanh[:, b], ps[:, b], ACT.Tanh, scale=0.5).then_inc(tanh_done, 1)
                    act.wait_ge(h_made, n * TILES1 + (j + 3))
                    act.activation(h_hl[:, r, 0], h_f[:, r], ACT.Copy).then_inc(h_hi, 1)

                def output(self, n):
                    act.wait_ge(y_full, n + 1)
                    for k in range(KD):
                        act.activation(y_sb[:, k], ps[:, 4 + k], ACT.Copy).then_inc(y_free, 1)

            act.wait_ge(set_up, SETS)
            program(act, Scalar())

        @block.tensor
        def _(pe):
            pe.wait_ge(set_up, SETS)
            pe.wait_ge(w_lo, PIECES)

            def take(w):
                pe.wait_ge(w_free[w[0]], w[1] + 1)
                return ps[:, 6 + w[0]]

            def emptied(w):
                pe.wait_ge(w_free[w[0]], w[1] + 2)

            class Tensor(Stages):
                def transpose_x(self, n, w):
                    pe.wait_ge(x_in_sem, n * 16 + 16)
                    for k in range(KD):
                        bank = take(later(w, k))
                        for t in range(NT):
                            ins = pe.transpose(bank[:, t * P:(t + 1) * P], x_sb[:, t, k * P:(k + 1) * P], ident[:])
                        ins.then_inc(w_full, 1)
                    self.w_x = w

                def logits(self, n, w):
                    for k in range(KD):
                        emptied(later(self.w_x, k))
                    bank = take(w)
                    for t in range(NT):
                        ins = matmul3(pe, bank[:, t * E:(t + 1) * E], xt, router_hl, slice(t * P, (t + 1) * P),
                                      slice(0, E), KD)
                    ins.then_inc(w_full, 1)

                def combine(self, n, w):
                    bank = take(w)
                    pe.wait_ge(combined, n + 1)
                    for t in range(NT):
                        ins = pe.transpose(bank[:, t * P:(t + 1) * P], raw(combine2[:, t]), ident[:])
                    ins.then_inc(w_full, 1)
                    self.w_c = w

                def tile(self, n, j, w):
                    pe.wait_ge(h_made, n * TILES1 + (j + 1))
                    matmul3(pe, ps[:, j % 2], gu_hl, xt, slice(j * P, (j + 1) * P), slice(0, S), KD).then_inc(g_full, 1)
                    if w:
                        bank = take(w)
                        if j == T_SHARED:
                            emptied(self.w_c)
                        pe.matmul(bank, spread_r[:, j - T_SHARED], combine_t[:], start=True, stop=True)\
                          .then_inc(w_full, 1)
                    matmul3(pe, ps[:, 2 + j % 2], gu_hl, xt, slice(HID1 + j * P, HID1 + (j + 1) * P), slice(0, S), KD)\
                        .then_inc(u_full, 1)

                def down(self, n, j):
                    r = j % RING1
                    pe.wait_ge(h_lo, n * TILES1 + (j + 1))
                    if j == 0:
                        pe.wait_ge(y_free, n * 2 + 2)
                    for k in range(KD):
                        for i, (a, b) in enumerate(TERMS):
                            ins = pe.matmul(ps[:, 4 + k], down_hl[:, a, j, k * P:(k + 1) * P], h_hl[:, r, b],
                                            start=(j == 0 and i == 0), stop=(j == TILES1 - 1 and i == 2))
                    if j == TILES1 - 1:
                        ins.then_inc(y_full, 1)

                def norm(self, n, w):
                    pe.wait_ge(y_free, n * 2 + 4)
                    ln.transposes(pe, take, [later(w, k) for k in range(2)], y_sb, ident, [w_full, w_full])

            program(pe, Tensor())


def transformer(nc, x, a0_weights, a0_bias_qk, a0_bias_v, a0_bias_o, causal, f0_w1, f0_w2, f0_b1, f0_b2, f0_gate,
                a1_weights, a1_rope, a1_select, band, f1_gate_up, f1_down, f1_router, f1_bias, f1_lower, f1_spread,
                ident, out):
    x1 = nc.dram_tensor("x1", (B * S, D), F32, kind="Internal").ap()
    x2 = nc.dram_tensor("x2", (B * S, D), F32, kind="Internal").ap()
    x3 = nc.dram_tensor("x3", (B * S, D), F32, kind="Internal").ap()
    qk_scratch = nc.dram_tensor("qk_scratch", (2, HALF, 2, HD, S), F32, kind="Internal").ap()
    rows = "b s d -> (b s) d"
    attention0(nc, x.rearrange(rows), a0_weights, a0_bias_qk, a0_bias_v, a0_bias_o, ident, causal, qk_scratch, x1)
    feed_forward0(nc, x1, f0_w1, f0_w2, f0_b1, f0_b2, f0_gate, ident, x2)
    attention1(nc, x2, a1_weights, a1_rope, a1_select, ident, band, x3)
    feed_forward1(nc, x3, f1_gate_up, f1_down, f1_router, f1_bias, f1_lower, f1_spread, ident, out.rearrange(rows))


def lay_out(d):
    import numpy as np

    def swapped(w):
        return w.reshape(D, -1, 2)[:, :, ::-1].reshape(w.shape)

    def column(v, n):
        return v.reshape(n, P).T

    lane, token = np.arange(P), np.arange(S)
    heads = [d["L0_attn_W_" + c].transpose(1, 0, 2).reshape(D, D) for c in "qkv"]
    a0_weights = np.concatenate(heads + [d["L0_attn_W_o"].T], axis=1)
    a0_bias_qk = np.stack([column(d["L0_attn_b_q"], KD), column(d["L0_attn_b_k"], KD)], axis=1)
    a0_bias_v = np.broadcast_to(d["L0_attn_b_v"].reshape(1, D), (P, D))
    a0_bias_o = column(d["L0_attn_b_o"], KD)
    query_key = np.where(lane[None, :] <= lane[:, None], 0, MASKED)
    causal = np.stack([query_key, query_key.T], axis=1).astype(np.float32)

    f0_w1 = np.concatenate([d["L0_ffn_sw1"], *d["L0_ffn_w1"]], axis=1)
    f0_w2 = np.concatenate([d["L0_ffn_sw2"], *d["L0_ffn_w2"]], axis=0)
    f0_b1 = column(np.concatenate([d["L0_ffn_sb1"], *d["L0_ffn_b1"]]), TILES0)
    f0_b2 = np.stack([d["L0_ffn_sb2"], *d["L0_ffn_b2"]]).reshape(3, KD, P).transpose(2, 0, 1)
    f0_gate = d["L0_ffn_gate_w"].T.reshape(KD, P, 2).transpose(1, 0, 2)

    wq, wk, wv, wo = [d["L1_attn_W" + c] for c in "qkvo"]
    a1_weights = np.concatenate([wq, swapped(wq), wk, wk, swapped(wk), swapped(wk), wv, wo], axis=1)
    frequency = np.float32(1.0) / np.float32(10000.0) ** (np.arange(0, HD, 2, dtype=np.float32) / np.float32(HD))
    angle = (token.astype(np.float32)[None, :] * frequency[:, None])[lane % HD // 2].astype(np.float64)
    sign = np.where(lane % 2 == 0, -1.0, 1.0)[:, None]
    a1_rope = np.stack([np.cos(angle), np.sin(angle) * sign], axis=1).astype(np.float32)
    a1_select = np.zeros((P, 24, P), np.float32)
    e = np.arange(HD)
    for half in range(2):
        for r in range(4):
            for part, at in ((0, 0), (1, 1), (0, 2)):
                a1_select[HD * (4 * half + r) + e, 2 * r + part, 64 * half + HD * at + e] = 1
    for c in range(KV):
        for part, at in ((0, 0), (0, 1), (1, 2)):
            a1_select[HD * c + e, 8 + 2 * c + part, 64 * (c % 2) + HD * at + e] = 1
    for h in range(G_HEADS):
        a1_select[[h, G_HEADS + h], 16 + h] = 1
    near = np.abs(lane[:, None] - (np.arange(WINDOW)[None, :] - REACH)) <= REACH
    band = np.repeat(np.where(near, 0, MASKED).astype(np.float32)[:, None], 2, axis=1)

    gate, up = [d[f"L1_ffn_{c}_w"].transpose(1, 0, 2).reshape(D, E * HID_EXPERT) for c in ("gate", "up")]
    f1_gate_up = np.concatenate([d["L1_ffn_shared_gate_w"].T, gate, d["L1_ffn_shared_up_w"].T, up], axis=1)
    f1_down = np.concatenate([d["L1_ffn_shared_down_w"].T, d["L1_ffn_down_w"].reshape(E * HID_EXPERT, D)], axis=0)
    f1_router = d["L1_ffn_router_w"].T.reshape(KD, P, E).transpose(1, 0, 2)
    f1_bias = np.broadcast_to(d["L1_ffn_correction_bias"], (P, E))
    f1_lower = np.broadcast_to(np.tril(np.ones((E, E), np.float32), -1), (P, E, E))
    f1_spread = np.zeros((P, E // 2, P), np.float32)
    for x in range(E):
        f1_spread[[x, E + x], x // 2, HID_EXPERT * (x % 2):HID_EXPERT * (x % 2 + 1)] = 1
    ident = np.eye(P, dtype=np.float32)
    return dict(x=d["L0_attn_inputs"], a0_weights=a0_weights, a0_bias_qk=a0_bias_qk, a0_bias_v=a0_bias_v,
                a0_bias_o=a0_bias_o, causal=causal, f0_w1=f0_w1, f0_w2=f0_w2, f0_b1=f0_b1, f0_b2=f0_b2,
                f0_gate=f0_gate, a1_weights=a1_weights, a1_rope=a1_rope, a1_select=a1_select, band=band,
                f1_gate_up=f1_gate_up, f1_down=f1_down, f1_router=f1_router, f1_bias=f1_bias, f1_lower=f1_lower,
                f1_spread=f1_spread, ident=ident)


def kernel(**inputs):
    import numpy as _np
    import concourse.bacc as _bacc
    from concourse import mybir as _mybir
    from concourse.bass_utils import run_bass_kernel_spmd as _run

    nc = _bacc.Bacc("TRN2", target_bir_lowering=False, num_devices=1)
    arrays, args = {}, []
    for name, value in lay_out({k: _np.asarray(v) for k, v in inputs.items()}).items():
        a = _np.ascontiguousarray(value)
        arrays[f"in_{name}_dram"] = a
        args.append(nc.dram_tensor(f"in_{name}_dram", a.shape, _mybir.dt.from_np(a.dtype), kind="ExternalInput").ap())
    args.append(nc.dram_tensor("out_0_dram", (B, S, D), _mybir.dt.from_np(_np.dtype("float32")),
                               kind="ExternalOutput").ap())
    transformer(nc, *args)
    r = _run(nc, [arrays], core_ids=[0])
    return r.results[0]["out_0_dram"]
```

```python
from contextlib import ExitStack

import concourse.bass as bass
from concourse import mybir

F32 = mybir.dt.float32
F32R = mybir.dt.float32r
BF16 = mybir.dt.bfloat16
ALU = mybir.AluOpType
ACT = mybir.ActivationFunctionType
AX = mybir.AxisListType

P = 128
B = 8
S = 512
D = 256
KD = D // P
NT = S // P
H = 16
HD = D // H
LN_EPS = 1e-5
MASKED = -1.0e37
TERMS = ((0, 0), (0, 1), (1, 0))


class Phase:

    def __init__(self, nc, ctx, name):
        self.nc, self.ctx, self.name = nc, ctx, name

    def sb(self, name, shape, dt=F32):
        return self.ctx.enter_context(self.nc.sbuf_tensor(f"{self.name}_{name}", shape, dt))

    def psum(self, name, shape, dt=F32):
        return self.ctx.enter_context(self.nc.psum_tensor(f"{self.name}_{name}", shape, dt))

    def sem(self, name):
        return self.ctx.enter_context(self.nc.semaphore(f"{self.name}_{name}"))


def raw(ap):
    return ap.bitcast(F32)


def matmul3(pe, out, w, x, wcols, xcols, blocks, last=True):
    n = 0
    for i, j in TERMS:
        for k in range(blocks):
            ins = pe.matmul(out, w[:, i, k, wcols], x[:, j, k, xcols],
                            start=(n == 0), stop=(n == 3 * blocks - 1))
            n += 1
    return ins


def settle(eng, sem, value, passed):
    eng.wait_ge(sem, value)
    eng.sem_inc(passed, 1)


class LayerNorm:

    def __init__(self, ph):
        self.z = ph.sb("ln_z", [P, NT, D])
        self.stats = ph.sb("ln_stats", [P, NT, 6])
        self.mv = ph.sb("ln_mv", [P, NT, 2])
        self.rstd = ph.sb("ln_rstd", [P, NT])
        self.var = ph.sb("ln_var", [P, NT])
        self.power = ph.sb("ln_power", [P, NT])
        self.out = ph.sb("ln_out", [P, NT, D])
        self.stat = ph.sem("ln_stat")
        self.vared = ph.sem("ln_vared")
        self.rooted = ph.sem("ln_rooted")
        self.passed = ph.sem("ln_passed")
        self.applied = ph.sem("ln_applied")

    def constants(self, pool, done):
        pool.memset(self.power[:], -0.5).then_inc(done, 1)

    def transposes(self, pe, take, uses, y, ident, full):
        for pair in range(NT // 2):
            bank = take(uses[pair])
            for t in range(2):
                for k in range(KD):
                    at = t * D + k * P
                    ins = pe.transpose(bank[:, at:at + P], y[:, k, (2 * pair + t) * P:(2 * pair + t + 1) * P], ident[:])
            ins.then_inc(full[uses[pair][0]], 1)

    def root(self, pool, n):
        pool.wait_ge(self.applied, n * NT + 1)
        settle(pool, self.stat, n * (2 * NT) + (2 * NT + 1), self.passed)
        pool.tensor_scalar(self.var[:], self.mv[:, :, 1], LN_EPS, None, ALU.add).then_inc(self.vared, 1)
        pool.wait_ge(self.vared, n + 1)
        pool.tensor_tensor(self.rstd[:], self.var[:], self.power[:], ALU.pow).then_inc(self.rooted, 1)

    def apply(self, eng, n, stored):
        settle(eng, self.rooted, n + 2, self.passed)
        settle(eng, stored, n * 16 + 1, self.passed)
        for t in range(NT):
            eng.tensor_scalar(self.out[:, t], self.z[:, t], self.mv[:, t, 0:1], self.rstd[:, t:t + 1],
                              ALU.subtract, ALU.mult).then_inc(self.applied, 1)

    def run(self, dve, n, uses, wait_full, w_free, ps, bank0, x_res, xres_in):
        dve.wait_ge(xres_in, n * 16 + 16)
        dve.wait_ge(self.applied, n * NT + 1)
        for pair, use in enumerate(uses):
            slot = use[0]
            wait_full(use)
            dve.tensor_tensor(self.z[:, 2 * pair:2 * pair + 2],
                              ps[:, bank0 + slot].rearrange("p (t d) -> p t d", t=2),
                              x_res[:, 2 * pair:2 * pair + 2], ALU.add).then_inc(w_free[slot], 1)
        for pair, use in enumerate(uses):
            dve.wait_ge(w_free[use[0]], use[1] + 2)
            for t in range(2 * pair, 2 * pair + 2):
                dve.bn_stats(self.stats[:, t], self.z[:, t]).then_inc(self.stat, 1)
        for t in range(NT):
            settle(dve, self.stat, n * (2 * NT) + (t + 2), self.passed)
            dve.bn_aggr(self.mv[:, t], self.stats[:, t]).then_inc(self.stat, 1)


HALF = 8
PAIRS = HALF // 2
ROWS = 64
S_BLOCKS = ((0, 1), (2,), (3,))
T_BLOCKS = ((0,), (1,), (2, 3))
PARTS = len(S_BLOCKS)
TILES = HALF * PARTS
STEPS = TILES // 4
W_PRE = 16
W_LOOP = 20
M_LAG = 6


def attention0(nc, x_in, wqkv, bqk, bv_row, bo, ident_in, causal_in, qk_scratch, x_out):
    x_view = x_in.rearrange("(n t p) d -> n p t d", t=NT, p=P)
    out_view = x_out.rearrange("(n t p) d -> n p t d", t=NT, p=P)
    qk_write = qk_scratch.rearrange("o h i e s -> o i h e s")
    ctx = ExitStack()
    with ctx:
        ph = Phase(nc, ctx, "a0")
        sb, sem = ph.sb, ph.sem
        w_raw = sb("w_raw", [P, KD, 4 * D])
        w_hl = sb("w_hl", [P, 2, KD, 4 * D], F32R)
        bqk_sb = sb("bqk", [P, 2, 2])
        bo_sb = sb("bo", [P, KD])
        bv_sb = sb("bv", [P, D])
        ident = sb("ident", [P, P])
        ident_b = sb("ident_b", [P, P], BF16)
        causal = sb("causal", [P, 2, P])
        causal_b = sb("causal_b", [P, 2, P], BF16)
        zeros = sb("zeros", [32, P])
        ones = sb("ones", [2, S])
        x_sb = sb("x", [P, NT, D])
        x_res = sb("x_res", [P, NT, D])
        xt = sb("xt", [P, 2, KD, S], F32R)
        qk = sb("qk", [P, 2, 2, S], F32R)
        q_st = [sb(f"q_st{i}", [P, PAIRS, S], F32R) for i in range(2)]
        k_st = [sb(f"k_st{i}", [P, HALF, S], F32R) for i in range(2)]
        v_aug = [sb(f"v_aug{i}", [P, NT, HALF, 32]) for i in range(2)]
        nmax = sb("nmax", [P, 32])
        nmax2 = sb("nmax2", [P, 2, 2, 16], F32R)
        mrow = sb("mrow", [64, P], F32R)
        probs = sb("probs", [P, 8, S])
        pv_sb = [sb(f"pv_sb{i}", [P, S]) for i in range(2)]
        rden = sb("rden", [P, 2, NT, 4])
        o_tok = sb("o_tok", [P, NT, D])
        o_hl = sb("o_hl", [P, 2, KD, S], F32R)
        y_sb = sb("y", [P, KD, S])
        ln = LayerNorm(ph)

        ps = ph.psum("ps", [P, 8, S])

        loaded = sem("loaded")
        set_up = sem("set_up")
        w_split = sem("w_split")
        x_in_sem = sem("x_in")
        xres_in = sem("xres_in")
        w_full = sem("w_full")
        w_free = [sem("w_free0"), sem("w_free1")]
        hi_done = sem("hi_done")
        qk_out = sem("qk_out")
        stack_in = [sem("stack_in0"), sem("stack_in1")]
        s_full = sem("s_full")
        s_free = sem("s_free")
        t_full = sem("t_full")
        t_free = sem("t_free")
        pv_step = sem("pv_step")
        pv_free = sem("pv_free")
        nm_hi = sem("nm_hi")
        nm_ready = sem("nm_ready")
        mrow_in = [sem("mrow_in0"), sem("mrow_in1")]
        rden_ok = sem("rden_ok")
        o_split = sem("o_split")
        oproj_done = sem("oproj_done")
        y_out = sem("y_out")
        ones_in = sem("ones_in")

        def work(c, n):
            return c % 2, c // 2 + n * (W_LOOP // 2), c + n * W_LOOP

        def width(block):
            return S - block * P

        def slot_order(e, m, first, end):
            order = []
            lag = M_LAG if e and m else 0
            end = min(end, TILES + lag)
            for k in range(first, end):
                if e and k < TILES:
                    order.append(("t", k))
                    if k == 17:
                        order.append(("copy", 0))
                    if k % 4 == 3 and k > 4:
                        order.append(("pv", k // 4 - 1))
                if e and k == TILES - 1 + min(lag, 4):
                    order.append(("pv", STEPS - 1))
                    order.append(("copy", 1))
                if m and k >= lag:
                    order.append(("s", k - lag))
            return order

        LAST = B - 1
        END = TILES + M_LAG
        LOOP = {k: W_PRE + v for k, v in dict(p1=0, b_n0=2, b_n1=3, b_t=4, v=5, xt=7, ot=9, a_n0=11, p0=12,
                                              a_n1=14, a_t=15, o=16, yt=18).items()}
        TAIL = {k: W_PRE + v for k, v in dict(p1=0, b_n0=2, b_n1=3, b_t=4, v=5, ot=7, a_n0=9, a_n1=10, a_t=11,
                                              o=12, yt=14).items()}
        FINAL = {k: W_PRE + v for k, v in dict(n0=16, n1=17, ot=18, o=20, yt=22).items()}

        def turn(st, n, uses, more):
            def use(name):
                return work(uses[name], n)

            st.load_res(n)
            e, m = (n, 1), (n + 1, 0)
            st.slot(e, m, 0, 6)
            st.project((n + 1, 1), use("p1"))
            if more:
                st.load_x(n + 2)
            st.slot(e, m, 6, 19)
            st.normalise(e, 0, use("b_n0"))
            st.slot(e, m, 19, END)
            st.normalise(e, 1, use("b_n1"))
            st.maxima(m, use("b_t"))
            st.stack((n + 1, 1))
            st.values(n + 1, use("v"))
            if more:
                st.transpose_x(n + 2, use("xt"))
            e, m = (n + 1, 0), (n + 1, 1)
            st.slot(e, m, 0, 3)
            st.transpose_out(n, use("ot"))
            st.slot(e, m, 3, 19)
            st.normalise(e, 0, use("a_n0"))
            st.slot(e, m, 19, 22)
            if more:
                st.project((n + 2, 0), use("p0"))
            st.slot(e, m, 22, END)
            st.normalise(e, 1, use("a_n1"))
            st.maxima(m, use("a_t"))
            if more:
                st.stack((n + 2, 0))
            st.project_out(n, use("o"))
            st.norm(n, use("yt"))
            st.store(n)

        def program(eng, st):
            st.load_x(0)
            st.transpose_x(0, work(0, 0))
            st.project((0, 0), work(2, 0))
            st.stack((0, 0))
            st.values(0, work(4, 0))
            st.slot(None, (0, 0), 0, END)
            st.maxima((0, 0), work(6, 0))
            st.project((0, 1), work(7, 0))
            st.load_x(1)
            st.stack((0, 1))
            st.transpose_x(1, work(9, 0))
            st.slot((0, 0), (0, 1), 0, 19)
            st.normalise((0, 0), 0, work(11, 0))
            st.slot((0, 0), (0, 1), 19, 22)
            st.project((1, 0), work(12, 0))
            st.slot((0, 0), (0, 1), 22, END)
            st.normalise((0, 0), 1, work(14, 0))
            st.maxima((0, 1), work(15, 0))
            st.stack((1, 0))
            with eng.Fori(0, LAST - 1) as n:
                turn(st, n, LOOP, True)
            turn(st, LAST - 1, TAIL, False)
            st.load_res(LAST)
            n = LAST - 1
            st.slot((LAST, 1), None, 0, 19)
            st.normalise((LAST, 1), 0, work(FINAL["n0"], n))
            st.slot((LAST, 1), None, 19, END)
            st.normalise((LAST, 1), 1, work(FINAL["n1"], n))
            st.transpose_out(LAST, work(FINAL["ot"], n))
            st.project_out(LAST, work(FINAL["o"], n))
            st.norm(LAST, work(FINAL["yt"], n))
            st.store(LAST)

        def later(w, k):
            slot, before, count = w
            return (slot + k) % 2, before + (slot + k) // 2, count + k

        def unit(u, per, k):
            return u[0] * (2 * per) + (u[1] * per + k)

        class Stages:
            def load_x(self, n): pass
            def load_res(self, n): pass
            def transpose_x(self, n, w): pass
            def project(self, u, w): pass
            def stack(self, u): pass
            def values(self, n, w): pass
            def slot(self, e, m, first, end): pass
            def maxima(self, u, w): pass
            def normalise(self, u, g, w): pass
            def transpose_out(self, n, w): pass
            def project_out(self, n, w): pass
            def norm(self, n, w): pass
            def store(self, n): pass

        SETS = 11
        block = ctx.enter_context(nc.Block())

        @block.sync
        def _(sp):
            for dst, src in ((w_raw[:], wqkv.rearrange("(k p) n -> p k n", p=P)),
                             (bqk_sb[:], bqk), (bo_sb[:], bo), (bv_sb[:], bv_row),
                             (ident[:], ident_in), (causal[:], causal_in)):
                sp.dma_start(dst, src).then_inc(loaded, 16)
            sp.sem_inc(w_free[0], 1)
            sp.sem_inc(w_free[1], 1)
            sp.sem_inc(s_free, 3)
            sp.sem_inc(t_free, 2)
            sp.sem_inc(pv_step, 2)
            sp.sem_inc(pv_free, 1)

            class Sync(Stages):
                def load_x(self, n):
                    sp.dma_start(x_sb[:], x_view[n]).then_inc(x_in_sem, 16)

                def load_res(self, n):
                    sp.wait_ge(ln.stat, n * 8 + 1)
                    sp.dma_start(x_res[:], x_view[n]).then_inc(xres_in, 16)

                def project(self, u, w):
                    n, q = u
                    if q == 1:
                        settle(sp, stack_in[0], n * 160 + 160, ln.passed)
                    elif not (isinstance(n, int) and n == 0):
                        settle(sp, stack_in[1], n * 160, ln.passed)
                    for o in range(2):
                        slot, before, _ = later(w, o)
                        sp.wait_ge(w_free[slot], before + 2)
                        for i in range(2):
                            sp.dma_start(qk_write[o, i], raw(qk[:, o, i])).then_inc(qk_out, 16)

                def stack(self, u):
                    n, q = u
                    if not (isinstance(n, int) and n == 0):
                        settle(sp, t_full, unit(u, TILES, -TILES), ln.passed)
                    sp.wait_ge(qk_out, unit(u, 64, 64))
                    for p in range(2):
                        r = ROWS * p
                        q_heads = qk_scratch[0].rearrange("(j p) i e s -> p (i e) j s", p=2)[p]
                        k_heads = qk_scratch[1].rearrange("(j p) i e s -> p (i e) j s", p=2)[p]
                        k_dst = raw(k_st[q][:]).rearrange("r (j p) s -> r p j s", p=2)[:, p]
                        q_dst = raw(q_st[q][:])
                        sp.dma_start(q_dst[r:r + 32], q_heads).then_inc(stack_in[q], 16)
                        sp.dma_start(q_dst[r + 32:r + 48], q_heads[0:16]).then_inc(stack_in[q], 16)
                        sp.dma_start(k_dst[r:r + 16], k_heads[0:16]).then_inc(stack_in[q], 16)
                        sp.dma_start(k_dst[r + 16:r + 48], k_heads).then_inc(stack_in[q], 16)
                        sp.dma_start(q_dst[r + 48:r + 50].rearrange("r j (i s) -> r (j i) s", s=P), zeros[:, :])\
                          .then_inc(stack_in[q], 16)

                def maxima(self, u, w):
                    slot, before, _ = w
                    sp.wait_ge(w_free[slot], before + 2)
                    for p in range(2):
                        r = ROWS * p
                        sp.dma_start(raw(q_st[u[1]][r + 48:r + 50]).rearrange("r j (i s) -> r (j i) s", s=P),
                                     raw(mrow[32 * p:32 * p + 32, :])).then_inc(mrow_in[u[1]], 16)

                def store(self, n):
                    sp.wait_ge(ln.applied, n * NT + (NT + 1))
                    sp.dma_start(out_view[n], ln.out[:]).then_inc(y_out, 16)

            sp.sem_inc(ln.stat, 1)
            sp.sem_inc(ln.applied, 1)
            sp.sem_inc(ln.rooted, 1)
            sp.sem_inc(y_out, 1)
            sp.wait_ge(set_up, SETS)
            for q in range(2):
                for h in range(HALF):
                    r = ROWS * (h % 2) + 48
                    sp.dma_start(raw(k_st[q][r:r + 2, h]), ones[:, :]).then_inc(ones_in, 16)
            sp.wait_ge(ones_in, 2 * HALF * 16)
            program(sp, Sync())
            sp.wait_ge(y_out, 16 * B + 1)

        @block.gpsimd
        def _(pool):
            pool.memset(zeros[:], 0.0).then_inc(set_up, 1)
            pool.memset(ones[:], 1.0).then_inc(set_up, 1)
            for i in range(2):
                pool.memset(raw(q_st[i][:]), 0.0).then_inc(set_up, 1)
                pool.memset(raw(k_st[i][:]), 0.0).then_inc(set_up, 1)
                pool.memset(v_aug[i][:], 1.0).then_inc(set_up, 1)
            ln.constants(pool, set_up)
            pool.wait_ge(set_up, SETS)
            pool.wait_ge(loaded, 16 * 6)

            class Pool(Stages):
                def norm(self, n, w):
                    ln.root(pool, n)
                    ln.apply(pool, n, y_out)

            program(pool, Pool())

        @block.vector
        def _(dve):
            dve.wait_ge(loaded, 16 * 6)
            dve.tensor_copy(ident_b[:], ident[:]).then_inc(set_up, 1)
            dve.tensor_copy(causal_b[:], causal[:]).then_inc(set_up, 1)
            dve.wait_ge(w_split, 1)
            dve.tensor_tensor(w_hl[:, 1], w_raw[:], raw(w_hl[:, 0]), ALU.subtract).then_inc(w_split, 1)
            dve.wait_ge(set_up, SETS)

            class Vector(Stages):

                def lo(self, out, psum, hi, bias, count, w):
                    slot, before, _ = w
                    dve.wait_ge(hi_done, count)
                    if bias is None:
                        ins = dve.tensor_tensor(out, psum, raw(hi), ALU.subtract)
                    else:
                        ins = dve.scalar_tensor_tensor(out, psum, bias, raw(hi), ALU.add, ALU.subtract)
                    ins.then_inc(w_free[slot], 1)

                def transpose_x(self, n, w):
                    for k in range(KD):
                        slot, before, _ = later(w, k)
                        self.lo(xt[:, 1, k], ps[:, 6 + slot], xt[:, 0, k], None, n * 6 + (k + 1), later(w, k))

                def project(self, u, w):
                    n, q = u
                    for o in range(2):
                        slot, _, _ = later(w, o)
                        self.lo(qk[:, o, 1], ps[:, 6 + slot], qk[:, o, 0], bqk_sb[:, o, q:q + 1],
                                n * 6 + (2 + 2 * q + o + 1), later(w, o))

                def values(self, n, w):
                    for pair in range(NT // 2):
                        slot, _, count = later(w, pair)
                        dve.wait_ge(w_full, count + 1)
                        tile = ps[:, 6 + slot].rearrange("p (t q h e) -> p q t h e", t=2, q=2, e=HD)
                        for q in range(2):
                            bias = bv_sb[:, q * P:(q + 1) * P].rearrange("p (h e) -> p h e", e=HD)
                            ins = dve.tensor_tensor(v_aug[q][:, 2 * pair:2 * pair + 2, :, 0:HD], tile[:, q],
                                                    bias.unsqueeze(1).broadcast_to([P, 2, HALF, HD]), ALU.add)
                        ins.then_inc(w_free[slot], 1)

                def slot(self, e, m, first, end):
                    for kind, k in slot_order(e, m, first, end):
                        if kind == "s":
                            h, part = k // PARTS, k % PARTS
                            dve.wait_ge(s_full, unit(m, TILES, k + 1))
                            col = 0
                            for i in S_BLOCKS[part]:
                                at = 16 * (h % 2) + 4 * (h // 2) + i
                                ins = dve.tensor_reduce(nmax[:, at:at + 1], ps[:, k % 3, col:col + (i + 1) * P], AX.X,
                                                        ALU.max, negate=True)
                                col += (i + 1) * P
                            ins.then_inc(s_free, 1)

                def maxima(self, u, w):
                    dve.wait_ge(s_free, unit(u, TILES, TILES + 3))
                    src = nmax[:].rearrange("p (a r) -> p a r", a=2)
                    dve.tensor_copy(nmax2[:, :, 0], src).then_inc(nm_hi, 1)
                    dve.wait_ge(nm_hi, unit(u, 1, 1))
                    dve.tensor_tensor(nmax2[:, :, 1], src, raw(nmax2[:, :, 0]), ALU.subtract).then_inc(nm_ready, 1)

                def normalise(self, u, g, w):
                    slot, before, count = w
                    dve.wait_ge(w_full, count + 1)
                    tile = ps[:, 6 + slot].rearrange("p (t r c) -> p t r c", t=NT, r=4)
                    dve.reciprocal(rden[:, g], tile[:, :, :, HD]).then_inc(rden_ok, 1)
                    dve.wait_ge(rden_ok, unit(u, 2, g + 1))
                    at = (u[1] * 2 + g) * 4 * HD
                    dve.tensor_tensor(o_tok[:, :, at:at + 4 * HD].rearrange("p t (r e) -> p t r e", e=HD),
                                      tile[:, :, :, 0:HD],
                                      rden[:, g].unsqueeze(3).broadcast_to([P, NT, 4, HD]),
                                      ALU.mult).then_inc(w_free[slot], 1)

                def transpose_out(self, n, w):
                    for k in range(KD):
                        slot, _, _ = later(w, k)
                        dve.wait_ge(o_split, n * KD + (k + 1))
                        dve.tensor_tensor(o_hl[:, 1, k], ps[:, 6 + slot], raw(o_hl[:, 0, k]), ALU.subtract)\
                           .then_inc(w_free[slot], 1)

                def norm(self, n, w):
                    ln.run(dve, n, [later(w, k) for k in range(2)], lambda w: dve.wait_ge(w_full, w[2] + 1),
                           w_free, ps, 6, x_res, xres_in)

            program(dve, Vector())

        @block.scalar
        def _(act):
            act.wait_ge(loaded, 16 * 6)
            act.activation(w_hl[:, 0], w_raw[:], ACT.Copy).then_inc(w_split, 1)
            act.wait_ge(set_up, SETS)

            class Scalar(Stages):
                def transpose_x(self, n, w):
                    for k in range(KD):
                        slot, _, count = later(w, k)
                        act.wait_ge(w_full, count + 1)
                        act.activation(xt[:, 0, k], ps[:, 6 + slot], ACT.Copy).then_inc(hi_done, 1)

                def project(self, u, w):
                    n, q = u
                    for o in range(2):
                        slot, _, count = later(w, o)
                        act.wait_ge(w_full, count + 1)
                        if o == 0 and not (isinstance(n, int) and n == 0 and q == 0):
                            act.wait_ge(qk_out, unit(u, 64, 0))
                        act.activation(qk[:, o, 0], ps[:, 6 + slot], ACT.Identity, bias=bqk_sb[:, o, q:q + 1])\
                           .then_inc(hi_done, 1)

                def slot(self, e, m, first, end):
                    for kind, k in slot_order(e, m, first, end):
                        if kind == "t":
                            step, r = k // 4, k % 4
                            wd = sum(width(tb) for tb in T_BLOCKS[step % PARTS])
                            act.wait_ge(t_full, unit(e, TILES, k + 1))
                            if r == 0:
                                act.wait_ge(pv_step, unit(e, STEPS, step + 1))
                            act.activation(probs[:, (step % 2) * 4 + r, 0:wd], ps[:, 3 + k % 2, 0:wd], ACT.Exp,
                                           scale=HD ** -0.5).then_inc(t_free, 1)
                        elif kind == "copy":
                            act.wait_ge(pv_step, unit(e, STEPS, PARTS * (k + 1) + 2))
                            act.activation(pv_sb[k][:], ps[:, 5], ACT.Copy).then_inc(pv_free, 1)

                def maxima(self, u, w):
                    slot, _, count = w
                    act.wait_ge(w_full, count + 1)
                    n, q = u
                    if not (isinstance(n, int) and n == 0 and q == 0):
                        act.wait_ge(mrow_in[1 - q], n * 32 + (32 if q else 0))
                    act.activation(mrow[:, :], ps[0:64, 6 + slot, 0:P], ACT.Copy).then_inc(w_free[slot], 1)

                def transpose_out(self, n, w):
                    for k in range(KD):
                        slot, _, count = later(w, k)
                        act.wait_ge(w_full, count + 1)
                        act.activation(o_hl[:, 0, k], ps[:, 6 + slot], ACT.Copy).then_inc(o_split, 1)

                def project_out(self, n, w):
                    for k in range(KD):
                        slot, _, count = later(w, k)
                        act.wait_ge(w_full, count + 1)
                        act.activation(y_sb[:, k], ps[:, 6 + slot], ACT.Identity, bias=bo_sb[:, k:k + 1])\
                           .then_inc(w_free[slot], 1)

            program(act, Scalar())

        @block.tensor
        def _(pe):
            pe.wait_ge(set_up, SETS)
            pe.wait_ge(w_split, 2)

            def take(w):
                slot, before, _ = w
                pe.wait_ge(w_free[slot], before + 1)
                return ps[:, 6 + slot]

            def emptied(w):
                slot, before, _ = w
                pe.wait_ge(w_free[slot], before + 2)

            class Tensor(Stages):
                def transpose_x(self, n, w):
                    pe.wait_ge(x_in_sem, n * 16 + 16)
                    for k in range(KD):
                        bank = take(later(w, k))
                        for t in range(NT):
                            ins = pe.transpose(bank[:, t * P:(t + 1) * P], x_sb[:, t, k * P:(k + 1) * P], ident[:])
                        ins.then_inc(w_full, 1)
                    self.w_x = w

                def project(self, u, w):
                    n, q = u
                    if isinstance(n, int) and (n, q) == (0, 0):
                        for k in range(KD):
                            emptied(later(self.w_x, k))
                    for o in range(2):
                        bank = take(later(w, o))
                        matmul3(pe, bank, w_hl, xt, slice(o * D + q * P, o * D + (q + 1) * P), slice(0, S), KD)\
                            .then_inc(w_full, 1)

                def values(self, n, w):
                    self.w_v = w
                    for pair in range(NT // 2):
                        bank = take(later(w, pair))
                        for t in range(2):
                            at = (2 * pair + t) * P
                            ins = matmul3(pe, bank[:, t * D:(t + 1) * D], xt, w_hl, slice(at, at + P),
                                          slice(2 * D, 3 * D), KD)
                        ins.then_inc(w_full, 1)

                def slot(self, e, m, first, end):
                    for kind, k in slot_order(e, m, first, end):
                        if kind == "t":
                            if k == 0:
                                pe.wait_ge(mrow_in[e[1]], e[0] * 32 + 32)
                            g, part, r = k // (4 * PARTS), k // 4 % PARTS, k % 4
                            h = 4 * g + r
                            pe.wait_ge(t_free, unit(e, TILES, k + 1))
                            col = 0
                            for tb in T_BLOCKS[part]:
                                tile = ps[:, 3 + k % 2, col:col + width(tb)]
                                pe.matmul(tile, k_st[e[1]][:, h, tb * P:(tb + 1) * P], q_st[e[1]][:, h // 2, tb * P:S],
                                          start=True, stop=False)
                                ins = pe.matmul(tile[:, 0:P], ident_b[:], causal_b[:, 1], start=False, stop=True)
                                col += width(tb)
                            ins.then_inc(t_full, 1)
                        elif kind == "s":
                            if k == 0:
                                pe.wait_ge(stack_in[m[1]], m[0] * 160 + 160)
                            h, part = k // PARTS, k % PARTS
                            pe.wait_ge(s_free, unit(m, TILES, k + 1))
                            col = 0
                            for i in S_BLOCKS[part]:
                                tile = ps[:, k % 3, col:col + (i + 1) * P]
                                pe.matmul(tile, q_st[m[1]][:, h // 2, i * P:(i + 1) * P],
                                          k_st[m[1]][:, h, 0:(i + 1) * P], start=True, stop=False)
                                ins = pe.matmul(tile[:, i * P:], ident_b[:], causal_b[:, 0], start=False, stop=True)
                                col += (i + 1) * P
                            ins.then_inc(s_full, 1)
                        elif kind == "pv":
                            g, part = k // PARTS, k % PARTS
                            if k == 0 and e[1] == 0:
                                for pair in range(NT // 2):
                                    emptied(later(self.w_v, pair))
                            if part == 0:
                                pe.wait_ge(pv_free, unit(e, 2, g + 1))
                            pe.wait_ge(t_free, unit(e, TILES, 4 * k + 4 + 2))
                            col = 0
                            for tb in T_BLOCKS[part]:
                                for r in range(4):
                                    ins = pe.matmul(ps[32 * r:32 * r + 32, 5, tb * P:S],
                                                    v_aug[e[1]][:, tb, 4 * g + r, :],
                                                    probs[:, (k % 2) * 4 + r, col:col + width(tb)],
                                                    start=(tb == 0), stop=(tb == NT - 1), skip_group_check=True)
                                col += width(tb)
                            ins.then_inc(pv_step, 1)

                def maxima(self, u, w):
                    bank = take(w)
                    settle(pe, nm_ready, unit(u, 1, 1), ln.passed)
                    pe.transpose(bank[0:64, 0:P], raw(nmax2[:]).rearrange("p a i r -> p (a i r)"), ident[:])\
                      .then_inc(w_full, 1)

                def normalise(self, u, g, w):
                    bank = take(w)
                    pe.wait_ge(pv_free, unit(u, 2, g + 1 + 1))
                    for t in range(NT):
                        ins = pe.transpose(bank[:, t * P:(t + 1) * P], pv_sb[g][:, t * P:(t + 1) * P], ident[:])
                    ins.then_inc(w_full, 1)
                    self.w_n = w

                def transpose_out(self, n, w):
                    if isinstance(n, int) and n == LAST:
                        emptied(self.w_n)
                    for k in range(KD):
                        bank = take(later(w, k))
                        for t in range(NT):
                            ins = pe.transpose(bank[:, t * P:(t + 1) * P], o_tok[:, t, k * P:(k + 1) * P], ident[:])
                        ins.then_inc(w_full, 1)
                    self.w_o = w

                def project_out(self, n, w):
                    for k in range(KD):
                        emptied(later(self.w_o, k))
                    for k in range(KD):
                        bank = take(later(w, k))
                        matmul3(pe, bank, w_hl, o_hl, slice(3 * D + k * P, 3 * D + (k + 1) * P), slice(0, S), KD)\
                            .then_inc(w_full, 1)
                    self.w_y = w

                def norm(self, n, w):
                    for k in range(KD):
                        emptied(later(self.w_y, k))
                    ln.transposes(pe, take, [later(w, k) for k in range(2)], y_sb, ident, [w_full, w_full])

            program(pe, Tensor())


HID0 = 3 * 1024
TILES0 = HID0 // P
THIRD = TILES0 // 3
RING_H = 3


def feed_forward0(nc, x_in, w1, w2, b1, b2, gate, ident_in, x_out):
    x_view = x_in.rearrange("(n t p) d -> n p t d", t=NT, p=P)
    out_view = x_out.rearrange("(n t p) d -> n p t d", t=NT, p=P)
    w1_view = w1.rearrange("(k p) (c n) -> c p k n", p=P, c=3)
    w2_view = w2.rearrange("(c j p) n -> c p j n", p=P, c=3)
    ctx = ExitStack()
    with ctx:
        ph = Phase(nc, ctx, "f0")
        sb, sem = ph.sb, ph.sem
        stage = [sb(f"stage{i}", [P, 2 * 1024]) for i in range(2)]
        w1_hl = sb("w1", [P, 2, KD, HID0], F32R)
        w2_hl = sb("w2", [P, 2, TILES0, D], F32R)
        b1_sb = sb("b1", [P, TILES0])
        b2_sb = sb("b2", [P, 3, KD])
        b2_sum = sb("b2_sum", [P, 2, KD])
        gate_sb = sb("gate", [P, KD, 2])
        gate_d = sb("gate_d", [P, KD])
        gate_hl = sb("gate_hl", [P, 2, KD, P], F32R)
        ident = sb("ident", [P, P])
        x_sb = sb("x", [P, NT, D])
        x_res = sb("x_res", [P, NT, D])
        xt = sb("xt", [P, 2, KD, S], F32R)
        xm = [sb(f"xm{e}", [P, 2, KD, S], F32R) for e in range(2)]
        chosen0 = sb("chosen0", [P, S])
        h_f = sb("h_f", [P, RING_H, S])
        h_hl = sb("h_hl", [P, RING_H, 2, 1, S], F32R)
        y_sb = sb("y", [P, KD, S])
        ln = LayerNorm(ph)
        ps = ph.psum("ps", [P, 8, S])

        loaded = sem("loaded")
        set_up = sem("set_up")
        staged = [sem("staged0"), sem("staged1")]
        w_hi = sem("w_hi")
        w_lo = sem("w_lo")
        x_in_sem = sem("x_in")
        xres_in = sem("xres_in")
        full = [sem("full0"), sem("full1")]
        free = [sem("free0"), sem("free1")]
        xt_hi = sem("xt_hi")
        h_full = sem("h_full")
        h_free = sem("h_free")
        h_hi = sem("h_hi")
        h_lo = sem("h_lo")
        down_done = sem("down_done")
        y_free = sem("y_free")
        masked = sem("masked")
        y_out = sem("y_out")

        def use_x(k, n, pre=False):
            return (0, 0 if pre else n * 3 + 2) if k == 0 else (1, 0 if pre else n * 2 + 1)

        def use_gate(n, pre=False):
            return (0, 1 if pre else n * 3 + 3)

        def use_y(n, tail=False):
            return [(0, n * 3 + 2) if tail else (0, n * 3 + 4), (1, n * 2 + 1) if tail else (1, n * 2 + 2)]

        LAST = B - 1
        SETS = 4

        def program(eng, st):
            st.load_x(0)
            st.transpose_x(0, True)
            st.gate(0, True)
            st.mask(0, 0)
            st.mask(0, 1)
            st.tile(0, 0)
            st.tile(0, 1)
            with eng.Fori(0, LAST) as n:
                st.load_res(n)
                for j in range(2, TILES0):
                    st.tile(n, j)
                    st.down(n, j - 2)
                    if j == 3:
                        st.load_x(n + 1)
                    if j == 12:
                        st.transpose_x(n + 1, False)
                    if j == 14:
                        st.gate(n + 1, False)
                    if j == 18:
                        st.mask(n + 1, 0)
                st.down(n, TILES0 - 2)
                st.down(n, TILES0 - 1)
                st.output(n)
                st.mask(n + 1, 1)
                st.tile(n + 1, 0)
                st.tile(n + 1, 1)
                st.norm(n, False)
            n = LAST
            st.load_res(n)
            for j in range(2, TILES0):
                st.tile(n, j)
                st.down(n, j - 2)
            st.down(n, TILES0 - 2)
            st.down(n, TILES0 - 1)
            st.output(n)
            st.norm(n, True)

        class Stages:
            def load_x(self, n): pass
            def load_res(self, n): pass
            def transpose_x(self, n, pre): pass
            def gate(self, n, pre): pass
            def mask(self, n, e): pass
            def tile(self, n, j): pass
            def down(self, n, j): pass
            def output(self, n): pass
            def norm(self, n, tail): pass

        block = ctx.enter_context(nc.Block())

        @block.sync
        def _(sp):
            for dst, src in ((ident[:], ident_in), (b1_sb[:], b1), (b2_sb[:], b2), (gate_sb[:], gate)):
                sp.dma_start(dst, src).then_inc(loaded, 16)
            for s, v in ((free[0], 1), (free[1], 1), (h_free, 4), (down_done, 3), (y_free, 2),
                         (ln.stat, 1), (ln.applied, 1), (ln.rooted, 1), (y_out, 1)):
                sp.sem_inc(s, v)
            for c in range(6):
                if c >= 2:
                    sp.wait_ge(w_lo, 2 + c - 1)
                    sp.wait_ge(staged[c % 2], 16 * (c // 2))
                src = w1_view[c // 2] if c % 2 == 0 else w2_view[c // 2]
                dst = stage[c % 2][:].rearrange("p (k n) -> p k n", k=KD if c % 2 == 0 else THIRD)
                sp.dma_start(dst, src).then_inc(staged[c % 2], 16)

            class Sync(Stages):
                def load_x(self, n):
                    if not isinstance(n, int):
                        sp.wait_ge(h_free, n * TILES0 - TILES0 + 6)
                    sp.dma_start(x_sb[:], x_view[n]).then_inc(x_in_sem, 16)

                def load_res(self, n):
                    sp.wait_ge(ln.stat, n * 8 + 1)
                    sp.dma_start(x_res[:], x_view[n]).then_inc(xres_in, 16)

                def norm(self, n, tail):
                    sp.wait_ge(ln.applied, n * NT + (NT + 1))
                    sp.dma_start(out_view[n], ln.out[:]).then_inc(y_out, 16)

            program(sp, Sync())
            sp.wait_ge(y_out, 16 * B + 1)

        @block.gpsimd
        def _(pool):
            ln.constants(pool, set_up)

            class Pool(Stages):
                def norm(self, n, tail):
                    ln.root(pool, n)

            pool.wait_ge(set_up, SETS)
            program(pool, Pool())

        @block.vector
        def _(dve):
            dve.wait_ge(loaded, 64)
            dve.tensor_tensor(gate_d[:], gate_sb[:, :, 0], gate_sb[:, :, 1], ALU.subtract).then_inc(set_up, 1)
            dve.tensor_tensor(b2_sum[:, 0], b2_sb[:, 0], b2_sb[:, 1], ALU.add).then_inc(set_up, 1)
            dve.wait_ge(set_up, 3)
            dve.tensor_tensor(b2_sum[:, 1], b2_sum[:, 0], b2_sb[:, 2], ALU.add).then_inc(set_up, 1)
            spread = gate_d[:].unsqueeze(2).broadcast_to([P, KD, P])
            dve.tensor_copy(gate_hl[:, 0], spread).then_inc(w_lo, 1)
            dve.wait_ge(w_lo, 1)
            dve.tensor_tensor(gate_hl[:, 1], spread, raw(gate_hl[:, 0]), ALU.subtract).then_inc(w_lo, 1)
            for c in range(6):
                dve.wait_ge(w_hi, c + 1)
                third = c // 2
                if c % 2 == 0:
                    at, view = slice(third * 1024, third * 1024 + 1024), stage[0][:].rearrange("p (k n) -> p k n", k=KD)
                    dve.tensor_tensor(w1_hl[:, 1, :, at], view, raw(w1_hl[:, 0, :, at]), ALU.subtract).then_inc(w_lo, 1)
                else:
                    at, view = slice(third * THIRD, third * THIRD + THIRD), stage[1][:].rearrange("p (j n) -> p j n", j=THIRD)
                    dve.tensor_tensor(w2_hl[:, 1, at], view, raw(w2_hl[:, 0, at]), ALU.subtract).then_inc(w_lo, 1)

            class Vector(Stages):
                def transpose_x(self, n, pre):
                    for k in range(KD):
                        bank, before = use_x(k, n - 1 if not pre else 0, pre)
                        dve.wait_ge(xt_hi, n * KD + (k + 1))
                        dve.tensor_tensor(xt[:, 1, k], ps[:, 6 + bank], raw(xt[:, 0, k]), ALU.subtract)\
                           .then_inc(free[bank], 1)

                def gate(self, n, pre):
                    bank, before = use_gate(n - 1 if not pre else 0, pre)
                    dve.wait_ge(full[bank], before + 1)
                    dve.tensor_scalar(chosen0[:], ps[:, 6 + bank], 0.0, None, ALU.is_ge).then_inc(free[bank], 1)

                def mask(self, n, e):
                    if e == 0:
                        bank, before = use_gate(n - 1 if not isinstance(n, int) else 0, isinstance(n, int))
                        dve.wait_ge(free[bank], before + 2)
                        if not isinstance(n, int):
                            dve.wait_ge(h_full, n * TILES0 - THIRD)
                        dve.tensor_tensor(xm[0][:].rearrange("p i k s -> p (i k) s"),
                                          raw(xt[:]).rearrange("p i k s -> p (i k) s"),
                                          chosen0[:].unsqueeze(1).broadcast_to([P, 2 * KD, S]), ALU.mult)\
                           .then_inc(masked, 1)
                    else:
                        dve.wait_ge(masked, n * 2 + 1)
                        if not isinstance(n, int):
                            dve.wait_ge(h_full, n * TILES0)
                        dve.tensor_tensor(xm[1][:].rearrange("p i k s -> p (i k s)"),
                                          raw(xt[:]).rearrange("p i k s -> p (i k s)"),
                                          raw(xm[0][:]).rearrange("p i k s -> p (i k s)"), ALU.subtract)\
                           .then_inc(masked, 1)

                def tile(self, n, j):
                    dve.wait_ge(h_hi, n * TILES0 + (j + 1))
                    r = j % RING_H
                    dve.tensor_tensor(h_hl[:, r, 1, 0], h_f[:, r], raw(h_hl[:, r, 0, 0]), ALU.subtract)\
                       .then_inc(h_lo, 1)

                def norm(self, n, tail):
                    ln.run(dve, n, use_y(n, tail), lambda w: dve.wait_ge(full[w[0]], w[1] + 1), free, ps, 6,
                           x_res, xres_in)
                    ln.apply(dve, n, y_out)

            dve.wait_ge(set_up, SETS)
            program(dve, Vector())

        @block.scalar
        def _(act):
            act.wait_ge(loaded, 64)
            for c in range(6):
                act.wait_ge(staged[c % 2], 16 * (c // 2 + 1))
                third = c // 2
                if c % 2 == 0:
                    at = slice(third * 1024, third * 1024 + 1024)
                    act.activation(w1_hl[:, 0, :, at], stage[0][:].rearrange("p (k n) -> p k n", k=KD), ACT.Copy)\
                       .then_inc(w_hi, 1)
                else:
                    at = slice(third * THIRD, third * THIRD + THIRD)
                    act.activation(w2_hl[:, 0, at], stage[1][:].rearrange("p (j n) -> p j n", j=THIRD), ACT.Copy)\
                       .then_inc(w_hi, 1)

            class Scalar(Stages):
                def transpose_x(self, n, pre):
                    for k in range(KD):
                        bank, before = use_x(k, n - 1 if not pre else 0, pre)
                        act.wait_ge(full[bank], before + 1)
                        act.activation(xt[:, 0, k], ps[:, 6 + bank], ACT.Copy).then_inc(xt_hi, 1)

                def tile(self, n, j):
                    r = j % RING_H
                    act.wait_ge(h_full, n * TILES0 + (j + 1))
                    act.wait_ge(down_done, n * TILES0 + (j + 1))
                    act.activation(h_f[:, r], ps[:, j % 4], ACT.Relu, bias=b1_sb[:, j:j + 1]).then_inc(h_free, 1)
                    act.wait_ge(h_free, n * TILES0 + (j + 5))
                    act.activation(h_hl[:, r, 0, 0], h_f[:, r], ACT.Copy).then_inc(h_hi, 1)

                def output(self, n):
                    act.wait_ge(down_done, n * TILES0 + (TILES0 + 3))
                    for k in range(KD):
                        act.activation(y_sb[:, k], ps[:, 4 + k], ACT.Identity, bias=b2_sum[:, 1, k:k + 1])\
                           .then_inc(y_free, 1)

            act.wait_ge(set_up, SETS)
            program(act, Scalar())

        @block.tensor
        def _(pe):
            pe.wait_ge(set_up, SETS)
            pe.wait_ge(w_lo, 8)

            def take(use):
                pe.wait_ge(free[use[0]], use[1] + 1)
                return ps[:, 6 + use[0]]

            class Tensor(Stages):
                def transpose_x(self, n, pre):
                    pe.wait_ge(x_in_sem, n * 16 + 16)
                    for k in range(KD):
                        use = use_x(k, n - 1 if not pre else 0, pre)
                        bank = take(use)
                        for t in range(NT):
                            ins = pe.transpose(bank[:, t * P:(t + 1) * P], x_sb[:, t, k * P:(k + 1) * P], ident[:])
                        ins.then_inc(full[use[0]], 1)

                def gate(self, n, pre):
                    m = n - 1 if not pre else 0
                    for k in range(KD):
                        bank, before = use_x(k, m, pre)
                        pe.wait_ge(free[bank], before + 2)
                    use = use_gate(m, pre)
                    matmul3(pe, take(use), gate_hl, xt, slice(0, P), slice(0, S), KD).then_inc(full[use[0]], 1)

                def tile(self, n, j):
                    third = j // THIRD
                    pe.wait_ge(h_free, n * TILES0 + (j + 1))
                    if j == THIRD:
                        pe.wait_ge(masked, n * 2 + 1)
                    if j == 2 * THIRD:
                        pe.wait_ge(masked, n * 2 + 2)
                    x = xt if third == 0 else xm[third - 1]
                    matmul3(pe, ps[:, j % 4], w1_hl, x, slice(j * P, (j + 1) * P), slice(0, S), KD).then_inc(h_full, 1)

                def down(self, n, j):
                    r = j % RING_H
                    pe.wait_ge(h_lo, n * TILES0 + (j + 1))
                    if j == 0:
                        pe.wait_ge(y_free, n * 2 + 2)
                    for k in range(KD):
                        for i, (a, b) in enumerate(TERMS):
                            ins = pe.matmul(ps[:, 4 + k], w2_hl[:, a, j, k * P:(k + 1) * P], h_hl[:, r, b, 0],
                                            start=(j == 0 and i == 0), stop=(j == TILES0 - 1 and i == 2))
                    ins.then_inc(down_done, 1)

                def norm(self, n, tail):
                    pe.wait_ge(y_free, n * 2 + 4)
                    ln.transposes(pe, take, use_y(n, tail), y_sb, ident, full)

            program(pe, Tensor())


KV = 4
REACH = 32
WINDOW = P + 2 * REACH
G_HEADS = 8
G_TILES = 2 * NT * 2
G_STEPS = 2 * NT
C_Q, C_QS, C_K, C_KS, C_V, C_O = 0, D, 2 * D, 2 * D + P, 2 * D + 2 * P, 2 * D + 2 * P + KV * HD
W1_COLS = C_O + D
A1_PRE = 38
A1_LOOP = 34
S_LAG = 1


def attention1(nc, x_in, weights, tables, select, ident_in, band_in, x_out):
    x_view = x_in.rearrange("(n t p) d -> n p t d", t=NT, p=P)
    out_view = x_out.rearrange("(n t p) d -> n p t d", t=NT, p=P)
    ctx = ExitStack()
    with ctx:
        ph = Phase(nc, ctx, "a1")
        sb, sem = ph.sb, ph.sem
        w_raw = sb("w_raw", [P, KD, W1_COLS])
        w_hl = sb("w_hl", [P, 2, KD, W1_COLS], F32R)
        sel_raw = sb("sel_raw", [P, 24, P])
        sel = sb("sel", [P, 24, P], F32R)
        rope = sb("rope", [P, 2, S])
        ident = sb("ident", [P, P])
        ident_b = sb("ident_b", [P, P], BF16)
        band = sb("band", [P, 2, WINDOW])
        band_b = sb("band_b", [P, 2, WINDOW], BF16)
        x_sb = sb("x", [P, NT, D])
        x_res = sb("x_res", [P, NT, D])
        xt = sb("xt", [P, 2, KD, S], F32R)
        rot = [[sb(f"rot{o}{i}", [P, S]) for i in range(2)] for o in range(2)]
        qk = [sb(f"qk{o}", [P, S]) for o in range(2)]
        qk_hl = [sb(f"qk_hl{o}", [P, 2, S], F32R) for o in range(2)]
        q_st = [sb(f"q_st{i}", [P, 4, S], F32R) for i in range(2)]
        k_st = [sb(f"k_st{i}", [P, 2, S], F32R) for i in range(2)]
        v_aug = [sb(f"v_aug{i}", [P, NT, 2, 32]) for i in range(2)]
        nmax = sb("nmax", [P, NT, G_HEADS])
        nmax2 = sb("nmax2", [P, NT, P], F32R)
        m_t = sb("m_t", [P, S], F32R)
        probs = sb("probs", [P, 4, 2 * WINDOW])
        pv_sb = [sb(f"pv_sb{i}", [P, S]) for i in range(2)]
        rden = sb("rden", [P, 2, NT, 4])
        o_tok = sb("o_tok", [P, NT, D])
        o_hl = sb("o_hl", [P, 2, KD, S], F32R)
        y_sb = sb("y", [P, KD, S])
        ln = LayerNorm(ph)

        ps = ph.psum("ps", [P, 8, S])

        loaded = sem("loaded")
        set_up = sem("set_up")
        w_split = sem("w_split")
        x_in_sem = sem("x_in")
        xres_in = sem("xres_in")
        w_full = sem("w_full")
        w_free = [sem("w_free0"), sem("w_free1")]
        xt_hi = sem("xt_hi")
        rotated = sem("rotated")
        qk_hi = sem("qk_hi")
        qk_lo = sem("qk_lo")
        s_full = sem("s_full")
        s_free = sem("s_free")
        t_full = sem("t_full")
        t_free = sem("t_free")
        pv_step = sem("pv_step")
        pv_free = sem("pv_free")
        nm_hi = sem("nm_hi")
        nm_ready = sem("nm_ready")
        rden_ok = sem("rden_ok")
        o_hi = sem("o_hi")
        y_out = sem("y_out")

        def work(c, n):
            return c % 2, c // 2 + n * (A1_LOOP // 2), c + n * A1_LOOP

        def later(w, k):
            slot, before, count = w
            return (slot + k) % 2, before + (slot + k) // 2, count + k

        def unit(u, per, k):
            return u[0] * (2 * per) + (u[1] * per + k)

        def window(block):
            lo, hi = max(0, block * P - REACH), min(S, (block + 1) * P + REACH)
            return lo, hi, lo - (block * P - REACH)

        def tile_at(k):
            return k // (2 * NT), k // 2 % NT, 2 * (k % 2)

        def slot_order(e, m, first, end):
            order = []
            lag = S_LAG if e and m else 0
            for k in range(first, min(end, G_TILES + lag)):
                if e and k < G_TILES:
                    order.append(("t", k))
                    if k == 10:
                        order.append(("copy", 0))
                    if k % 2 and k >= 3:
                        order.append(("pv", k // 2 - 1))
                if e and k == G_TILES - 1 + min(lag, 1):
                    order.append(("pv", G_STEPS - 1))
                    order.append(("copy", 1))
                if m and k >= lag:
                    order.append(("s", k - lag))
            return order

        LAST = B - 1
        END = G_TILES + S_LAG
        LOOP = {k: A1_PRE + v for k, v in dict(r1=0, b_n0=2, b_t=3, b_n1=4, s1=5, v=11, xt=13, r0=15, ot=19, o=21,
                                               yt=23, a_n0=25, a_t=26, a_n1=27, s0=28).items()}
        TAIL = {k: A1_PRE + v for k, v in dict(r1=0, b_n0=2, b_t=3, b_n1=4, s1=5, v=11, ot=13, o=15, yt=17, a_n0=19,
                                               a_t=20, a_n1=21).items()}
        FINAL = {k: A1_PRE + v for k, v in dict(n0=22, n1=23, ot=24, o=26, yt=28).items()}

        def turn(st, n, uses, more):
            def use(name):
                return work(uses[name], n)

            st.load_res(n)
            e, m = (n, 1), (n + 1, 0)
            st.slot(e, m, 0, 4)
            st.rotate((n + 1, 1), use("r1"))
            if more:
                st.load_x(n + 2)
            st.slot(e, m, 4, 14)
            st.normalise(e, 0, use("b_n0"))
            st.slot(e, m, 14, END)
            st.maxima(m, use("b_t"))
            st.normalise(e, 1, use("b_n1"))
            st.stack((n + 1, 1), use("s1"))
            st.values(n + 1, use("v"))
            if more:
                st.transpose_x(n + 2, use("xt"))
            e, m = (n + 1, 0), (n + 1, 1)
            st.slot(e, m, 0, 3)
            if more:
                st.rotate((n + 2, 0), use("r0"))
            st.slot(e, m, 3, 6)
            st.transpose_out(n, use("ot"))
            st.slot(e, m, 6, 9)
            st.project_out(n, use("o"))
            st.slot(e, m, 9, 12)
            st.norm(n, use("yt"))
            st.slot(e, m, 12, 14)
            st.normalise(e, 0, use("a_n0"))
            st.slot(e, m, 14, END)
            st.maxima(m, use("a_t"))
            st.normalise(e, 1, use("a_n1"))
            st.store(n)
            if more:
                st.stack((n + 2, 0), use("s0"))

        def program(eng, st):
            st.load_x(0)
            st.transpose_x(0, work(0, 0))
            st.rotate((0, 0), work(2, 0))
            st.stack((0, 0), work(6, 0))
            st.values(0, work(12, 0))
            st.slot(None, (0, 0), 0, END)
            st.maxima((0, 0), work(14, 0))
            st.rotate((0, 1), work(15, 0))
            st.load_x(1)
            st.stack((0, 1), work(17, 0))
            st.transpose_x(1, work(23, 0))
            st.slot((0, 0), (0, 1), 0, 6)
            st.rotate((1, 0), work(25, 0))
            st.slot((0, 0), (0, 1), 6, 14)
            st.normalise((0, 0), 0, work(29, 0))
            st.slot((0, 0), (0, 1), 14, END)
            st.maxima((0, 1), work(30, 0))
            st.normalise((0, 0), 1, work(31, 0))
            st.stack((1, 0), work(32, 0))
            with eng.Fori(0, LAST - 1) as n:
                turn(st, n, LOOP, True)
            turn(st, LAST - 1, TAIL, False)
            st.load_res(LAST)
            n = LAST - 1
            st.slot((LAST, 1), None, 0, 14)
            st.normalise((LAST, 1), 0, work(FINAL["n0"], n))
            st.slot((LAST, 1), None, 14, END)
            st.normalise((LAST, 1), 1, work(FINAL["n1"], n))
            st.transpose_out(LAST, work(FINAL["ot"], n))
            st.project_out(LAST, work(FINAL["o"], n))
            st.norm(LAST, work(FINAL["yt"], n))
            st.store(LAST)

        def made(u):
            return (0, 1) if u[1] == 0 else (0,)

        def operand(u, o):
            return u[0] * 3 + (2 if u[1] else o)

        class Stages:
            def load_x(self, n): pass
            def load_res(self, n): pass
            def transpose_x(self, n, w): pass
            def rotate(self, u, w): pass
            def stack(self, u, w): pass
            def values(self, n, w): pass
            def slot(self, e, m, first, end): pass
            def maxima(self, u, w): pass
            def normalise(self, u, g, w): pass
            def transpose_out(self, n, w): pass
            def project_out(self, n, w): pass
            def norm(self, n, w): pass
            def store(self, n): pass

        SETS = 6
        block = ctx.enter_context(nc.Block())

        @block.sync
        def _(sp):
            for dst, src in ((w_raw[:], weights.rearrange("(k p) n -> p k n", p=P)), (sel_raw[:], select),
                             (rope[:], tables), (ident[:], ident_in), (band[:], band_in)):
                sp.dma_start(dst, src).then_inc(loaded, 16)
            for s, v in ((w_free[0], 1), (w_free[1], 1), (s_free, 2), (t_free, 2), (pv_step, 2), (pv_free, 2),
                         (ln.stat, 1), (ln.applied, 1), (ln.rooted, 1), (y_out, 1)):
                sp.sem_inc(s, v)

            class Sync(Stages):
                def load_x(self, n):
                    if not (isinstance(n, int) and n == 0):
                        sp.wait_ge(rotated, n * 3)
                    sp.dma_start(x_sb[:], x_view[n]).then_inc(x_in_sem, 16)

                def load_res(self, n):
                    sp.wait_ge(ln.stat, n * 8 + 1)
                    sp.dma_start(x_res[:], x_view[n]).then_inc(xres_in, 16)

                def store(self, n):
                    sp.wait_ge(ln.applied, n * NT + (NT + 1))
                    sp.dma_start(out_view[n], ln.out[:]).then_inc(y_out, 16)

            program(sp, Sync())
            sp.wait_ge(y_out, 16 * B + 1)

        @block.gpsimd
        def _(pool):
            pool.memset(raw(nmax2[:]), 0.0).then_inc(set_up, 1)
            for i in range(2):
                pool.memset(v_aug[i][:], 1.0).then_inc(set_up, 1)
            ln.constants(pool, set_up)
            pool.wait_ge(set_up, SETS)

            class Pool(Stages):
                def rotate(self, u, w):
                    for o in made(u):
                        for i in range(2):
                            slot, before, _ = later(w, 2 * o + i)
                            pool.wait_ge(w_free[slot], before + 2)
                        pool.tensor_tensor(qk[o][:], rot[o][0][:], rot[o][1][:], ALU.add).then_inc(rotated, 1)
                    for o in made(u):
                        pool.wait_ge(qk_hi, operand(u, o) + 1)
                        pool.tensor_tensor(qk_hl[o][:, 1], qk[o][:], raw(qk_hl[o][:, 0]), ALU.subtract)\
                            .then_inc(qk_lo, 1)

                def norm(self, n, w):
                    ln.root(pool, n)
                    ln.apply(pool, n, y_out)

            program(pool, Pool())

        @block.vector
        def _(dve):
            dve.wait_ge(loaded, 16 * 5)
            dve.tensor_copy(ident_b[:], ident[:]).then_inc(set_up, 1)
            dve.tensor_copy(band_b[:], band[:]).then_inc(set_up, 1)
            dve.wait_ge(w_split, 2)
            dve.tensor_tensor(w_hl[:, 1], w_raw[:], raw(w_hl[:, 0]), ALU.subtract).then_inc(w_split, 1)
            dve.wait_ge(set_up, SETS)

            class Vector(Stages):
                def transpose_x(self, n, w):
                    for k in range(KD):
                        slot, _, _ = later(w, k)
                        dve.wait_ge(xt_hi, n * KD + (k + 1))
                        dve.tensor_tensor(xt[:, 1, k], ps[:, 6 + slot], raw(xt[:, 0, k]), ALU.subtract)\
                           .then_inc(w_free[slot], 1)

                def rotate(self, u, w):
                    for o in made(u):
                        for i in range(2):
                            slot, _, count = later(w, 2 * o + i)
                            dve.wait_ge(w_full, count + 1)
                            dve.tensor_tensor(rot[o][i][:], ps[:, 6 + slot], rope[:, i], ALU.mult)\
                               .then_inc(w_free[slot], 1)

                def values(self, n, w):
                    for pair in range(NT // 2):
                        slot, _, count = later(w, pair)
                        dve.wait_ge(w_full, count + 1)
                        tile = ps[:, 6 + slot, 0:2 * KV * HD].rearrange("p (t q c e) -> p q t c e", t=2, q=2, e=HD)
                        for q in range(2):
                            ins = dve.tensor_copy(v_aug[q][:, 2 * pair:2 * pair + 2, :, 0:HD], tile[:, q])
                        ins.then_inc(w_free[slot], 1)

                def stack(self, u, w):
                    q = u[1]
                    for dst, i in ((q_st[q][:, 1], 1), (q_st[q][:, 3], 3), (k_st[q][:, 1], 5)):
                        slot, _, count = later(w, i)
                        dve.wait_ge(w_full, count + 1)
                        dve.tensor_copy(dst, ps[:, 6 + slot]).then_inc(w_free[slot], 1)

                def slot(self, e, m, first, end):
                    for kind, k in slot_order(e, m, first, end):
                        if kind == "s":
                            c, i, r = tile_at(k)
                            lo, hi, _ = window(i)
                            dve.wait_ge(s_full, unit(m, G_TILES, k + 1))
                            dve.tensor_reduce(nmax[:, i, 4 * c + r:4 * c + r + 2],
                                              ps[:, k % 2, 0:2 * (hi - lo)].rearrange("p (h s) -> p h s", h=2),
                                              AX.X, ALU.max, negate=True).then_inc(s_free, 1)

                def maxima(self, u, w):
                    dve.wait_ge(s_free, unit(u, G_TILES, G_TILES + 2))
                    dve.tensor_copy(nmax2[:, :, 0:G_HEADS], nmax[:]).then_inc(nm_hi, 1)
                    dve.wait_ge(nm_hi, unit(u, 1, 1))
                    dve.tensor_tensor(nmax2[:, :, G_HEADS:2 * G_HEADS], nmax[:], raw(nmax2[:, :, 0:G_HEADS]),
                                      ALU.subtract).then_inc(nm_ready, 1)

                def normalise(self, u, g, w):
                    slot, _, count = w
                    dve.wait_ge(w_full, count + 1)
                    tile = ps[:, 6 + slot].rearrange("p (t r c) -> p t r c", t=NT, r=4)
                    dve.reciprocal(rden[:, g], tile[:, :, :, HD]).then_inc(rden_ok, 1)
                    dve.wait_ge(rden_ok, unit(u, 2, g + 1))
                    at = (u[1] * 2 + g) * 4 * HD
                    dve.tensor_tensor(o_tok[:, :, at:at + 4 * HD].rearrange("p t (r e) -> p t r e", e=HD),
                                      tile[:, :, :, 0:HD],
                                      rden[:, g].unsqueeze(3).broadcast_to([P, NT, 4, HD]),
                                      ALU.mult).then_inc(w_free[slot], 1)

                def transpose_out(self, n, w):
                    for k in range(KD):
                        slot, _, _ = later(w, k)
                        dve.wait_ge(o_hi, n * KD + (k + 1))
                        dve.tensor_tensor(o_hl[:, 1, k], ps[:, 6 + slot], raw(o_hl[:, 0, k]), ALU.subtract)\
                           .then_inc(w_free[slot], 1)

                def norm(self, n, w):
                    ln.run(dve, n, [later(w, k) for k in range(2)], lambda w: dve.wait_ge(w_full, w[2] + 1),
                           w_free, ps, 6, x_res, xres_in)

            program(dve, Vector())

        @block.scalar
        def _(act):
            act.wait_ge(loaded, 16 * 5)
            act.activation(sel[:], sel_raw[:], ACT.Copy).then_inc(w_split, 1)
            act.activation(w_hl[:, 0], w_raw[:], ACT.Copy).then_inc(w_split, 1)
            act.wait_ge(set_up, SETS)

            class Scalar(Stages):
                def transpose_x(self, n, w):
                    for k in range(KD):
                        slot, _, count = later(w, k)
                        act.wait_ge(w_full, count + 1)
                        act.activation(xt[:, 0, k], ps[:, 6 + slot], ACT.Copy).then_inc(xt_hi, 1)

                def rotate(self, u, w):
                    for o in made(u):
                        act.wait_ge(rotated, operand(u, o) + 1)
                        act.activation(qk_hl[o][:, 0], qk[o][:], ACT.Copy).then_inc(qk_hi, 1)

                def stack(self, u, w):
                    q = u[1]
                    for dst, i in ((q_st[q][:, 0], 0), (q_st[q][:, 2], 2), (k_st[q][:, 0], 4)):
                        slot, _, count = later(w, i)
                        act.wait_ge(w_full, count + 1)
                        act.activation(dst, ps[:, 6 + slot], ACT.Copy).then_inc(w_free[slot], 1)

                def slot(self, e, m, first, end):
                    for kind, k in slot_order(e, m, first, end):
                        if kind == "t":
                            lo, hi, _ = window(tile_at(k)[1])
                            act.wait_ge(t_full, unit(e, G_TILES, k + 1))
                            if k % 2 == 0:
                                act.wait_ge(pv_step, unit(e, G_STEPS, k // 2 + 1))
                            act.activation(probs[:, k % 4, 0:2 * (hi - lo)], ps[:, 2 + k % 2, 0:2 * (hi - lo)],
                                           ACT.Exp, scale=HD ** -0.5).then_inc(t_free, 1)
                        elif kind == "copy":
                            act.wait_ge(pv_step, unit(e, G_STEPS, NT * (k + 1) + 2))
                            act.activation(pv_sb[k][:], ps[:, 4 + k], ACT.Copy).then_inc(pv_free, 1)

                def maxima(self, u, w):
                    slot, _, count = w
                    act.wait_ge(w_full, count + 1)
                    act.activation(m_t[:], ps[:, 6 + slot], ACT.Copy).then_inc(w_free[slot], 1)

                def transpose_out(self, n, w):
                    for k in range(KD):
                        slot, _, count = later(w, k)
                        act.wait_ge(w_full, count + 1)
                        act.activation(o_hl[:, 0, k], ps[:, 6 + slot], ACT.Copy).then_inc(o_hi, 1)

                def project_out(self, n, w):
                    for k in range(KD):
                        slot, _, count = later(w, k)
                        act.wait_ge(w_full, count + 1)
                        act.activation(y_sb[:, k], ps[:, 6 + slot], ACT.Copy).then_inc(w_free[slot], 1)

            program(act, Scalar())

        @block.tensor
        def _(pe):
            pe.wait_ge(set_up, SETS)
            pe.wait_ge(w_split, 3)

            def take(w):
                slot, before, _ = w
                pe.wait_ge(w_free[slot], before + 1)
                return ps[:, 6 + slot]

            def emptied(w):
                slot, before, _ = w
                pe.wait_ge(w_free[slot], before + 2)

            class Tensor(Stages):
                def transpose_x(self, n, w):
                    pe.wait_ge(x_in_sem, n * 16 + 16)
                    for k in range(KD):
                        bank = take(later(w, k))
                        for t in range(NT):
                            ins = pe.transpose(bank[:, t * P:(t + 1) * P], x_sb[:, t, k * P:(k + 1) * P], ident[:])
                        ins.then_inc(w_full, 1)
                    self.w_x = w

                def rotate(self, u, w):
                    n, q = u
                    if q == 0:
                        for k in range(KD):
                            emptied(later(self.w_x, k))
                    for o in made(u):
                        for i in range(2):
                            at = (C_Q, C_QS)[i] + q * P if o == 0 else (C_K, C_KS)[i]
                            matmul3(pe, take(later(w, 2 * o + i)), w_hl, xt, slice(at, at + P), slice(0, S), KD)\
                                .then_inc(w_full, 1)

                def stack(self, u, w):
                    q = u[1]
                    pe.wait_ge(qk_lo, operand(u, made(u)[-1]) + 1)
                    for i, (o, first) in enumerate([(0, 2 * r) for r in range(4)]
                                                   + [(1, 8 + 2 * (2 * q + c)) for c in range(2)]):
                        bank = take(later(w, i))
                        for part in range(2):
                            ins = pe.matmul(bank, sel[:, first + part], qk_hl[o][:, part], start=(part == 0),
                                            stop=(part == 1))
                        ins.then_inc(w_full, 1)
                    for i in (4, 5):
                        emptied(later(w, i))

                def values(self, n, w):
                    self.w_v = w
                    for pair in range(NT // 2):
                        bank = take(later(w, pair))
                        for t in range(2):
                            at, wide = (2 * pair + t) * P, KV * HD
                            ins = matmul3(pe, bank[:, t * wide:(t + 1) * wide], xt, w_hl, slice(at, at + P),
                                          slice(C_V, C_V + wide), KD)
                        ins.then_inc(w_full, 1)

                def slot(self, e, m, first, end):
                    for kind, k in slot_order(e, m, first, end):
                        if kind == "t":
                            q = e[1]
                            c, tb, r = tile_at(k)
                            lo, hi, off = window(tb)
                            wd = hi - lo
                            if k == 0 and isinstance(e[0], int) and e == (LAST, 1):
                                emptied(self.w_m)
                            pe.wait_ge(t_free, unit(e, G_TILES, k + 1))
                            tile = ps[:, 2 + k % 2, 0:2 * wd]
                            pe.matmul(tile, ident_b[:], band_b[:, :, off:off + wd], start=True, stop=False)
                            pe.matmul(tile, k_st[q][:, c, tb * P:(tb + 1) * P], q_st[q][:, r:r + 2, lo:hi],
                                      start=False, stop=False)
                            for j in range(2):
                                ins = pe.matmul(tile[:, j * wd:(j + 1) * wd], sel[:, 16 + 4 * c + r + j], m_t[:, lo:hi],
                                                start=False, stop=(j == 1))
                            ins.then_inc(t_full, 1)
                        elif kind == "s":
                            q = m[1]
                            c, i, r = tile_at(k)
                            lo, hi, off = window(i)
                            wd = hi - lo
                            pe.wait_ge(s_free, unit(m, G_TILES, k + 1))
                            tile = ps[:, k % 2, 0:2 * wd]
                            pe.matmul(tile, ident_b[:], band_b[:, :, off:off + wd], start=True, stop=False)
                            for j in range(2):
                                ins = pe.matmul(tile[:, j * wd:(j + 1) * wd], q_st[q][:, r + j, i * P:(i + 1) * P],
                                                k_st[q][:, c, lo:hi], start=False, stop=(j == 1))
                            ins.then_inc(s_full, 1)
                        elif kind == "pv":
                            c, tb = k // NT, k % NT
                            lo, hi, _ = window(tb)
                            wd = hi - lo
                            if k == 0 and e[1] == 0:
                                for pair in range(NT // 2):
                                    emptied(later(self.w_v, pair))
                            if tb == 0:
                                pe.wait_ge(pv_free, unit(e, 2, c + 1))
                            pe.wait_ge(t_free, unit(e, G_TILES, 2 * k + 2 + 2))
                            for r in range(4):
                                at = (r % 2) * wd
                                ins = pe.matmul(ps[32 * r:32 * r + 32, 4 + c, lo:hi], v_aug[e[1]][:, tb, c, :],
                                                probs[:, (2 * k + r // 2) % 4, at:at + wd],
                                                start=(tb == 0), stop=(tb == NT - 1), skip_group_check=True)
                            ins.then_inc(pv_step, 1)

                def maxima(self, u, w):
                    bank = take(w)
                    pe.wait_ge(nm_ready, unit(u, 1, 1))
                    for t in range(NT):
                        ins = pe.transpose(bank[:, t * P:(t + 1) * P], raw(nmax2[:, t]), ident[:])
                    ins.then_inc(w_full, 1)
                    self.w_m = w

                def normalise(self, u, g, w):
                    bank = take(w)
                    pe.wait_ge(pv_free, unit(u, 2, g + 1 + 2))
                    for t in range(NT):
                        ins = pe.transpose(bank[:, t * P:(t + 1) * P], pv_sb[g][:, t * P:(t + 1) * P], ident[:])
                    ins.then_inc(w_full, 1)
                    self.w_n = w

                def transpose_out(self, n, w):
                    if isinstance(n, int) and n == LAST:
                        emptied(self.w_n)
                    for k in range(KD):
                        bank = take(later(w, k))
                        for t in range(NT):
                            ins = pe.transpose(bank[:, t * P:(t + 1) * P], o_tok[:, t, k * P:(k + 1) * P], ident[:])
                        ins.then_inc(w_full, 1)
                    self.w_o = w

                def project_out(self, n, w):
                    for k in range(KD):
                        emptied(later(self.w_o, k))
                    for k in range(KD):
                        matmul3(pe, take(later(w, k)), w_hl, o_hl, slice(C_O + k * P, C_O + (k + 1) * P),
                                slice(0, S), KD).then_inc(w_full, 1)
                    self.w_y = w

                def norm(self, n, w):
                    for k in range(KD):
                        emptied(later(self.w_y, k))
                    ln.transposes(pe, take, [later(w, k) for k in range(2)], y_sb, ident, [w_full, w_full])

            program(pe, Tensor())


E = 16
GROUPS = 4
EPG = E // GROUPS
TOP_GROUPS = 2
TOP_K = 4
HID_SHARED = 512
HID_EXPERT = 64
HID1 = HID_SHARED + E * HID_EXPERT
T_SHARED = HID_SHARED // P
TILES1 = HID1 // P
RING1 = 3
FIRST = 6
BIG = 1.0e30
ROUTE_PARTS = 3
ROUTE = 27
F1_PRE = 6
F1_LOOP = 14


def feed_forward1(nc, x_in, w_gu, w_down, w_router, bias, lower, spread, ident_in, x_out):
    x_view = x_in.rearrange("(n t p) d -> n p t d", t=NT, p=P)
    out_view = x_out.rearrange("(n t p) d -> n p t d", t=NT, p=P)
    gu_view = w_gu.rearrange("(k p) (c n) -> c p k n", p=P, c=3)
    down_view = w_down.rearrange("(c j p) n -> c p j n", p=P, c=2)
    ctx = ExitStack()
    with ctx:
        ph = Phase(nc, ctx, "f1")
        sb, sem = ph.sb, ph.sem
        stage = [sb(f"stage{i}", [P, 2 * 1024]) for i in range(2)]
        gu_hl = sb("gu", [P, 2, KD, 2 * HID1], F32R)
        down_hl = sb("down", [P, 2, TILES1, D], F32R)
        router_sb = sb("router", [P, KD, E])
        router_hl = sb("router_hl", [P, 2, KD, E], F32R)
        bias_sb = sb("bias", [P, E])
        lower_sb = sb("lower", [P, E, E])
        spread_sb = sb("spread", [P, E // 2, P])
        spread_r = sb("spread_r", [P, E // 2, P], F32R)
        ident = sb("ident", [P, P])
        x_sb = sb("x", [P, NT, D])
        x_res = sb("x_res", [P, NT, D])
        xt = sb("xt", [P, 2, KD, S], F32R)
        e_neg = sb("e_neg", [P, NT, E])
        denom = sb("denom", [P, NT, E])
        score = sb("score", [P, NT, E])
        biased = sb("biased", [P, NT, E])
        pair_max = sb("pair_max", [P, NT, GROUPS, 2])
        pair_min = sb("pair_min", [P, NT, GROUPS, 2])
        top = sb("top", [P, 4, NT, GROUPS])
        group = sb("group", [P, NT, GROUPS])
        beats_g = sb("beats_g", [P, 2, NT, GROUPS, GROUPS])
        rank_g = sb("rank_g", [P, NT, GROUPS])
        keep_g = sb("keep_g", [P, 2, NT, GROUPS])
        masked = sb("masked", [P, 2, NT, E])
        beats = sb("beats", [P, 2, NT, E, E])
        rank = sb("rank", [P, NT, E])
        chosen = sb("chosen", [P, NT, E])
        total = sb("total", [P, 2, NT])
        inverse = sb("inverse", [P, NT])
        combine = sb("combine", [P, NT, E])
        combine2 = sb("combine2", [P, NT, P], F32R)
        combine_t = sb("combine_t", [P, S], F32R)
        tanh = sb("tanh", [P, 2, S])
        gated = sb("gated", [P, 2, S])
        scaled = sb("scaled", [P, 2, S])
        h_f = sb("h_f", [P, RING1, S])
        h_hl = sb("h_hl", [P, RING1, 2, S], F32R)
        y_sb = sb("y", [P, KD, S])
        ln = LayerNorm(ph)
        ps = ph.psum("ps", [P, 8, S])

        loaded = sem("loaded")
        set_up = sem("set_up")
        staged = [sem("staged0"), sem("staged1")]
        w_hi = sem("w_hi")
        w_lo = sem("w_lo")
        x_in_sem = sem("x_in")
        xres_in = sem("xres_in")
        w_full = sem("w_full")
        w_free = [sem("w_free0"), sem("w_free1")]
        xt_hi = sem("xt_hi")
        g_full = sem("g_full")
        u_full = sem("u_full")
        tanh_done = sem("tanh_done")
        gated_done = sem("gated_done")
        h_made = sem("h_made")
        h_hi = sem("h_hi")
        h_lo = sem("h_lo")
        y_full = sem("y_full")
        y_free = sem("y_free")
        routed = sem("routed")
        combined = sem("combined")
        y_out = sem("y_out")

        def work(c, n):
            return c % 2, c // 2 + n * (F1_LOOP // 2), c + n * F1_LOOP

        def later(w, k):
            slot, before, count = w
            return (slot + k) % 2, before + (slot + k) // 2, count + k

        LAST = B - 1
        LOOP = {k: F1_PRE + v for k, v in dict(c=0, xt=6, logits=8, first_c=9, yt=12).items()}
        TAIL = {"yt": F1_PRE + 6}

        def program(eng, st):
            st.load_x(0)
            st.transpose_x(0, work(0, 0))
            st.logits(0, work(2, 0))
            first_tiles(st, 0, work(2, 0), [work(c, 0) for c in (3, 4, 5)], None)
            with eng.Fori(0, LAST) as n:
                st.load_res(n)
                last_tiles(st, n, LOOP["c"])
                st.load_x(n + 1)
                st.transpose_x(n + 1, work(LOOP["xt"], n))
                st.down(n, TILES1 - 2)
                st.down(n, TILES1 - 1)
                st.output(n)
                st.logits(n + 1, work(LOOP["logits"], n))
                first_tiles(st, n + 1, work(LOOP["logits"], n), [work(LOOP["first_c"] + c, n) for c in range(3)],
                            (n, work(LOOP["yt"], n)))
            st.load_res(LAST)
            last_tiles(st, LAST, LOOP["c"])
            st.down(LAST, TILES1 - 2)
            st.down(LAST, TILES1 - 1)
            st.output(LAST)
            st.norm(LAST, work(TAIL["yt"], LAST))

        def first_tiles(st, n, logits_use, uses, before):
            for j in range(FIRST):
                st.gate(n, j)
                if j == T_SHARED:
                    st.combine(n, uses[0])
                st.tile(n, j, uses[1 + j - T_SHARED] if j >= T_SHARED else None)
                if j < ROUTE_PARTS:
                    st.route(n, j, logits_use)
                if j >= 2:
                    st.down(n, j - 2)
            if before:
                st.norm(*before)

        def last_tiles(st, n, c_use):
            for j in range(FIRST, TILES1):
                st.gate(n, j)
                st.tile(n, j, work(c_use + j - FIRST, n))
                st.down(n, j - 2)

        class Stages:
            def load_x(self, n): pass
            def load_res(self, n): pass
            def transpose_x(self, n, w): pass
            def logits(self, n, w): pass
            def route(self, n, part, w): pass
            def combine(self, n, w): pass
            def gate(self, n, j): pass
            def tile(self, n, j, w): pass
            def down(self, n, j): pass
            def output(self, n): pass
            def norm(self, n, w): pass

        SETS = 5
        PIECES = 5
        block = ctx.enter_context(nc.Block())

        def piece(c):
            if c < 3:
                at = slice(c * 1024, (c + 1) * 1024)
                return (stage[c % 2][:].rearrange("p (k n) -> p k n", k=KD), gu_view[c],
                        gu_hl[:, 0, :, at], gu_hl[:, 1, :, at])
            at = slice((c - 3) * 6, (c - 3) * 6 + 6)
            return (stage[c % 2][:, 0:6 * D].rearrange("p (j n) -> p j n", j=6), down_view[c - 3],
                    down_hl[:, 0, at], down_hl[:, 1, at])

        @block.sync
        def _(sp):
            for dst, src in ((ident[:], ident_in), (router_sb[:], w_router), (bias_sb[:], bias),
                             (lower_sb[:], lower), (spread_sb[:], spread)):
                sp.dma_start(dst, src).then_inc(loaded, 16)
            for s, v in ((w_free[0], 1), (w_free[1], 1), (h_made, 2), (y_free, 2), (routed, 1),
                         (ln.stat, 1), (ln.applied, 1), (ln.rooted, 1), (y_out, 1)):
                sp.sem_inc(s, v)
            for c in range(PIECES):
                if c >= 2:
                    sp.wait_ge(w_lo, c - 1)
                    sp.wait_ge(staged[c % 2], 16 * (c // 2))
                sp.dma_start(piece(c)[0], piece(c)[1]).then_inc(staged[c % 2], 16)

            class Sync(Stages):
                def load_x(self, n):
                    if not isinstance(n, int):
                        sp.wait_ge(h_made, n * TILES1 - TILES1 + 3)
                    sp.dma_start(x_sb[:], x_view[n]).then_inc(x_in_sem, 16)

                def load_res(self, n):
                    sp.wait_ge(ln.stat, n * 8 + 1)
                    sp.dma_start(x_res[:], x_view[n]).then_inc(xres_in, 16)

                def norm(self, n, w):
                    sp.wait_ge(ln.applied, n * NT + (NT + 1))
                    sp.dma_start(out_view[n], ln.out[:]).then_inc(y_out, 16)

            program(sp, Sync())
            sp.wait_ge(y_out, 16 * B + 1)

        @block.gpsimd
        def _(pool):
            pool.memset(raw(combine2[:]), 0.0).then_inc(set_up, 1)
            ln.constants(pool, set_up)

            class Pool(Stages):
                def tile(self, n, j, w):
                    r = j % RING1
                    pool.wait_ge(h_hi, n * TILES1 + (j + 1))
                    pool.tensor_tensor(h_hl[:, r, 1], h_f[:, r], raw(h_hl[:, r, 0]), ALU.subtract).then_inc(h_lo, 1)

                def norm(self, n, w):
                    ln.root(pool, n)

            pool.wait_ge(set_up, SETS)
            program(pool, Pool())

        @block.vector
        def _(dve):
            dve.wait_ge(set_up, 4)
            dve.tensor_tensor(router_hl[:, 1], router_sb[:], raw(router_hl[:, 0]), ALU.subtract).then_inc(set_up, 1)
            for c in range(PIECES):
                dve.wait_ge(w_hi, c + 1)
                src, _, hi, lo = piece(c)
                if c < 3:
                    dve.tensor_tensor(lo, src, raw(hi), ALU.subtract).then_inc(w_lo, 1)
                else:
                    dve.scalar_tensor_tensor(lo, src, 0.5, raw(hi), ALU.mult, ALU.subtract).then_inc(w_lo, 1)

            class Vector(Stages):
                def transpose_x(self, n, w):
                    for k in range(KD):
                        slot, _, _ = later(w, k)
                        dve.wait_ge(xt_hi, n * KD + (k + 1))
                        dve.tensor_tensor(xt[:, 1, k], ps[:, 6 + slot], raw(xt[:, 0, k]), ALU.subtract)\
                           .then_inc(w_free[slot], 1)

                def route(self, n, part, w):
                    k = (0, 8, 17)[part]

                    def step():
                        nonlocal k
                        k += 1
                        return n * ROUTE + k

                    def ranks(out2, values, size, result):
                        shape = [P, NT, size, size]
                        own = values.unsqueeze(3).broadcast_to(shape)
                        other = values.unsqueeze(2).broadcast_to(shape)
                        tri = lower_sb[:, 0:size, 0:size].unsqueeze(1).broadcast_to(shape)
                        dve.wait_ge(routed, step())
                        dve.tensor_tensor(out2[:, 0], other, own, ALU.is_equal).then_inc(routed, 1)
                        dve.wait_ge(routed, step())
                        dve.tensor_tensor(out2[:, 0], out2[:, 0], tri, ALU.mult).then_inc(routed, 1)
                        dve.wait_ge(routed, step())
                        dve.tensor_tensor(out2[:, 1], other, own, ALU.is_gt).then_inc(routed, 1)
                        dve.wait_ge(routed, step())
                        dve.tensor_tensor(out2[:, 1], out2[:, 1], out2[:, 0], ALU.add).then_inc(routed, 1)
                        dve.wait_ge(routed, step())
                        dve.tensor_reduce(result, out2[:, 1], AX.X, ALU.add).then_inc(routed, 1)

                    by_group = "p t (g e) -> p t g e"
                    if part == 0:
                        slot, before, _ = w
                        dve.wait_ge(w_free[slot], before + 2)
                        dve.wait_ge(routed, step())
                        dve.tensor_scalar(denom[:], e_neg[:], 1.0, None, ALU.add).then_inc(routed, 1)
                        dve.wait_ge(routed, step())
                        dve.reciprocal(score[:], denom[:]).then_inc(routed, 1)
                        dve.wait_ge(routed, step())
                        dve.tensor_tensor(biased[:], score[:], bias_sb[:].unsqueeze(1).broadcast_to([P, NT, E]),
                                          ALU.add).then_inc(routed, 1)
                        pairs = biased[:].rearrange("p t (g a b) -> p t g a b", g=GROUPS, a=2)
                        dve.wait_ge(routed, step())
                        dve.tensor_tensor(pair_max[:], pairs[:, :, :, :, 0], pairs[:, :, :, :, 1], ALU.max).then_inc(routed, 1)
                        dve.wait_ge(routed, step())
                        dve.tensor_tensor(pair_min[:], pairs[:, :, :, :, 0], pairs[:, :, :, :, 1], ALU.min).then_inc(routed, 1)
                        dve.wait_ge(routed, step())
                        dve.tensor_tensor(top[:, 0], pair_max[:, :, :, 0], pair_max[:, :, :, 1], ALU.max).then_inc(routed, 1)
                        dve.wait_ge(routed, step())
                        dve.tensor_tensor(top[:, 1], pair_max[:, :, :, 0], pair_max[:, :, :, 1], ALU.min).then_inc(routed, 1)
                        dve.wait_ge(routed, step())
                        dve.tensor_tensor(top[:, 2], pair_min[:, :, :, 0], pair_min[:, :, :, 1], ALU.max).then_inc(routed, 1)
                    elif part == 1:
                        dve.wait_ge(routed, step())
                        dve.tensor_tensor(top[:, 3], top[:, 1], top[:, 2], ALU.max).then_inc(routed, 1)
                        dve.wait_ge(routed, step())
                        dve.tensor_tensor(group[:], top[:, 0], top[:, 3], ALU.add).then_inc(routed, 1)
                        ranks(beats_g, group[:], GROUPS, rank_g[:])
                        dve.wait_ge(routed, step())
                        dve.tensor_scalar(keep_g[:, 0], rank_g[:], TOP_GROUPS - 0.5, None, ALU.is_lt).then_inc(routed, 1)
                        dve.wait_ge(routed, step())
                        dve.tensor_scalar(keep_g[:, 1], keep_g[:, 0], 1.0, BIG, ALU.subtract, ALU.mult).then_inc(routed, 1)
                    else:
                        def wide(i):
                            return keep_g[:, i].unsqueeze(3).broadcast_to([P, NT, GROUPS, EPG])
                        dve.wait_ge(routed, step())
                        dve.tensor_tensor(masked[:, 0].rearrange(by_group, g=GROUPS),
                                          biased[:].rearrange(by_group, g=GROUPS), wide(0), ALU.mult).then_inc(routed, 1)
                        dve.wait_ge(routed, step())
                        dve.tensor_tensor(masked[:, 1].rearrange(by_group, g=GROUPS),
                                          masked[:, 0].rearrange(by_group, g=GROUPS), wide(1), ALU.add).then_inc(routed, 1)
                        ranks(beats, masked[:, 1], E, rank[:])
                        dve.wait_ge(routed, step())
                        dve.scalar_tensor_tensor(chosen[:], rank[:], TOP_K - 0.5, score[:], ALU.is_lt, ALU.mult)\
                           .then_inc(routed, 1)
                        dve.wait_ge(routed, step())
                        dve.tensor_reduce(total[:, 0], chosen[:], AX.X, ALU.add).then_inc(routed, 1)
                        dve.wait_ge(routed, step())
                        dve.tensor_scalar(total[:, 1], total[:, 0], 1e-20, None, ALU.add).then_inc(routed, 1)

                def combine(self, n, w):
                    dve.wait_ge(routed, n * ROUTE + (ROUTE + 1))
                    dve.reciprocal(inverse[:], total[:, 1]).then_inc(gated_done, 1)
                    dve.wait_ge(gated_done, n * (TILES1 + 3) + (T_SHARED + 1))
                    dve.tensor_tensor(combine[:], chosen[:], inverse[:].unsqueeze(2).broadcast_to([P, NT, E]),
                                      ALU.mult).then_inc(gated_done, 1)
                    dve.wait_ge(gated_done, n * (TILES1 + 3) + (T_SHARED + 2))
                    dve.tensor_copy(combine2[:, :, 0:E], combine[:]).then_inc(gated_done, 1)
                    dve.wait_ge(gated_done, n * (TILES1 + 3) + (T_SHARED + 3))
                    dve.tensor_tensor(combine2[:, :, E:2 * E], combine[:], raw(combine2[:, :, 0:E]), ALU.subtract)\
                       .then_inc(combined, 1)

                def tile(self, n, j, w):
                    b, r = j % 2, j % RING1
                    steps = n * (TILES1 + 3) + (j + (3 if w else 0))
                    dve.wait_ge(tanh_done, n * TILES1 + (j + 1))
                    dve.scalar_tensor_tensor(gated[:, b], tanh[:, b], 1.0, ps[:, b], ALU.add, ALU.mult)\
                       .then_inc(gated_done, 1)
                    dve.wait_ge(gated_done, steps + 1)
                    src = gated
                    if w:
                        slot, before, count = w
                        dve.wait_ge(w_full, count + 1)
                        dve.tensor_tensor(scaled[:, b], gated[:, b], ps[:, 6 + slot], ALU.mult).then_inc(w_free[slot], 1)
                        dve.wait_ge(w_free[slot], before + 2)
                        src = scaled
                    dve.wait_ge(u_full, n * TILES1 + (j + 1))
                    dve.tensor_tensor(h_f[:, r], src[:, b], ps[:, 2 + b], ALU.mult).then_inc(h_made, 1)

                def norm(self, n, w):
                    ln.run(dve, n, [later(w, k) for k in range(2)], lambda w: dve.wait_ge(w_full, w[2] + 1),
                           w_free, ps, 6, x_res, xres_in)
                    ln.apply(dve, n, y_out)

            dve.wait_ge(set_up, SETS)
            program(dve, Vector())

        @block.scalar
        def _(act):
            act.wait_ge(loaded, 16 * 5)
            act.activation(spread_r[:], spread_sb[:], ACT.Copy).then_inc(set_up, 1)
            act.activation(router_hl[:, 0], router_sb[:], ACT.Copy).then_inc(set_up, 1)
            for c in range(PIECES):
                act.wait_ge(staged[c % 2], 16 * (c // 2 + 1))
                src, _, hi, _ = piece(c)
                act.activation(hi, src, ACT.Copy, scale=1.0 if c < 3 else 0.5).then_inc(w_hi, 1)

            class Scalar(Stages):
                def transpose_x(self, n, w):
                    for k in range(KD):
                        slot, _, count = later(w, k)
                        act.wait_ge(w_full, count + 1)
                        act.activation(xt[:, 0, k], ps[:, 6 + slot], ACT.Copy).then_inc(xt_hi, 1)

                def logits(self, n, w):
                    slot, _, count = w
                    act.wait_ge(w_full, count + 1)
                    act.activation(e_neg[:], ps[:, 6 + slot, 0:NT * E].rearrange("p (t e) -> p t e", e=E),
                                   ACT.Exp, scale=-1.0).then_inc(w_free[slot], 1)

                def combine(self, n, w):
                    slot, _, count = w
                    act.wait_ge(w_full, count + 1)
                    act.activation(combine_t[:], ps[:, 6 + slot], ACT.Copy).then_inc(w_free[slot], 1)

                def gate(self, n, j):
                    b = j % 2
                    act.wait_ge(g_full, n * TILES1 + (j + 1))
                    act.activation(tanh[:, b], ps[:, b], ACT.Tanh, scale=0.5).then_inc(tanh_done, 1)

                def tile(self, n, j, w):
                    r = j % RING1
                    act.wait_ge(h_made, n * TILES1 + (j + 3))
                    act.activation(h_hl[:, r, 0], h_f[:, r], ACT.Copy).then_inc(h_hi, 1)

                def output(self, n):
                    act.wait_ge(y_full, n + 1)
                    for k in range(KD):
                        act.activation(y_sb[:, k], ps[:, 4 + k], ACT.Copy).then_inc(y_free, 1)

            act.wait_ge(set_up, SETS)
            program(act, Scalar())

        @block.tensor
        def _(pe):
            pe.wait_ge(set_up, SETS)
            pe.wait_ge(w_lo, PIECES)

            def take(w):
                pe.wait_ge(w_free[w[0]], w[1] + 1)
                return ps[:, 6 + w[0]]

            def emptied(w):
                pe.wait_ge(w_free[w[0]], w[1] + 2)

            class Tensor(Stages):
                def transpose_x(self, n, w):
                    pe.wait_ge(x_in_sem, n * 16 + 16)
                    for k in range(KD):
                        bank = take(later(w, k))
                        for t in range(NT):
                            ins = pe.transpose(bank[:, t * P:(t + 1) * P], x_sb[:, t, k * P:(k + 1) * P], ident[:])
                        ins.then_inc(w_full, 1)
                    self.w_x = w

                def logits(self, n, w):
                    for k in range(KD):
                        emptied(later(self.w_x, k))
                    bank = take(w)
                    for t in range(NT):
                        ins = matmul3(pe, bank[:, t * E:(t + 1) * E], xt, router_hl, slice(t * P, (t + 1) * P),
                                      slice(0, E), KD)
                    ins.then_inc(w_full, 1)

                def combine(self, n, w):
                    bank = take(w)
                    pe.wait_ge(combined, n + 1)
                    for t in range(NT):
                        ins = pe.transpose(bank[:, t * P:(t + 1) * P], raw(combine2[:, t]), ident[:])
                    ins.then_inc(w_full, 1)
                    self.w_c = w

                def gate(self, n, j):
                    pe.wait_ge(h_made, n * TILES1 + (j + 1))
                    matmul3(pe, ps[:, j % 2], gu_hl, xt, slice(j * P, (j + 1) * P), slice(0, S), KD).then_inc(g_full, 1)

                def tile(self, n, j, w):
                    if w:
                        bank = take(w)
                        if j == T_SHARED:
                            emptied(self.w_c)
                        pe.matmul(bank, spread_r[:, j - T_SHARED], combine_t[:], start=True, stop=True)\
                          .then_inc(w_full, 1)
                    matmul3(pe, ps[:, 2 + j % 2], gu_hl, xt, slice(HID1 + j * P, HID1 + (j + 1) * P), slice(0, S), KD)\
                        .then_inc(u_full, 1)

                def down(self, n, j):
                    r = j % RING1
                    pe.wait_ge(h_lo, n * TILES1 + (j + 1))
                    if j == 0:
                        pe.wait_ge(y_free, n * 2 + 2)
                    for k in range(KD):
                        for i, (a, b) in enumerate(TERMS):
                            ins = pe.matmul(ps[:, 4 + k], down_hl[:, a, j, k * P:(k + 1) * P], h_hl[:, r, b],
                                            start=(j == 0 and i == 0), stop=(j == TILES1 - 1 and i == 2))
                    if j == TILES1 - 1:
                        ins.then_inc(y_full, 1)

                def norm(self, n, w):
                    pe.wait_ge(y_free, n * 2 + 4)
                    ln.transposes(pe, take, [later(w, k) for k in range(2)], y_sb, ident, [w_full, w_full])

            program(pe, Tensor())


def transformer(nc, x, a0_weights, a0_bias_qk, a0_bias_v, a0_bias_o, causal, f0_w1, f0_w2, f0_b1, f0_b2, f0_gate,
                a1_weights, a1_rope, a1_select, band, f1_gate_up, f1_down, f1_router, f1_bias, f1_lower, f1_spread,
                ident, out):
    x1 = nc.dram_tensor("x1", (B * S, D), F32, kind="Internal").ap()
    x2 = nc.dram_tensor("x2", (B * S, D), F32, kind="Internal").ap()
    x3 = nc.dram_tensor("x3", (B * S, D), F32, kind="Internal").ap()
    qk_scratch = nc.dram_tensor("qk_scratch", (2, HALF, 2, HD, S), F32, kind="Internal").ap()
    rows = "b s d -> (b s) d"
    attention0(nc, x.rearrange(rows), a0_weights, a0_bias_qk, a0_bias_v, a0_bias_o, ident, causal, qk_scratch, x1)
    feed_forward0(nc, x1, f0_w1, f0_w2, f0_b1, f0_b2, f0_gate, ident, x2)
    attention1(nc, x2, a1_weights, a1_rope, a1_select, ident, band, x3)
    feed_forward1(nc, x3, f1_gate_up, f1_down, f1_router, f1_bias, f1_lower, f1_spread, ident, out.rearrange(rows))


def lay_out(d):
    import numpy as np

    def swapped(w):
        return w.reshape(D, -1, 2)[:, :, ::-1].reshape(w.shape)

    def column(v, n):
        return v.reshape(n, P).T

    lane, token = np.arange(P), np.arange(S)
    heads = [d["L0_attn_W_" + c].transpose(1, 0, 2).reshape(D, D) for c in "qkv"]
    a0_weights = np.concatenate(heads + [d["L0_attn_W_o"].T], axis=1)
    a0_bias_qk = np.stack([column(d["L0_attn_b_q"], KD), column(d["L0_attn_b_k"], KD)], axis=1)
    a0_bias_v = np.broadcast_to(d["L0_attn_b_v"].reshape(1, D), (P, D))
    a0_bias_o = column(d["L0_attn_b_o"], KD)
    query_key = np.where(lane[None, :] <= lane[:, None], 0, MASKED)
    causal = np.stack([query_key, query_key.T], axis=1).astype(np.float32)

    f0_w1 = np.concatenate([d["L0_ffn_sw1"], *d["L0_ffn_w1"]], axis=1)
    f0_w2 = np.concatenate([d["L0_ffn_sw2"], *d["L0_ffn_w2"]], axis=0)
    f0_b1 = column(np.concatenate([d["L0_ffn_sb1"], *d["L0_ffn_b1"]]), TILES0)
    f0_b2 = np.stack([d["L0_ffn_sb2"], *d["L0_ffn_b2"]]).reshape(3, KD, P).transpose(2, 0, 1)
    f0_gate = d["L0_ffn_gate_w"].T.reshape(KD, P, 2).transpose(1, 0, 2)

    wq, wk, wv, wo = [d["L1_attn_W" + c] for c in "qkvo"]
    a1_weights = np.concatenate([wq, swapped(wq), wk, wk, swapped(wk), swapped(wk), wv, wo], axis=1)
    frequency = np.float32(1.0) / np.float32(10000.0) ** (np.arange(0, HD, 2, dtype=np.float32) / np.float32(HD))
    angle = (token.astype(np.float32)[None, :] * frequency[:, None])[lane % HD // 2].astype(np.float64)
    sign = np.where(lane % 2 == 0, -1.0, 1.0)[:, None]
    a1_rope = np.stack([np.cos(angle), np.sin(angle) * sign], axis=1).astype(np.float32)
    a1_select = np.zeros((P, 24, P), np.float32)
    e = np.arange(HD)
    for half in range(2):
        for r in range(4):
            for part, at in ((0, 0), (1, 1), (0, 2)):
                a1_select[HD * (4 * half + r) + e, 2 * r + part, 64 * half + HD * at + e] = 1
    for c in range(KV):
        for part, at in ((0, 0), (0, 1), (1, 2)):
            a1_select[HD * c + e, 8 + 2 * c + part, 64 * (c % 2) + HD * at + e] = 1
    for h in range(G_HEADS):
        a1_select[[h, G_HEADS + h], 16 + h] = 1
    near = np.abs(lane[:, None] - (np.arange(WINDOW)[None, :] - REACH)) <= REACH
    band = np.repeat(np.where(near, 0, MASKED).astype(np.float32)[:, None], 2, axis=1)

    gate, up = [d[f"L1_ffn_{c}_w"].transpose(1, 0, 2).reshape(D, E * HID_EXPERT) for c in ("gate", "up")]
    f1_gate_up = np.concatenate([d["L1_ffn_shared_gate_w"].T, gate, d["L1_ffn_shared_up_w"].T, up], axis=1)
    f1_down = np.concatenate([d["L1_ffn_shared_down_w"].T, d["L1_ffn_down_w"].reshape(E * HID_EXPERT, D)], axis=0)
    f1_router = d["L1_ffn_router_w"].T.reshape(KD, P, E).transpose(1, 0, 2)
    f1_bias = np.broadcast_to(d["L1_ffn_correction_bias"], (P, E))
    f1_lower = np.broadcast_to(np.tril(np.ones((E, E), np.float32), -1), (P, E, E))
    f1_spread = np.zeros((P, E // 2, P), np.float32)
    for x in range(E):
        f1_spread[[x, E + x], x // 2, HID_EXPERT * (x % 2):HID_EXPERT * (x % 2 + 1)] = 1
    ident = np.eye(P, dtype=np.float32)
    return dict(x=d["L0_attn_inputs"], a0_weights=a0_weights, a0_bias_qk=a0_bias_qk, a0_bias_v=a0_bias_v,
                a0_bias_o=a0_bias_o, causal=causal, f0_w1=f0_w1, f0_w2=f0_w2, f0_b1=f0_b1, f0_b2=f0_b2,
                f0_gate=f0_gate, a1_weights=a1_weights, a1_rope=a1_rope, a1_select=a1_select, band=band,
                f1_gate_up=f1_gate_up, f1_down=f1_down, f1_router=f1_router, f1_bias=f1_bias, f1_lower=f1_lower,
                f1_spread=f1_spread, ident=ident)


def kernel(**inputs):
    import numpy as _np
    import concourse.bacc as _bacc
    from concourse import mybir as _mybir
    from concourse.bass_utils import run_bass_kernel_spmd as _run

    nc = _bacc.Bacc("TRN2", target_bir_lowering=False, num_devices=1)
    arrays, args = {}, []
    for name, value in lay_out({k: _np.asarray(v) for k, v in inputs.items()}).items():
        a = _np.ascontiguousarray(value)
        arrays[f"in_{name}_dram"] = a
        args.append(nc.dram_tensor(f"in_{name}_dram", a.shape, _mybir.dt.from_np(a.dtype), kind="ExternalInput").ap())
    args.append(nc.dram_tensor("out_0_dram", (B, S, D), _mybir.dt.from_np(_np.dtype("float32")),
                               kind="ExternalOutput").ap())
    transformer(nc, *args)
    r = _run(nc, [arrays], core_ids=[0])
    return r.results[0]["out_0_dram"]
```
